# Optimizing a Trainium2 kernel written in Bass

```python
import numpy as np
import jax
import jax.numpy as jnp

def _softmax(x, axis=-1):
    return jax.nn.softmax(x, axis=axis)

def _gelu(x):
    return jax.nn.gelu(x, approximate=True)

def _silu(x):
    return jax.nn.silu(x)

def _sigmoid(x):
    return jax.nn.sigmoid(x)

def _layernorm(x, axis=-1, eps=1e-05):
    m = jnp.mean(x, axis=axis, keepdims=True)
    v = jnp.var(x, axis=axis, keepdims=True)
    return (x - m) / jnp.sqrt(v + eps)

def _scatter_add(tgt, idx, src, axis=0):
    return tgt.at[idx].add(src)

def _segment_sum(src, seg, n):
    return jax.ops.segment_sum(src, seg, n)
kernel_name = 'mk_hybrid_d1_jaxref_r8_9dc3aa'

def setup_inputs(seed: int=0):
    np.random.seed(seed)
    _w = jnp.asarray

    def _L0_attn_a_setup():
        import jax, jax.numpy as jnp
        import numpy as np
        D_MODEL, N_HEADS, D_HEAD, D_VALUE = (128, 16, 4, 64)
        B, T = (2, 256)
        SCALE = 1.0 / np.sqrt(D_HEAD)

        def _h4_simple_roots():
            c = np.cos(np.pi / 5)
            G = np.eye(4)
            G[0, 1] = G[1, 0] = -c
            G[1, 2] = G[2, 1] = -0.5
            G[2, 3] = G[3, 2] = -0.5
            return np.linalg.cholesky(G).astype(np.float32)

        def _normalize(v):
            return v / jnp.maximum(jnp.linalg.norm(v, axis=-1, keepdims=True), 1e-12)
        key = jax.random.key(seed)
        ks = jax.random.split(key, 8)
        x = jax.random.normal(ks[0], (B, T, D_MODEL), dtype=jnp.float32)
        W_q = jax.random.normal(ks[1], (D_HEAD * N_HEADS, D_MODEL), jnp.float32) / np.sqrt(D_MODEL)
        W_k = jax.random.normal(ks[2], (D_HEAD * N_HEADS, D_MODEL), jnp.float32) / np.sqrt(D_MODEL)
        W_v = jax.random.normal(ks[3], (D_VALUE * N_HEADS, D_MODEL), jnp.float32) / np.sqrt(D_MODEL)
        W_out = jax.random.normal(ks[4], (D_MODEL, D_VALUE * N_HEADS), jnp.float32) / np.sqrt(D_VALUE * N_HEADS)
        W_nudge = jnp.eye(4, dtype=jnp.float32)[None] + 0.01 * jax.random.normal(ks[5], (N_HEADS, 4, 4), jnp.float32)
        chamber_bonus = 0.02 * jax.random.normal(ks[6], (N_HEADS, 16), jnp.float32)
        simple_roots = jnp.asarray(_h4_simple_roots())
        return {'x': x, 'W_q': W_q, 'W_k': W_k, 'W_v': W_v, 'W_nudge': W_nudge, 'chamber_bonus': chamber_bonus, 'W_out': W_out, 'simple_roots': simple_roots}
    _L0_attn_a_in = _L0_attn_a_setup()

    def _L0_attn_b_setup():
        import jax, jax.numpy as jnp
        import numpy as np
        B, T, D_MODEL, N_HEADS = (2, 256, 128, 16)
        HEAD_DIM = D_MODEL // N_HEADS
        GN_EPS = 1e-05

        def decay_gammas(n_heads):
            h = jnp.arange(n_heads, dtype=jnp.float32)
            return 1.0 - jnp.power(2.0, -5.0 - h * (8.0 / n_heads))
        key = jax.random.key(seed)
        ks = jax.random.split(key, 7)
        w_scale = 0.02
        return {'x': jax.random.normal(ks[0], (B, T, D_MODEL), dtype=jnp.float32), 'Wq': jax.random.normal(ks[1], (D_MODEL, D_MODEL), dtype=jnp.float32) * w_scale, 'Wk': jax.random.normal(ks[2], (D_MODEL, D_MODEL), dtype=jnp.float32) * w_scale, 'Wv': jax.random.normal(ks[3], (D_MODEL, D_MODEL), dtype=jnp.float32) * w_scale, 'Wo': jax.random.normal(ks[4], (D_MODEL, D_MODEL), dtype=jnp.float32) * w_scale, 'gn_w': jnp.ones((D_MODEL,), dtype=jnp.float32), 'gn_b': jnp.zeros((D_MODEL,), dtype=jnp.float32)}
    _L0_attn_b_in = _L0_attn_b_setup()

    def _L0_ffn_setup():
        import jax, jax.numpy as jnp
        import numpy as np
        TOP_K = 2
        E = 8
        D = 128
        F = 256
        B, S = (2, 128)
        key = jax.random.key(seed)
        ks = jax.random.split(key, 8)
        sc = 0.02
        return {'x_bsD': jax.random.normal(ks[0], (B, S, D), dtype=jnp.float32), 'router_DE': jax.random.normal(ks[1], (D, E), dtype=jnp.float32) * sc, 'w_in_shared_FD': jax.random.normal(ks[2], (F, D), dtype=jnp.float32) * sc, 'w_out_shared_DF': jax.random.normal(ks[3], (D, F), dtype=jnp.float32) * sc, 'w_swiglu_FD': jax.random.normal(ks[4], (F, D), dtype=jnp.float32) * sc, 'w_in_eDF': jax.random.normal(ks[5], (E, D, F), dtype=jnp.float32) * sc, 'w_swiglu_eDF': jax.random.normal(ks[6], (E, D, F), dtype=jnp.float32) * sc, 'w_out_eFD': jax.random.normal(ks[7], (E, F, D), dtype=jnp.float32) * sc}
    _L0_ffn_in = _L0_ffn_setup()
    _d = {'L0_attn_a_x': _L0_attn_a_in['x'], 'L0_attn_a_W_q': _L0_attn_a_in['W_q'], 'L0_attn_a_W_k': _L0_attn_a_in['W_k'], 'L0_attn_a_W_v': _L0_attn_a_in['W_v'], 'L0_attn_a_W_nudge': _L0_attn_a_in['W_nudge'], 'L0_attn_a_chamber_bonus': _L0_attn_a_in['chamber_bonus'], 'L0_attn_a_W_out': _L0_attn_a_in['W_out'], 'L0_attn_a_simple_roots': _L0_attn_a_in['simple_roots'], 'L0_attn_b_Wq': _L0_attn_b_in['Wq'], 'L0_attn_b_Wk': _L0_attn_b_in['Wk'], 'L0_attn_b_Wv': _L0_attn_b_in['Wv'], 'L0_attn_b_Wo': _L0_attn_b_in['Wo'], 'L0_attn_b_gn_w': _L0_attn_b_in['gn_w'], 'L0_attn_b_gn_b': _L0_attn_b_in['gn_b'], 'L0_ffn_router_DE': _L0_ffn_in['router_DE'], 'L0_ffn_w_in_shared_FD': _L0_ffn_in['w_in_shared_FD'], 'L0_ffn_w_out_shared_DF': _L0_ffn_in['w_out_shared_DF'], 'L0_ffn_w_swiglu_FD': _L0_ffn_in['w_swiglu_FD'], 'L0_ffn_w_in_eDF': _L0_ffn_in['w_in_eDF'], 'L0_ffn_w_swiglu_eDF': _L0_ffn_in['w_swiglu_eDF'], 'L0_ffn_w_out_eFD': _L0_ffn_in['w_out_eFD']}
    _x0 = _d['L0_attn_a_x']
    _d['L0_attn_a_x'] = jax.random.normal(jax.random.fold_in(jax.random.key(seed), 1), (4, 512, 128), dtype=_x0.dtype)
    del _x0
    return _d

def reference(L0_attn_a_x, L0_attn_a_W_q, L0_attn_a_W_k, L0_attn_a_W_v, L0_attn_a_W_nudge, L0_attn_a_chamber_bonus, L0_attn_a_W_out, L0_attn_a_simple_roots, L0_attn_b_Wq, L0_attn_b_Wk, L0_attn_b_Wv, L0_attn_b_Wo, L0_attn_b_gn_w, L0_attn_b_gn_b, L0_ffn_router_DE, L0_ffn_w_in_shared_FD, L0_ffn_w_out_shared_DF, L0_ffn_w_swiglu_FD, L0_ffn_w_in_eDF, L0_ffn_w_swiglu_eDF, L0_ffn_w_out_eFD):

    def _L0_attn_a_ref(x, W_q, W_k, W_v, W_nudge, chamber_bonus, W_out, simple_roots):
        import jax, jax.numpy as jnp
        import numpy as np
        D_MODEL, N_HEADS, D_HEAD, D_VALUE = (128, 16, 4, 64)
        B, T = (2, 256)
        SCALE = 1.0 / np.sqrt(D_HEAD)

        def _h4_simple_roots():
            c = np.cos(np.pi / 5)
            G = np.eye(4)
            G[0, 1] = G[1, 0] = -c
            G[1, 2] = G[2, 1] = -0.5
            G[2, 3] = G[3, 2] = -0.5
            return np.linalg.cholesky(G).astype(np.float32)

        def _normalize(v):
            return v / jnp.maximum(jnp.linalg.norm(v, axis=-1, keepdims=True), 1e-12)
        b, t, _ = x.shape
        Q = _normalize((x @ W_q.T).reshape(b, t, N_HEADS, D_HEAD))
        K = _normalize((x @ W_k.T).reshape(b, t, N_HEADS, D_HEAD))
        V = (x @ W_v.T).reshape(b, t, N_HEADS, D_VALUE)
        Qn = _normalize(jnp.einsum('bthd,hde->bthe', Q, W_nudge))
        scores = jnp.einsum('bqhd,bkhd->bhqk', Qn, K) * SCALE
        k_dots = jnp.einsum('bthd,rd->bthr', K, simple_roots)
        s = jax.nn.sigmoid(3.0 * k_dots)
        bits = (jnp.arange(16)[:, None] >> jnp.arange(4)[None, :] & 1).astype(x.dtype)
        cw = jnp.prod(s[..., None, :] * bits + (1.0 - s[..., None, :]) * (1.0 - bits), axis=-1)
        k_bonus = jnp.einsum('bthc,hc->bth', cw, chamber_bonus)
        scores = scores + k_bonus.transpose(0, 2, 1)[:, :, None, :]
        causal = jnp.triu(jnp.ones((t, t), dtype=bool), k=1)
        scores = jnp.where(causal[None, None], -jnp.inf, scores)
        attn = jax.nn.softmax(scores, axis=-1)
        out = jnp.einsum('bhqk,bkhv->bqhv', attn, V).reshape(b, t, N_HEADS * D_VALUE)
        return out @ W_out.T

    def _L0_attn_b_ref(x, Wq, Wk, Wv, Wo, gn_w, gn_b):
        import jax, jax.numpy as jnp
        import numpy as np
        B, T, D_MODEL, N_HEADS = (2, 256, 128, 16)
        HEAD_DIM = D_MODEL // N_HEADS
        GN_EPS = 1e-05

        def decay_gammas(n_heads):
            h = jnp.arange(n_heads, dtype=jnp.float32)
            return 1.0 - jnp.power(2.0, -5.0 - h * (8.0 / n_heads))
        Bx, Tx, C = x.shape
        H, D = (N_HEADS, C // N_HEADS)
        gammas = decay_gammas(H)

        def split_heads(y):
            return y.reshape(Bx, Tx, H, D).transpose(0, 2, 1, 3)
        Q = split_heads(x @ Wq.T)
        K = split_heads(x @ Wk.T)
        V = split_heads(x @ Wv.T)
        idx = jnp.arange(Tx, dtype=jnp.float32)
        diff = idx[:, None] - idx[None, :]
        mask = jnp.where(diff >= 0, gammas[:, None, None] ** jnp.maximum(diff, 0.0), 0.0)
        scores = jnp.einsum('bhtd,bhsd->bhts', Q, K) / jnp.sqrt(jnp.float32(D))
        scores = scores * mask[None]
        out = jnp.einsum('bhts,bhsd->bhtd', scores, V)
        y = out.transpose(0, 2, 1, 3).reshape(Bx, Tx, C)
        z = y.transpose(0, 2, 1).reshape(Bx, H, D, Tx)
        mu = z.mean(axis=(2, 3), keepdims=True)
        var = z.var(axis=(2, 3), keepdims=True)
        zn = (z - mu) * jax.lax.rsqrt(var + GN_EPS)
        zn = zn * gn_w.reshape(1, H, D, 1) + gn_b.reshape(1, H, D, 1)
        y = zn.reshape(Bx, C, Tx).transpose(0, 2, 1)
        return y @ Wo.T

    def _L0_ffn_ref(x_bsD, router_DE, w_in_shared_FD, w_out_shared_DF, w_swiglu_FD, w_in_eDF, w_swiglu_eDF, w_out_eFD):
        import jax, jax.numpy as jnp
        import numpy as np
        TOP_K = 2
        E = 8
        D = 128
        F = 256
        B, S = (2, 128)
        b, s, d = x_bsD.shape
        x_aD = x_bsD.reshape(-1, d)
        a = x_aD.shape[0]
        scores_aE = x_aD @ router_DE
        topv_aK, topi_aK = jax.lax.top_k(scores_aE, TOP_K)
        masked_aE = jnp.full_like(scores_aE, -jnp.inf)
        masked_aE = masked_aE.at[jnp.arange(a)[:, None], topi_aK].set(topv_aK)
        gates_Ea = jax.nn.sigmoid(masked_aE.astype(jnp.float32)).astype(x_aD.dtype).T
        routed_in_EaD = x_aD[None, :, :] * gates_Ea[:, :, None]
        routed_in_EaD = jax.lax.stop_gradient(routed_in_EaD)
        mid_EaF = jnp.einsum('ead,edf->eaf', routed_in_EaD, w_in_eDF)
        sw_EaF = jnp.einsum('ead,edf->eaf', routed_in_EaD, w_swiglu_eDF)
        h_EaF = jax.nn.silu(mid_EaF) * sw_EaF
        out_EaD = jnp.einsum('eaf,efd->ead', h_EaF, w_out_eFD)
        shared_aF = jax.nn.silu(x_aD @ w_in_shared_FD.T) * (x_aD @ w_swiglu_FD.T)
        shared_out_aD = jax.lax.stop_gradient(shared_aF @ w_out_shared_DF.T)
        out_aD = shared_out_aD + jnp.sum(out_EaD, axis=0)
        return out_aD.reshape(b, s, d)
    x = L0_attn_a_x
    x = x + _L0_attn_a_ref(_layernorm(x, axis=-1), L0_attn_a_W_q, L0_attn_a_W_k, L0_attn_a_W_v, L0_attn_a_W_nudge, L0_attn_a_chamber_bonus, L0_attn_a_W_out, L0_attn_a_simple_roots)
    x = x + _L0_ffn_ref(_layernorm(x, axis=-1), L0_ffn_router_DE, L0_ffn_w_in_shared_FD, L0_ffn_w_out_shared_DF, L0_ffn_w_swiglu_FD, L0_ffn_w_in_eDF, L0_ffn_w_swiglu_eDF, L0_ffn_w_out_eFD)
    x = x + _L0_attn_b_ref(_layernorm(x, axis=-1), L0_attn_b_Wq, L0_attn_b_Wk, L0_attn_b_Wv, L0_attn_b_Wo, L0_attn_b_gn_w, L0_attn_b_gn_b)
    x = x + _L0_ffn_ref(_layernorm(x, axis=-1), L0_ffn_router_DE, L0_ffn_w_in_shared_FD, L0_ffn_w_out_shared_DF, L0_ffn_w_swiglu_FD, L0_ffn_w_in_eDF, L0_ffn_w_swiglu_eDF, L0_ffn_w_out_eFD)
    return x

_drawn_inputs = setup_inputs


def setup_inputs(seed=0):
    import zlib

    import numpy as np

    out = dict(_drawn_inputs(seed))
    spreads = {'L0_attn_b_gn_w': (1.0, 0.2), 'L0_attn_b_gn_b': (0.0, 0.327)}
    factors = {'L0_attn_a_chamber_bonus': 8.0,
     'L0_attn_a_simple_roots': 8.0,
     'L0_ffn_router_DE': 8.0,
     'L0_ffn_w_in_shared_FD': 3.525,
     'L0_ffn_w_out_shared_DF': 3.479,
     'L0_ffn_w_swiglu_FD': 3.5,
     'L0_ffn_w_in_eDF': 7.855,
     'L0_ffn_w_swiglu_eDF': 7.897,
     'L0_ffn_w_out_eFD': 7.866}
    for name, (base, spread) in spreads.items():
        noise = np.random.default_rng([zlib.crc32(name.encode()), seed]).standard_normal(out[name].shape)
        drawn = base * np.exp(spread * noise) if base else spread * noise
        out[name] = jnp.asarray(drawn.astype(out[name].dtype))
    for name, factor in factors.items():
        out[name] = (out[name] * factor).astype(out[name].dtype)
    return out
```

```python
import numpy as np
import concourse.bass as bass
from concourse import mybir
from contextlib import ExitStack


def hybrid_block_kernel(nc: bass.Bass, x_in: bass.AP, w_qk: bass.AP, w_qk_rows: bass.AP, fold: bass.AP,
                        w_v: bass.AP, bonus: bass.AP, w_out: bass.AP, ret_qkv: bass.AP, ret_o: bass.AP,
                        gn: bass.AP, router: bass.AP, ffn_in: bass.AP, ffn_out: bass.AP,
                        consts: bass.AP, out: bass.AP, stages: str = "frf"):
    F32 = mybir.dt.float32
    BF16 = mybir.dt.bfloat16
    I32 = mybir.dt.int32
    ALU = mybir.AluOpType
    ACT = mybir.ActivationFunctionType
    AX = mybir.AxisListType

    P = 128
    B, T, D = x_in.shape
    TT = T // P
    NT = B * TT
    H = 16
    HG = 4
    NG = H // HG
    STEPS = B * NG
    J = TT * H
    DK = 4
    DV = w_v.shape[1] // H
    VW = DV + 1
    SLOT = 32
    E = router.shape[1]
    U = E + 1
    FF = ffn_in.shape[1] // (2 * U)
    RD = D // H
    EPS = 1e-5
    NORM2 = 1e-24
    LOW = -3.0e38
    PB = 4
    SPAN = 10 * P

    ctx = ExitStack()
    with ctx:
        def sb(name, shape, dt=F32):
            return ctx.enter_context(nc.sbuf_tensor(name, shape, dt))

        def sem(name):
            return ctx.enter_context(nc.semaphore(name))

        x = sb("x", [P, NT, D])
        cst = sb("cst", [P, consts.shape[1]])
        ident = cst[:, 0:128]
        causal = cst[:, 128:256]
        groupavg = cst[:, 256:384]
        statemask = cst[:, 384:512]
        qdecay = cst[:, 512:640]
        kdecay = cst[:, 640:768]
        before = cst[:, 768:832]
        decay128 = cst[:, 832:833]
        identb = sb("identb", [P, P], BF16)
        wff = sb("wff", [P, U, 2 * FF])
        wfo = sb("wfo", [P, U, 2, D])
        wr = sb("wr", [P, E])
        rqkv = sb("rqkv", [P, 3 * D])
        rwo = sb("rwo", [P, D])
        gnw = sb("gnw", [P, 2])
        wproj = sb("wproj", [P, 4 * H * DK])
        wrows = sb("wrows", [H * DK, 2 * D])
        wfold = sb("wfold", [H * DK, 2 * H * DK])
        wv = sb("wv", [P, H * DV])
        wo = sb("wo", [P, 2 * NG, D])
        st6 = sb("st6", [P, TT, 6])
        mv = sb("mv", [P, TT, 2])
        nv = sb("nv", [P, 2 * J])
        ny = sb("ny", [P, 2 * J])
        nt = sb("nt", [P, 2 * J])
        xn = sb("xn", [P, TT, D])
        xnT = sb("xnT", [P, T])
        big = sb("big", [P, STEPS * TT * HG * VW])
        V = big[:, :].rearrange("p (b g t r w) -> p b g t r w", b=B, g=NG, t=TT, r=HG)
        Vs = big[:, :].rearrange("p (s t r w) -> p s t r w", s=STEPS, t=TT, r=HG)
        qs = sb("qs", [P, STEPS, TT * P], BF16)
        ks = sb("ks", [P, STEPS, TT * P], BF16)
        probs = sb("probs", [P, PB, SPAN])
        qt = sb("qt", [P, T], BF16)
        kt = sb("kt", [P, T], BF16)
        o = sb("o", [P, TT, HG * DV])
        ot = sb("ot", [P, 2, T])
        rec = sb("rec", [P, TT])

        room = probs[:, :, :].rearrange("p a n -> p (a n)")
        taken = [0]

        def take(n):
            taken[0] += n
            assert taken[0] <= PB * SPAN
            return room[:, taken[0] - n:taken[0]]

        qk = take(4 * J * DK).rearrange("p (k j d) -> p k j d", k=4, d=DK)
        sq = take(3 * J * DK)
        n2 = take(3 * J)
        rqk = take(2 * J)
        ru = take(J)
        fu = take(J)
        dots = take(J * DK)
        sig = take(J * DK).rearrange("p (j d) -> p j d", d=DK)
        bon = take(J)
        bont = take(J)
        mneg = take(J)
        bT = take(T)
        mT = take(T)
        res = take(J * DK)
        oflat = o[:, :, :].rearrange("p a n -> p (a n)")
        otflat = ot[:, :, :].rearrange("p a n -> p (a n)")
        qv, kv = oflat[:, 0:J * DK], oflat[:, J * DK:2 * J * DK]
        lvl = otflat[:, 0:J * 8].rearrange("p (j c) -> p j c", c=8)
        dif = otflat[:, J * 8:J * 12].rearrange("p (j c) -> p j c", c=4)
        btab = sb("btab", [P, H, 16])
        blo = sb("blo", [P, J, 8])
        bdf = sb("bdf", [P, J, 8])
        part = sb("part", [P, 3, J * DK], BF16)
        mpart = sb("mpart", [P, 3, J], BF16)

        bank = [ctx.enter_context(nc.psum_tensor(f"bank{i}", [P, 512], F32)) for i in range(8)]

        names = """loads loads_late consts_ready fold_ready proj_ready xn_ready xn_turned xnT_ready qk_done
            qk_out qk_used v_done v_out dots_ready tanh_ready sig_ready bonus_ready bonus_turned max_ready
            max_turned phase turned operands scored expd masked averaged normed o_turned o_copied outed added
            f_scored f_gated x_static x_turned x_copied mids tanhs hidden h_turned h_copied f_out f_added
            r_ln r_turned r_xT r_qkv r_decayed r_opT
            r_op r_scored r_masked r_kv r_state r_summed r_ycopied r_yT r_stats r_avg r_z r_out r_added stored seen
            sc_ready m_static m_turned m_copied"""
        S = {n: sem(n) for n in names.split()}
        block = ctx.enter_context(nc.Block())

        def barrier(eng, n):
            eng.drain().then_inc(S["phase"], 1)
            eng.wait_ge(S["phase"], 4 * n)

        FINAL = 4 * (2 + 2 * stages.count('f') + stages.count('r'))
        QB, KB, AVB, SB = bank[6], bank[7], bank[4:6], bank[0:4]
        BLK = [0, 512, 1024, 896]
        CHUNKS = [((0, 0),), ((1, 0), (3, 384)), ((2, 0),)]
        WIDTH = [512, 512, 256]

        ve = nc.vector

        def rsqrt(v, y, t):
            ve.tensor_scalar(y.bitcast(I32), v.bitcast(I32), 1, None, ALU.logical_shift_right)
            ve.drain()
            ve.tensor_scalar(y.bitcast(I32), y.bitcast(I32), -1.0, float(0x5f3759df), ALU.mult, ALU.add)
            ve.drain()
            for _ in range(3):
                ve.tensor_tensor(t, y, y, ALU.mult)
                ve.drain()
                ve.scalar_tensor_tensor(t, t, -0.5, v, ALU.mult, ALU.mult)
                ve.drain()
                ve.scalar_tensor_tensor(y, t, 1.5, y, ALU.add, ALU.mult)
                ve.drain()

        def layernorm(b, outs):
            for t in range(TT):
                ve.bn_stats(st6[:, t, :], x[:, b * TT + t, :])
            ve.drain()
            for t in range(TT):
                ve.bn_aggr(mv[:, t, :], st6[:, t, :])
            ve.drain()
            ve.tensor_scalar(nv[:, 0:TT], mv[:, :, 1], EPS, None, ALU.add)
            ve.drain()
            rsqrt(nv[:, 0:TT], ny[:, 0:TT], nt[:, 0:TT])
            for t in range(TT):
                last = ve.tensor_scalar(outs(t), x[:, b * TT + t, :], mv[:, t, 0:1], ny[:, t:t + 1],
                                        ALU.subtract, ALU.mult)
            return last

        @block.sync
        def _(sp):
            early = ((x[:], x_in.rearrange("b (t p) d -> p (b t) d", p=P)), (cst[:], consts),
                     (wproj[:, 0:2 * H * DK], w_qk), (wrows[:], w_qk_rows), (wfold[:], fold),
                     (btab[:], bonus.partition_broadcast(P)), (wv[:], w_v))
            for dst, src in early:
                sp.dma_start(dst, src).then_inc(S["loads"], 16)
            late = ((wo[:], w_out), (wr[:], router), (wff[:], ffn_in), (wfo[:], ffn_out),
                    (rqkv[:], ret_qkv), (rwo[:], ret_o), (gnw[:], gn))
            for dst, src in late:
                sp.dma_start(dst, src).then_inc(S["loads_late"], 16)
            sp.wait_ge(S["phase"], FINAL)
            sp.dma_start(out.rearrange("b (t p) d -> p (b t) d", p=P), x[:]).then_inc(S["stored"], 16)
            sp.wait_ge(S["stored"], 16)

        def proj_pe(pe):
            te = nc.tensor
            pe.wait_ge(S["loads"], 7 * 16)
            pe.wait_ge(S["consts_ready"], 1)
            te.matmul(bank[0][:, 0:64], wrows[:, 0:D], wfold[:, 0:64], start=True, stop=True)
            te.matmul(bank[0][:, 64:128], wrows[:, D:2 * D], wfold[:, 64:128], start=True, stop=True)\
                .then_inc(S["fold_ready"], 1)
            pe.wait_ge(S["proj_ready"], 1)
            pe.sem_inc(S["xn_turned"], 1)
            with pe.Fori(0, B) as b:
                pe.wait_ge(S["xn_ready"], b + 1)
                for t in range(TT):
                    last = te.transpose(bank[0][:, t * P:(t + 1) * P], xn[:, t, :], ident)
                last.then_inc(S["xn_turned"], 1)
                pe.wait_ge(S["xnT_ready"], b + 1)
                pe.wait_ge(S["qk_out"], b + 1)
                for t in range(TT):
                    last = te.matmul(bank[1 + t // 2][:, (t % 2) * 256:(t % 2) * 256 + 256],
                                     xnT[:, t * P:(t + 1) * P], wproj[:, :], start=True, stop=True)
                last.then_inc(S["qk_done"], 1)
                for n in range(2 * TT):
                    pe.wait_ge(S["v_out"], b * 2 * TT + n + 1)
                    te.matmul(bank[3 + n % 2][:, :], xnT[:, (n // 2) * P:(n // 2 + 1) * P],
                              wv[:, (n % 2) * 512:(n % 2 + 1) * 512], start=True, stop=True)\
                        .then_inc(S["v_done"], 1)
                pe.wait_ge(S["bonus_ready"], b + 1)
                for t in range(TT):
                    last = te.transpose(bank[5][0:H, t * P:(t + 1) * P],
                                        bont[:, t * H:(t + 1) * H], ident)
                last.then_inc(S["bonus_turned"], 1)
                pe.wait_ge(S["max_ready"], b + 1)
                pe.sem_inc(S["seen"], 1)
                for t in range(TT):
                    last = te.transpose(bank[6][:, t * H:(t + 1) * H], mT[0:H, t * P:(t + 1) * P],
                                        ident[0:H, 0:H])
                last.then_inc(S["max_turned"], 1)

        def proj_act(act):
            se = nc.scalar
            act.wait_ge(S["fold_ready"], 1)
            se.activation(wproj[:, 128:256], bank[0][:, 0:128], ACT.Copy).then_inc(S["proj_ready"], 1)
            act.sem_inc(S["qk_out"], 1)
            act.sem_inc(S["v_out"], 2)
            with act.Fori(0, B) as b:
                act.wait_ge(S["xn_turned"], b + 2)
                se.activation(xnT[:, :], bank[0][:, :], ACT.Copy).then_inc(S["xnT_ready"], 1)
                act.wait_ge(S["qk_done"], b + 1)
                act.wait_ge(S["qk_used"], b + 1)
                for half in range(2):
                    src = bank[1 + half][:, :].rearrange("p (t k g c) -> p t (k g) c", t=2, k=4, g=NG)
                    dst = qk.rearrange("p k (g t r) d -> p t (k g) (r d)", g=NG, t=TT)
                    dsq = sq.rearrange("p (k g t c) -> p t (k g) c", k=3, g=NG, t=TT)
                    for t in range(2):
                        se.activation(dsq[:, 2 * half + t], src[:, t, 0:3 * NG], ACT.Square)
                        last = se.activation(dst[:, 2 * half + t], src[:, t], ACT.Copy)
                last.then_inc(S["qk_out"], 1)
                for n in range(2 * TT):
                    act.wait_ge(S["v_done"], b * 2 * TT + n + 1)
                    for g in range(2):
                        last = se.activation(V[:, b, 2 * (n % 2) + g, n // 2, :, 0:DV],
                                             bank[3 + n % 2][:, g * 256:(g + 1) * 256]
                                             .rearrange("p (r w) -> p r w", r=HG), ACT.Copy)
                    last.then_inc(S["v_out"], 1)
                act.wait_ge(S["dots_ready"], b + 1)
                se.activation(sig.rearrange("p j d -> p (j d)"), dots, ACT.Tanh, scale=1.5)\
                    .then_inc(S["tanh_ready"], 1)

        def proj_pool(pool):
            ge = nc.gpsimd
            with pool.Fori(0, B) as b:
                pool.wait_ge(S["sig_ready"], b + 1)
                ge.tensor_tensor(lvl[:, :, :], bdf[:, :, :], sig[:, :, 3:4].to_broadcast([P, J, 8]), ALU.mult)
                pool.drain()
                ge.tensor_tensor(lvl[:, :, :], lvl[:, :, :], blo[:, :, :], ALU.add)
                for r, n in ((2, 4), (1, 2), (0, 1)):
                    pool.drain()
                    ge.tensor_tensor(dif[:, :, 0:n], lvl[:, :, n:2 * n], lvl[:, :, 0:n], ALU.subtract)
                    pool.drain()
                    ge.tensor_tensor(dif[:, :, 0:n], dif[:, :, 0:n], sig[:, :, r:r + 1].to_broadcast([P, J, n]),
                                     ALU.mult)
                    pool.drain()
                    dst = lvl[:, :, 0:n] if n > 1 else bon.rearrange("p (j c) -> p j c", c=1)
                    ge.tensor_tensor(dst, lvl[:, :, 0:n], dif[:, :, 0:n], ALU.add)
                pool.drain()
                ge.tensor_copy(bont[:, :].rearrange("p (t g r) -> p t g r", g=NG, t=TT),
                               bon.rearrange("p (g t r) -> p t g r", g=NG, t=TT)).then_inc(S["bonus_ready"], 1)
                pool.drain()

        def split(v, parts):
            n = v.shape[1]
            ve.tensor_copy(parts[:, 0, :], v)
            ve.drain()
            ve.tensor_tensor(res[:, 0:n], v, parts[:, 0, :], ALU.subtract)
            ve.drain()
            ve.tensor_copy(parts[:, 1, :], res[:, 0:n])
            ve.drain()
            ve.tensor_tensor(res[:, 0:n], res[:, 0:n], parts[:, 1, :], ALU.subtract)
            ve.drain()
            ve.tensor_copy(parts[:, 2, :], res[:, 0:n])
            ve.drain()

        def place(dst, b, slots, src, width):
            d = dst[:, bass.ds(b * NG, NG), :].rearrange("p g (q s) -> p (g q) s", s=SLOT)
            for s in slots:
                ve.tensor_copy(d[:, :, s:s + width], src.rearrange("p (j w) -> p j w", w=width))

        def proj_dve(dve):
            dve.wait_ge(S["loads"], 7 * 16)
            ve.tensor_copy(identb[:, :], ident).then_inc(S["consts_ready"], 1)
            for s in (qs, ks):
                ve.memset(s[:, :, :].rearrange("p s n -> p (s n)"), 0.0)
            ve.memset(Vs[:, :, :, :, DV:VW].rearrange("p s t r w -> p (s t r) w"), 1.0)
            for t in range(TT):
                hi = btab[:, :, 8:16].rearrange("p (g r) c -> p g r c", g=NG)
                lo = btab[:, :, 0:8].rearrange("p (g r) c -> p g r c", g=NG)
                ve.tensor_tensor(bdf[:, :, :].rearrange("p (g t r) c -> p t g r c", g=NG, t=TT)[:, t], hi, lo,
                                 ALU.subtract)
                ve.tensor_copy(blo[:, :, :].rearrange("p (g t r) c -> p t g r c", g=NG, t=TT)[:, t], lo)
            ve.drain()
            ve.memset(qs[:, :, :].rearrange("p s (q n) -> p (s q) n", n=SLOT)[:, :, 24:27], 1.0)
            ve.memset(ks[:, :, :].rearrange("p s (q n) -> p (s q) n", n=SLOT)[:, :, 27:30], 1.0)
            dve.sem_inc(S["qk_used"], 1)
            with dve.Fori(0, B) as b:
                dve.wait_ge(S["xn_turned"], b + 1)
                layernorm(b, lambda t: xn[:, t, :]).then_inc(S["xn_ready"], 1)
                dve.wait_ge(S["qk_out"], b + 2)
                ve.tensor_reduce(n2, sq.rearrange("p (j d) -> p j d", d=DK), AX.X, ALU.add)
                ve.drain()
                ve.tensor_scalar(nv[:, :], n2[:, 0:2 * J], NORM2, None, ALU.max)
                ve.drain()
                rsqrt(nv[:, :], rqk, nt[:, :])
                rq, rk = rqk[:, 0:J], rqk[:, J:2 * J]

                def wide(v):
                    return v.rearrange("p (j d) -> p j d", d=1).to_broadcast([P, J, DK])

                def by4(v):
                    return v.rearrange("p (j d) -> p j d", d=DK)

                ve.tensor_tensor(by4(dots), qk[:, 3], wide(rk), ALU.mult).then_inc(S["dots_ready"], 1)
                ve.tensor_tensor(by4(kv), qk[:, 1], wide(rk), ALU.mult)
                ve.tensor_tensor(nv[:, 0:J], n2[:, 2 * J:3 * J], rq, ALU.mult)
                ve.drain()
                ve.tensor_tensor(nv[:, 0:J], nv[:, 0:J], rq, ALU.mult)
                ve.drain()
                ve.tensor_scalar(nv[:, 0:J], nv[:, 0:J], NORM2, None, ALU.max)
                ve.drain()
                rsqrt(nv[:, 0:J], ru, nt[:, 0:J])
                ve.scalar_tensor_tensor(fu, ru, 1.0 / np.sqrt(DK), rq, ALU.mult, ALU.mult)
                ve.drain()
                ve.tensor_tensor(by4(qv), qk[:, 2], wide(fu), ALU.mult).then_inc(S["qk_used"], 1)
                dve.wait_ge(S["tanh_ready"], b + 1)
                ve.tensor_scalar(sig, sig, 0.5, 0.5, ALU.mult, ALU.add).then_inc(S["sig_ready"], 1)
                ve.drain()
                split(qv, part)
                place(qs, b, (0, 4, 8), part[:, 0, :], DK)
                place(qs, b, (12, 16), part[:, 1, :], DK)
                place(qs, b, (20,), part[:, 2, :], DK)
                ve.drain()
                split(kv, part)
                place(ks, b, (0, 12, 20), part[:, 0, :], DK)
                place(ks, b, (4, 16), part[:, 1, :], DK)
                place(ks, b, (8,), part[:, 2, :], DK)
                ve.drain()
                dve.wait_ge(S["bonus_turned"], b + 1)
                split(bon, mpart)
                for i in range(3):
                    place(ks, b, (24 + i,), mpart[:, i, :], 1)
                ve.tensor_copy(bT[0:H, :], bank[5][0:H, :])
                ve.drain()
                ve.tensor_tensor_scan(mT[0:H, :], bT[0:H, :], bT[0:H, :], LOW, ALU.max, ALU.max)\
                    .then_inc(S["max_ready"], 1)
                dve.wait_ge(S["max_turned"], b + 1)
                ve.tensor_scalar(mneg.rearrange("p (g t r) -> p t g r", g=NG, t=TT),
                                 bank[6][:, 0:J].rearrange("p (t g r) -> p t g r", t=TT, g=NG),
                                 -1.0, None, ALU.mult)
                ve.drain()
                split(mneg, mpart)
                for i in range(3):
                    place(qs, b, (27 + i,), mpart[:, i, :], 1)
                ve.drain()

        def turn(pe, te, s):
            pe.wait_ge(S["added"], s)
            for b_, src in ((QB, qs), (KB, ks)):
                for t in range(TT):
                    last = te.matmul(b_[:, t * P:(t + 1) * P], src[:, s, t * P:(t + 1) * P], identb[:, :],
                                     start=True, stop=True)
                last.then_inc(S["turned"], 1)

        def scores(pe, te, s, g):
            row = slice(SLOT * g, SLOT * (g + 1))
            for c in range(3):
                pe.wait_ge(S["expd"], 12 * s + 3 * g + c + 1)
                for k, off in CHUNKS[c]:
                    last = te.matmul(SB[(3 * g + c) % 4][:, off:off + T - k * P], kt[row, k * P:(k + 1) * P],
                                     qt[row, k * P:T], start=True, stop=True)
                last.then_inc(S["scored"], 1)

        def average(pe, te, s, g):
            pe.wait_ge(S["masked"], HG * s + g + 1)
            pe.wait_ge(S["normed"], HG * s + g + 1)
            for q in range(TT):
                for k in range(q + 1):
                    at = BLK[k] + (q - k) * P
                    last = te.matmul(AVB[g % 2][:, q * VW:(q + 1) * VW], probs[:, g, at:at + P],
                                     Vs[:, s, k, g, :], start=(k == 0), stop=(k == q))
            last.then_inc(S["averaged"], 1)

        def turn_out(pe, te, s):
            pe.wait_ge(S["normed"], HG * s + HG + 2)
            for c in range(2):
                for t in range(TT):
                    last = te.transpose((QB, KB)[c][:, t * P:(t + 1) * P], o[:, t, c * P:(c + 1) * P], ident)
                last.then_inc(S["o_turned"], 1)

        def project(pe, te, s):
            pe.wait_ge(S["o_copied"], 2 * s + 2)
            for t in range(TT):
                for c in range(2):
                    last = te.matmul(KB[:, t * P:(t + 1) * P], ot[:, c, t * P:(t + 1) * P],
                                     wo[:, (s % NG) * 2 + c, :], start=(c == 0), stop=(c == 1))
            last.then_inc(S["outed"], 1)

        def attn_pe(pe):
            te = nc.tensor
            pe.wait_ge(S["loads_late"], 7 * 16)

            def step(s, first=False, final=False):
                scores(pe, te, s, 1)
                average(pe, te, s, 0)
                if not first:
                    turn_out(pe, te, s - 1)
                scores(pe, te, s, 2)
                average(pe, te, s, 1)
                if not first:
                    project(pe, te, s - 1)
                scores(pe, te, s, 3)
                if not final:
                    turn(pe, te, s + 1)
                average(pe, te, s, 2)
                if not final:
                    pe.wait_ge(S["operands"], 2 * s + 4)
                    scores(pe, te, s + 1, 0)
                average(pe, te, s, 3)

            turn(pe, te, 0) if False else None
            for b_, src in ((QB, qs), (KB, ks)):
                for t in range(TT):
                    last = te.matmul(b_[:, t * P:(t + 1) * P], src[:, 0, t * P:(t + 1) * P], identb[:, :],
                                     start=True, stop=True)
                last.then_inc(S["turned"], 1)
            pe.wait_ge(S["operands"], 2)
            scores(pe, te, 0, 0)
            step(0, first=True)
            with pe.Fori(1, STEPS - 1) as s:
                step(s)
            step(STEPS - 1, final=True)
            turn_out(pe, te, STEPS - 1)
            project(pe, te, STEPS - 1)

        def attn_act(act):
            se = nc.scalar
            act.sem_inc(S["expd"], 4)

            def operands(s):
                act.wait_ge(S["turned"], 2 * s + 1)
                se.activation(qt[:, :], QB[:, :], ACT.Copy).then_inc(S["operands"], 1)
                act.wait_ge(S["turned"], 2 * s + 2)
                se.activation(kt[:, :], KB[:, :], ACT.Copy).then_inc(S["operands"], 1)

            def exps(s, g, reuse=True):
                if reuse:
                    act.wait_ge(S["averaged"], HG * s + g - PB + 1)
                for c in range(3):
                    act.wait_ge(S["scored"], 12 * s + 3 * g + c + 1)
                    se.activation(probs[:, g, 512 * c:512 * c + WIDTH[c]], SB[(3 * g + c) % 4][:, 0:WIDTH[c]],
                                  ACT.Exp).then_inc(S["expd"], 1)

            def outputs(s):
                for c in range(2):
                    act.wait_ge(S["o_turned"], 2 * s + c + 1)
                    se.activation(ot[:, c, :], (QB, KB)[c][:, :], ACT.Copy).then_inc(S["o_copied"], 1)

            def step(s, first=False, final=False):
                exps(s, 1, not first)
                if not first:
                    outputs(s - 1)
                exps(s, 2, not first)
                exps(s, 3, not first)
                if not final:
                    operands(s + 1)
                    exps(s + 1, 0)

            operands(0)
            exps(0, 0, False)
            step(0, first=True)
            with act.Fori(1, STEPS - 1) as s:
                step(s)
            step(STEPS - 1, final=True)
            outputs(STEPS - 1)

        def attn_pool(pool):
            ge = nc.gpsimd

            def mask(s, g):
                for c, at, n in ((0, BLK[0], 1), (1, BLK[1], 2), (2, BLK[2], 1)):
                    pool.wait_ge(S["expd"], 12 * s + 3 * g + c + 5)
                    pool.sem_inc(S["seen"], 1)
                    blk = probs[:, g, at:at + P] if n == 1 else \
                        bass.AP(probs[:, g, at:at + P].tensor, probs[:, g, at:at + P].offset,
                                [probs[:, g, at:at + P].ap[0], [BLK[3] - BLK[1], 2], [1, P]])
                    last = ge.affine_select(out=blk, in_=blk, compare_op=ALU.is_ge, fill=0.0, base=0,
                                            pattern=[[0, n], [1, P]] if n > 1 else [[1, P]],
                                            channel_multiplier=-1)
                last.then_inc(S["masked"], 1)

            with pool.Fori(0, STEPS) as s:
                for g in range(HG):
                    mask(s, g)

        def attn_dve(dve):
            dve.sem_inc(S["normed"], 2)
            dve.sem_inc(S["added"], 1)

            def norm(s, g):
                dve.wait_ge(S["averaged"], HG * s + g + 1)
                sums = AVB[g % 2][:, 0:TT * VW].rearrange("p (t w) -> p t w", w=VW)
                ve.reciprocal(rec[:, :], sums[:, :, DV])
                ve.drain()
                ve.tensor_tensor(o[:, :, g * DV:(g + 1) * DV], sums[:, :, 0:DV],
                                 rec[:, :].rearrange("p (t w) -> p t w", w=1).to_broadcast([P, TT, DV]),
                                 ALU.mult).then_inc(S["normed"], 1)
                ve.drain()

            def add(s):
                dve.wait_ge(S["outed"], s + 1)
                xs_ = x[:, bass.ds((s // NG) * TT, TT), :]
                ve.tensor_tensor(xs_, xs_, KB[:, :].rearrange("p (t d) -> p t d", t=TT), ALU.add)\
                    .then_inc(S["added"], 1)
                ve.drain()

            def step(s, first=False):
                if not first:
                    dve.wait_ge(S["o_turned"], 2 * s)
                norm(s, 0)
                norm(s, 1)
                if not first:
                    add(s - 1)
                norm(s, 2)
                norm(s, 3)

            step(0, first=True)
            with dve.Fori(1, STEPS) as s:
                step(s)
            add(STEPS - 1)


        late = [0]

        def room2(n):
            late[0] += n
            assert late[0] <= STEPS * TT * HG * VW
            return big[:, late[0] - n:late[0]]

        xall = room2(NT * D).rearrange("p (t d) -> p t d", t=NT)
        ghalf = room2(NT * U).rearrange("p (t u) -> p t u", t=NT)
        gsq = room2(NT * U).rearrange("p (t u) -> p t u", t=NT)
        sc = room2(TT * E).rearrange("p (t e) -> p t e", t=TT)
        pair1 = room2(TT * E * E).rearrange("p (t e j) -> p t e j", t=TT, e=E)
        pair2 = room2(TT * E * E).rearrange("p (t e j) -> p t e j", t=TT, e=E)
        rank = room2(TT * E).rearrange("p (t e) -> p t e", t=TT)
        gate = room2(TT * E).rearrange("p (t e) -> p t e", t=TT)
        xstat = room2(D)
        xT = room2(P)
        hT = room2(3 * 2 * P).rearrange("p (n c) -> p n c", n=3)
        hid = room2(3 * 2 * P).rearrange("p (n c) -> p n c", n=3)
        tan = room2(3 * 2 * P).rearrange("p (n c) -> p n c", n=3)

        MID, HTB, OUTB, XTB = bank[0:3], bank[3:6], bank[6], bank[7]
        NU = U * NT

        def route_dve(dve, f):
            with dve.Fori(0, B) as b:
                dve.wait_ge(S["x_turned"], f * B + b + 1)
                layernorm(b, lambda t: xn[:, t, :]).then_inc(S["x_static"], 1)
                ve.drain()
                ve.tensor_copy(xall[:, bass.ds(b * TT, TT), :], xn[:, :, :])
                dve.wait_ge(S["f_scored"], f * B + b + 1)
                ve.tensor_copy(sc[:, :, :], bank[2][:, 0:TT * E].rearrange("p (t e) -> p t e", t=TT))\
                    .then_inc(S["sc_ready"], 1)
                ve.drain()
                for t in range(TT):
                    mine = sc[:, t, :].rearrange("p (e j) -> p e j", j=1).to_broadcast([P, E, E])
                    theirs = sc[:, t:t + 1, :].to_broadcast([P, E, E])
                    ve.tensor_tensor(pair1[:, t], theirs, mine, ALU.is_gt)
                    ve.tensor_tensor(pair2[:, t], theirs, mine, ALU.is_ge)
                ve.drain()
                for t in range(TT):
                    ve.tensor_tensor(pair2[:, t], pair2[:, t], before.rearrange("p (e j) -> p e j", e=E), ALU.mult)
                ve.drain()
                ve.tensor_tensor(pair1[:, :, :, :], pair1[:, :, :, :], pair2[:, :, :, :], ALU.max)
                ve.drain()
                ve.tensor_reduce(rank[:, :, :], pair1[:, :, :, :], AX.X, ALU.add)
                ve.drain()
                ve.tensor_scalar(rank[:, :, :], rank[:, :, :], 2.0, None, ALU.is_lt)
                dve.wait_ge(S["tanh_ready"], B + f * B + b + 1)
                ve.tensor_scalar(gate[:, :, :], gate[:, :, :], 0.25, 0.25, ALU.mult, ALU.add)
                ve.drain()
                gh = ghalf[:, bass.ds(b * TT, TT), 0:E]
                ve.tensor_tensor(rank[:, :, :], gate[:, :, :], rank[:, :, :], ALU.mult)
                ve.drain()
                ve.tensor_copy(gh, rank[:, :, :])
                ve.scalar_tensor_tensor(gsq[:, bass.ds(b * TT, TT), 0:E], rank[:, :, :], 2.0, rank[:, :, :],
                                        ALU.mult, ALU.mult).then_inc(S["f_gated"], 1)
                ve.drain()

        def route_pe(pe, f):
            te = nc.tensor
            if f == 0:
                pe.sem_inc(S["x_turned"], 1)
            with pe.Fori(0, B) as b:
                pe.wait_ge(S["x_static"], f * B + b + 1)
                for t in range(TT):
                    last = te.transpose(bank[0][:, t * P:(t + 1) * P], xn[:, t, :], ident)
                last.then_inc(S["x_turned"], 1)
                pe.wait_ge(S["x_copied"], f * B + b + 1)
                pe.wait_ge(S["f_gated"], f * B + b + 1)
                for t in range(TT):
                    last = te.matmul(bank[2][:, t * E:(t + 1) * E], xnT[:, t * P:(t + 1) * P], wr[:, :],
                                     start=True, stop=True)
                last.then_inc(S["f_scored"], 1)

        def route_act(act, f):
            se = nc.scalar
            with act.Fori(0, B) as b:
                act.wait_ge(S["x_turned"], f * B + b + 2)
                se.activation(xnT[:, :], bank[0][:, :], ACT.Copy).then_inc(S["x_copied"], 1)
                act.wait_ge(S["sc_ready"], f * B + b + 1)
                se.activation(gate[:, :, :], sc[:, :, :], ACT.Tanh, scale=0.5).then_inc(S["tanh_ready"], 1)

        def moe_pe(pe, f):
            te = nc.tensor
            base = f * NU

            def turn_x(t):
                pe.wait_ge(S["m_static"], f * NT + t + 1)
                te.transpose(XTB[:, 0:P], xstat, ident).then_inc(S["m_turned"], 1)

            def mid(t, u):
                if u == 0:
                    pe.wait_ge(S["m_copied"], f * NT + t + 1)
                pe.wait_ge(S["hidden"], base + U * t + u + 1)
                te.matmul(MID[u % 3][:, :], xT, wff[:, u, :], start=True, stop=True).then_inc(S["mids"], 1)

            def turn_h(t, u):
                pe.wait_ge(S["hidden"], base + U * t + u + 4)
                pe.wait_ge(S["h_copied"], base + U * t + u + 1)
                for c in range(2):
                    last = te.transpose(HTB[u % 3][:, c * P:(c + 1) * P], hid[:, u % 3, c * P:(c + 1) * P], ident)
                last.then_inc(S["h_turned"], 1)

            def down(t, u):
                pe.wait_ge(S["h_copied"], base + U * t + u + 4)
                if u == 0:
                    pe.wait_ge(S["f_added"], f * NT + t + 1)
                for c in range(2):
                    last = te.matmul(OUTB[:, 0:D], hT[:, u % 3, c * P:(c + 1) * P], wfo[:, u, c, :],
                                     start=(u == 0 and c == 0), stop=(u == U - 1 and c == 1))
                if u == U - 1:
                    last.then_inc(S["f_out"], 1)

            def tile(t, first=False, final=False):
                for u in range(U):
                    mid(t, u)
                    for k, fn in ((2, turn_h), (3, down)):
                        if u >= k:
                            fn(t, u - k)
                        elif not first:
                            fn(t - 1, U + u - k)
                    if u == 5 and not final:
                        turn_x(t + 1)

            turn_x(0)
            tile(0, first=True)
            with pe.Fori(1, NT - 1) as t:
                tile(t)
            tile(NT - 1, final=True)
            turn_h(NT - 1, U - 2)
            down(NT - 1, U - 3)
            turn_h(NT - 1, U - 1)
            down(NT - 1, U - 2)
            down(NT - 1, U - 1)

        def moe_act(act, f):
            se = nc.scalar
            base = f * NU
            if f == 0:
                act.sem_inc(S["h_copied"], 3)

            def tanh(t, u):
                act.wait_ge(S["mids"], base + U * t + u + 1)
                se.activation(tan[:, u % 3, :], MID[u % 3][:, 0:FF], ACT.Tanh, scale=ghalf[:, t, u:u + 1])\
                    .then_inc(S["tanhs"], 1)

            def copy_h(t, u):
                act.wait_ge(S["h_turned"], base + U * t + u + 1)
                se.activation(hT[:, u % 3, :], HTB[u % 3][:, 0:2 * P], ACT.Copy).then_inc(S["h_copied"], 1)

            def copy_x(t):
                act.wait_ge(S["m_turned"], f * NT + t + 1)
                se.activation(xT, XTB[:, 0:P], ACT.Copy).then_inc(S["m_copied"], 1)

            def tile(t, first=False, final=False):
                for u in range(U):
                    tanh(t, u)
                    if u == U - 1 and not final:
                        copy_x(t + 1)
                    if u >= 2:
                        copy_h(t, u - 2)
                    elif not first:
                        copy_h(t - 1, U + u - 2)

            copy_x(0)
            tile(0, first=True)
            with act.Fori(1, NT - 1) as t:
                tile(t)
            tile(NT - 1, final=True)
            copy_h(NT - 1, U - 2)
            copy_h(NT - 1, U - 1)

        def moe_dve(dve, f):
            base = f * NU
            if f == 0:
                dve.sem_inc(S["hidden"], 3)
                dve.sem_inc(S["f_added"], 1)

            def hide(t, u):
                dve.wait_ge(S["tanhs"], base + U * t + u + 1)
                m = MID[u % 3]
                ve.scalar_tensor_tensor(tan[:, u % 3, :], tan[:, u % 3, :], 1.0, m[:, 0:FF], ALU.add, ALU.mult)
                ve.drain()
                ve.scalar_tensor_tensor(hid[:, u % 3, :], tan[:, u % 3, :], gsq[:, t, u:u + 1], m[:, FF:2 * FF],
                                        ALU.mult, ALU.mult).then_inc(S["hidden"], 1)

            def add(t):
                dve.wait_ge(S["f_out"], f * NT + t + 1)
                ve.tensor_tensor(x[:, t, :], x[:, t, :], OUTB[:, 0:D], ALU.add).then_inc(S["f_added"], 1)

            def tile(t, first=False):
                for u in range(U):
                    hide(t, u)
                    if u == 1 and not first:
                        add(t - 1)

            tile(0, first=True)
            with dve.Fori(1, NT) as t:
                tile(t)
            add(NT - 1)

        def moe_pool(pool, f):
            ge = nc.gpsimd
            ge.tensor_copy(xstat, xall[:, 0, :]).then_inc(S["m_static"], 1)
            with pool.Fori(1, NT) as t:
                pool.wait_ge(S["m_turned"], f * NT + t)
                ge.tensor_copy(xstat, xall[:, t, :]).then_inc(S["m_static"], 1)

        late[0] = 0
        qkv = room2(TT * 3 * D).rearrange("p (t c) -> p t c", t=TT)
        qT = room2(T)
        kT = room2(4 * T).rearrange("p (m n) -> p m n", m=4)
        sT = room2(2 * H * P).rearrange("p (n h q) -> p n h q", n=2, h=H)
        state = room2(D)
        stmp = room2(D)
        y = room2(T)
        zT = room2(T)
        st = room2(16)

        def retain_dve(dve):
            mean, var, mu, avar, dev, rs_, aa, bb = (st[:, i:i + 1] for i in range(8))
            with dve.Fori(0, B) as b:
                layernorm(b, lambda t: xn[:, t, :]).then_inc(S["r_ln"], 1)
                for t in range(TT):
                    dve.wait_ge(S["r_qkv"], b * TT + t + 1)
                    ve.tensor_tensor(qkv[:, t, 0:2 * D], bank[1 + t][:, 0:2 * D], cst[:, 512:768], ALU.mult)\
                        .then_inc(S["r_decayed"], 1)
                for t in range(TT):
                    dve.wait_ge(S["r_scored"], b * TT + t + 1)
                    for r in range(4):
                        last = ve.tensor_tensor(sT[:, t % 2, 4 * r:4 * r + 4, :],
                                                bank[1 + r][:, :].rearrange("p (h q) -> p h q", h=4),
                                                causal.rearrange("p (h q) -> p h q", h=1).to_broadcast([P, 4, P]),
                                                ALU.mult)
                    last.then_inc(S["r_masked"], 1)
                    if t < TT - 1:
                        dve.wait_ge(S["r_kv"], b * (TT - 1) + t + 1)
                        if t == 0:
                            ve.tensor_tensor(state, bank[5][:, 0:D], statemask, ALU.mult).then_inc(S["r_state"], 1)
                        else:
                            ve.tensor_tensor(stmp, bank[5][:, 0:D], statemask, ALU.mult)
                            ve.drain()
                            ve.scalar_tensor_tensor(state, state, decay128, stmp, ALU.mult, ALU.add)\
                                .then_inc(S["r_state"], 1)
                        ve.drain()
                dve.wait_ge(S["r_yT"], b + 1)
                ve.bn_stats(st6[:, 0, :], bank[0][:, :])
                ve.drain()
                ve.bn_aggr(st[:, 0:2], st6[:, 0, :])
                ve.drain()
                ve.tensor_copy(st[:, 8:10], st[:, 0:2]).then_inc(S["r_stats"], 1)
                dve.wait_ge(S["r_avg"], 2 * b + 1)
                ve.tensor_copy(st[:, 2:4], bank[6][:, 0:2])
                ve.drain()
                ve.tensor_tensor(dev, mean, mu, ALU.subtract)
                ve.drain()
                ve.tensor_tensor(dev, dev, dev, ALU.mult).then_inc(S["r_stats"], 1)
                dve.wait_ge(S["r_avg"], 2 * b + 2)
                ve.tensor_copy(rs_, bank[6][:, 2:3])
                ve.drain()
                ve.scalar_tensor_tensor(nv[:, 0:1], rs_, EPS, avar, ALU.add, ALU.add)
                ve.drain()
                rsqrt(nv[:, 0:1], ny[:, 0:1], nt[:, 0:1])
                ve.tensor_tensor(aa, ny[:, 0:1], gnw[:, 0:1], ALU.mult)
                ve.drain()
                ve.tensor_tensor(bb, mu, aa, ALU.mult)
                ve.drain()
                ve.tensor_tensor(bb, gnw[:, 1:2], bb, ALU.subtract)
                ve.drain()
                ve.tensor_scalar(zT, bank[0][:, :], aa, bb, ALU.mult, ALU.add).then_inc(S["r_z"], 1)
                dve.wait_ge(S["r_out"], b + 1)
                xb = x[:, bass.ds(b * TT, TT), :]
                ve.tensor_tensor(xb, xb, bank[6][:, :].rearrange("p (t d) -> p t d", t=TT), ALU.add)\
                    .then_inc(S["r_added"], 1)
                ve.drain()

        def retain_pe(pe):
            te = nc.tensor

            def score(b, t):
                for m in range(4):
                    for r in range(4):
                        row, tok = slice(32 * r, 32 * r + 32), slice(t * P, (t + 1) * P)
                        last = te.matmul(bank[1 + r][:, m * P:(m + 1) * P], kT[row, m, tok], qT[row, tok],
                                         start=True, stop=True)
                last.then_inc(S["r_scored"], 1)

            with pe.Fori(0, B) as b:
                pe.wait_ge(S["r_ln"], b + 1)
                for t in range(TT):
                    last = te.transpose(bank[0][:, t * P:(t + 1) * P], xn[:, t, :], ident)
                last.then_inc(S["r_turned"], 1)
                pe.wait_ge(S["r_xT"], b + 1)
                for t in range(TT):
                    te.matmul(bank[1 + t][:, 0:3 * D], xnT[:, t * P:(t + 1) * P], rqkv[:, :], start=True, stop=True)\
                        .then_inc(S["r_qkv"], 1)
                for t in range(TT):
                    pe.wait_ge(S["r_decayed"], b * TT + t + 1)
                    te.transpose(bank[5][:, t * P:(t + 1) * P], qkv[:, t, 0:D], ident)
                    last = te.transpose(bank[6][:, t * P:(t + 1) * P], qkv[:, t, D:2 * D], ident)
                last.then_inc(S["r_opT"], 1)
                pe.wait_ge(S["r_op"], b + 1)
                score(b, 0)
                for t in range(TT):
                    pe.wait_ge(S["r_masked"], b * TT + t + 1)
                    if t < TT - 1:
                        score(b, t + 1)
                    if t > 0:
                        pe.wait_ge(S["r_ycopied"], b * TT + t)
                        pe.wait_ge(S["r_state"], b * (TT - 1) + t)
                        te.matmul(bank[7][:, 0:D], qT[:, t * P:(t + 1) * P], state, start=True, stop=False)
                    for h in range(H):
                        last = te.matmul(bank[7][:, h * RD:(h + 1) * RD], sT[:, t % 2, h, :],
                                         qkv[:, t, 2 * D + h * RD:2 * D + (h + 1) * RD],
                                         start=(t == 0 and h == 0), stop=(h == H - 1))
                    last.then_inc(S["r_summed"], 1)
                    if t < TT - 1:
                        te.matmul(bank[5][:, 0:D], qkv[:, t, D:2 * D], qkv[:, t, 2 * D:3 * D], start=True, stop=True)\
                            .then_inc(S["r_kv"], 1)
                pe.wait_ge(S["r_ycopied"], b * TT + TT)
                for t in range(TT):
                    last = te.transpose(bank[0][:, t * P:(t + 1) * P], y[:, t * P:(t + 1) * P], ident)
                last.then_inc(S["r_yT"], 1)
                pe.wait_ge(S["r_stats"], 2 * b + 1)
                te.matmul(bank[6][:, 0:2], groupavg, st[:, 8:10], start=True, stop=True).then_inc(S["r_avg"], 1)
                pe.wait_ge(S["r_stats"], 2 * b + 2)
                te.matmul(bank[6][:, 2:3], groupavg, st[:, 4:5], start=True, stop=True).then_inc(S["r_avg"], 1)
                pe.wait_ge(S["r_z"], b + 1)
                for t in range(TT):
                    last = te.matmul(bank[6][:, t * P:(t + 1) * P], zT[:, t * P:(t + 1) * P], rwo[:, :],
                                     start=True, stop=True)
                last.then_inc(S["r_out"], 1)
                pe.wait_ge(S["r_added"], b + 1)

        def retain_act(act):
            se = nc.scalar
            with act.Fori(0, B) as b:
                act.wait_ge(S["r_turned"], b + 1)
                se.activation(xnT[:, :], bank[0][:, :], ACT.Copy).then_inc(S["r_xT"], 1)
                for t in range(TT):
                    act.wait_ge(S["r_decayed"], b * TT + t + 1)
                    se.activation(qkv[:, t, 2 * D:3 * D], bank[1 + t][:, 2 * D:3 * D], ACT.Copy)
                act.wait_ge(S["r_opT"], b + 1)
                se.activation(qT, bank[5][:, :], ACT.Copy)
                for m in range(4):
                    last = se.activation(kT[:, m, :], bank[6][:, :], ACT.Copy, scale=cst[:, 833 + m:834 + m])
                last.then_inc(S["r_op"], 1)
                for t in range(TT):
                    act.wait_ge(S["r_summed"], b * TT + t + 1)
                    se.activation(y[:, t * P:(t + 1) * P], bank[7][:, 0:D], ACT.Copy).then_inc(S["r_ycopied"], 1)

        @block.tensor
        def _(pe):
            proj_pe(pe)
            barrier(pe, 1)
            attn_pe(pe)
            barrier(pe, 2)
            n, f = 2, 0
            for st in stages:
                if st == "f":
                    route_pe(pe, f)
                    barrier(pe, n + 1)
                    moe_pe(pe, f)
                    n, f = n + 2, f + 1
                else:
                    retain_pe(pe)
                    n += 1
                barrier(pe, n)

        @block.scalar
        def _(act):
            proj_act(act)
            barrier(act, 1)
            attn_act(act)
            barrier(act, 2)
            n, f = 2, 0
            for st in stages:
                if st == "f":
                    route_act(act, f)
                    barrier(act, n + 1)
                    moe_act(act, f)
                    n, f = n + 2, f + 1
                else:
                    retain_act(act)
                    n += 1
                barrier(act, n)

        @block.gpsimd
        def _(pool):
            proj_pool(pool)
            barrier(pool, 1)
            attn_pool(pool)
            barrier(pool, 2)
            n, f = 2, 0
            for st in stages:
                if st == "f":
                    barrier(pool, n + 1)
                    moe_pool(pool, f)
                    n, f = n + 2, f + 1
                else:
                    n += 1
                barrier(pool, n)

        @block.vector
        def _(dve):
            proj_dve(dve)
            barrier(dve, 1)
            attn_dve(dve)
            barrier(dve, 2)
            n, f = 2, 0
            for st in stages:
                if st == "f":
                    if f == 0:
                        dve.sem_inc(S["f_gated"], 1)
                    ve.memset(ghalf[:, :, E:U].rearrange("p t u -> p (t u)"), 0.5)
                    ve.memset(gsq[:, :, E:U].rearrange("p t u -> p (t u)"), 0.5)
                    route_dve(dve, f)
                    barrier(dve, n + 1)
                    moe_dve(dve, f)
                    n, f = n + 2, f + 1
                else:
                    retain_dve(dve)
                    n += 1
                barrier(dve, n)


def host_layout(i):
    H, DK, D, P, E = 16, 4, 128, 128, 8
    f = lambda n: np.asarray(i[n])
    a = {}
    a["x_in"] = f("L0_attn_a_x")
    wq, wk = f("L0_attn_a_W_q"), f("L0_attn_a_W_k")
    a["w_qk"] = np.concatenate([wq.T, wk.T], 1)
    a["w_qk_rows"] = np.concatenate([wq, wk], 1)
    fold = np.zeros((H * DK, 2 * H * DK), np.float32)
    for h in range(H):
        s = slice(h * DK, (h + 1) * DK)
        fold[s, s] = f("L0_attn_a_W_nudge")[h]
        fold[s, slice(H * DK + h * DK, H * DK + (h + 1) * DK)] = f("L0_attn_a_simple_roots").T
    a["fold"] = fold
    a["w_v"] = f("L0_attn_a_W_v").T
    a["bonus"] = f("L0_attn_a_chamber_bonus")
    a["w_out"] = f("L0_attn_a_W_out").T.reshape(8, P, D).transpose(1, 0, 2)
    a["ret_qkv"] = np.concatenate([f(f"L0_attn_b_W{n}").T for n in "qkv"], 1)
    a["ret_o"] = f("L0_attn_b_Wo").T
    a["gn"] = np.stack([f("L0_attn_b_gn_w"), f("L0_attn_b_gn_b")], 1)
    a["router"] = f("L0_ffn_router_DE")
    pairs = [np.concatenate([f("L0_ffn_w_in_eDF")[e], f("L0_ffn_w_swiglu_eDF")[e]], 1) for e in range(E)]
    pairs.append(np.concatenate([f("L0_ffn_w_in_shared_FD").T, f("L0_ffn_w_swiglu_FD").T], 1))
    a["ffn_in"] = np.concatenate(pairs, 1)
    outs = [f("L0_ffn_w_out_eFD")[e] for e in range(E)] + [f("L0_ffn_w_out_shared_DF").T]
    a["ffn_out"] = np.concatenate([w.reshape(2, P, D).transpose(1, 0, 2).reshape(P, 2 * D) for w in outs], 1)
    gam = 1.0 - 2.0 ** (-5.0 - np.arange(H) * (8.0 / H))
    ch = np.repeat(gam, D // H)
    tok = np.arange(P)[:, None]
    same = (np.arange(D)[:, None] // 8 == np.arange(D)[None, :] // 8)
    c = [np.eye(P), np.arange(P)[:, None] <= np.arange(P)[None, :], same / 8.0, same * (ch[:, None] ** P),
         ch[None, :] ** tok / np.sqrt(8.0), ch[None, :] ** -tok,
         np.broadcast_to((np.arange(E)[None, :] < np.arange(E)[:, None]).reshape(1, -1), (P, E * E)),
         ch[:, None] ** P,
         (np.arange(D)[:, None] // 8 % 4 == np.arange(4)[None, :])]
    a["consts"] = np.concatenate([np.asarray(m, np.float32) for m in c], 1)
    return {n: np.ascontiguousarray(v) for n, v in a.items()}


def kernel(**inputs):
    import concourse.bacc as _bacc
    from concourse.bass_utils import run_bass_kernel_spmd as _run

    arrays = host_layout(inputs)
    nc = _bacc.Bacc("TRN2", target_bir_lowering=False, num_devices=1)
    args = [nc.dram_tensor(f"in_{n}", v.shape, mybir.dt.from_np(v.dtype), kind="ExternalInput").ap()
            for n, v in arrays.items()]
    res = nc.dram_tensor("out_0", arrays["x_in"].shape, mybir.dt.float32, kind="ExternalOutput").ap()
    hybrid_block_kernel(nc, *args, res)
    r = _run(nc, [{f"in_{n}": v for n, v in arrays.items()}], core_ids=[0])
    return r.results[0]["out_0"]
```

```python
import numpy as np
import concourse.bass as bass
from concourse import mybir
from contextlib import ExitStack


def hybrid_block_kernel(nc: bass.Bass, x_in: bass.AP, w_qk: bass.AP, w_qk_rows: bass.AP, fold: bass.AP,
                        w_v: bass.AP, bonus: bass.AP, w_out: bass.AP, ret_qkv: bass.AP, ret_o: bass.AP,
                        gn: bass.AP, router: bass.AP, ffn_in: bass.AP, ffn_out: bass.AP,
                        consts: bass.AP, out: bass.AP, stages: str = "frf"):
    F32 = mybir.dt.float32
    BF16 = mybir.dt.bfloat16
    I32 = mybir.dt.int32
    ALU = mybir.AluOpType
    ACT = mybir.ActivationFunctionType
    AX = mybir.AxisListType

    P = 128
    B, T, D = x_in.shape
    TT = T // P
    NT = B * TT
    H = 16
    HG = 4
    NG = H // HG
    STEPS = B * NG
    J = TT * H
    DK = 4
    DV = w_v.shape[1] // H
    VW = DV + 1
    SLOT = 32
    E = router.shape[1]
    U = E + 1
    FF = ffn_in.shape[1] // (2 * U)
    RD = D // H
    EPS = 1e-5
    NORM2 = 1e-24
    LOW = -3.0e38
    PB = 4
    SPAN = 10 * P

    xg = nc.dram_tensor("slot_rows", (40 * P, D + 2), F32, kind="Internal").ap()
    yg = nc.dram_tensor("slot_results", (40 * P, D), F32, kind="Internal").ap()

    ctx = ExitStack()
    with ctx:
        def sb(name, shape, dt=F32):
            return ctx.enter_context(nc.sbuf_tensor(name, shape, dt))

        def sem(name):
            return ctx.enter_context(nc.semaphore(name))

        x = sb("x", [P, NT, D])
        cst = sb("cst", [P, consts.shape[1]])
        ident = cst[:, 0:128]
        causal = cst[:, 128:256]
        groupavg = cst[:, 256:384]
        statemask = cst[:, 384:512]
        qdecay = cst[:, 512:640]
        kdecay = cst[:, 640:768]
        before = cst[:, 768:832]
        decay128 = cst[:, 832:833]
        identb = sb("identb", [P, P], BF16)
        wff = sb("wff", [P, U, 2 * FF])
        wfo = sb("wfo", [P, U, 2, D])
        wr = sb("wr", [P, E])
        rqkv = sb("rqkv", [P, 3 * D])
        rwo = sb("rwo", [P, D])
        gnw = sb("gnw", [P, 2])
        wproj = sb("wproj", [P, 4 * H * DK])
        wrows = sb("wrows", [H * DK, 2 * D])
        wfold = sb("wfold", [H * DK, 2 * H * DK])
        wv = sb("wv", [P, H * DV])
        wo = sb("wo", [P, 2 * NG, D])
        slots = sb("slots", [P, 2 * NT], I32)
        expert = sb("expert", [P, 40], I32)
        ints = sb("ints", [P, E], I32)
        ones = sb("ones", [P, P])
        zrow = sb("zrow", [P, D + 2])
        st6 = sb("st6", [P, TT, 6])
        mv = sb("mv", [P, TT, 2])
        nv = sb("nv", [P, 2 * J])
        ny = sb("ny", [P, 2 * J])
        nt = sb("nt", [P, 2 * J])
        xn = sb("xn", [P, TT, D])
        xnT = sb("xnT", [P, T])
        big = sb("big", [P, STEPS * TT * HG * VW])
        V = big[:, :].rearrange("p (b g t r w) -> p b g t r w", b=B, g=NG, t=TT, r=HG)
        Vs = big[:, :].rearrange("p (s t r w) -> p s t r w", s=STEPS, t=TT, r=HG)
        qs = sb("qs", [P, STEPS, TT * P], BF16)
        ks = sb("ks", [P, STEPS, TT * P], BF16)
        probs = sb("probs", [P, PB, SPAN])
        qt = sb("qt", [P, T], BF16)
        kt = sb("kt", [P, T], BF16)
        o = sb("o", [P, TT, HG * DV])
        ot = sb("ot", [P, 2, T])
        rec = sb("rec", [P, TT])

        room = probs[:, :, :].rearrange("p a n -> p (a n)")
        taken = [0]

        def take(n):
            taken[0] += n
            assert taken[0] <= PB * SPAN
            return room[:, taken[0] - n:taken[0]]

        qk = take(4 * J * DK).rearrange("p (k j d) -> p k j d", k=4, d=DK)
        sq = take(3 * J * DK)
        n2 = take(3 * J)
        rqk = take(2 * J)
        ru = take(J)
        fu = take(J)
        dots = take(J * DK)
        sig = take(J * DK).rearrange("p (j d) -> p j d", d=DK)
        bon = take(J)
        bont = take(J)
        mneg = take(J)
        bT = take(T)
        mT = take(T)
        res = take(J * DK)
        oflat = o[:, :, :].rearrange("p a n -> p (a n)")
        otflat = ot[:, :, :].rearrange("p a n -> p (a n)")
        qv, kv = oflat[:, 0:J * DK], oflat[:, J * DK:2 * J * DK]
        lvl = otflat[:, 0:J * 8].rearrange("p (j c) -> p j c", c=8)
        dif = otflat[:, J * 8:J * 12].rearrange("p (j c) -> p j c", c=4)
        btab = sb("btab", [P, H, 16])
        blo = sb("blo", [P, J, 8])
        bdf = sb("bdf", [P, J, 8])
        part = sb("part", [P, 3, J * DK], BF16)
        mpart = sb("mpart", [P, 3, J], BF16)

        bank = [ctx.enter_context(nc.psum_tensor(f"bank{i}", [P, 512], F32)) for i in range(8)]

        names = """loads loads_late consts_ready fold_ready proj_ready xn_ready xn_turned xnT_ready qk_done
            qk_out qk_used v_done v_out dots_ready tanh_ready sig_ready bonus_ready bonus_turned max_ready
            max_turned phase turned operands scored expd masked averaged normed o_turned o_copied outed added
            f_scored f_gated x_static x_turned x_copied mids tanhs hidden h_turned h_copied f_out f_added
            r_ln r_turned r_xT r_qkv r_decayed r_opT
            r_op r_opq r_qk r_v r_xn r_inv r_var r_affine r_zeroed r_vspread r_scored r_masked r_kv r_state
            r_summed r_ycopied r_stats r_avg r_z r_out r_added stored seen
            x_kept picked topped counted gated routed mapped scattered zeroed zero_set
            u_turned u_copied downs y_copied"""
        S = {n: sem(n) for n in names.split()}
        loaded = [sem(f"loaded{k}") for k in range(4)]
        stored_y = [sem(f"stored_y{k}") for k in range(4)]
        fetched = [sem(f"fetched{b}") for b in range(B)]
        block = ctx.enter_context(nc.Block())

        def barrier(eng, n):
            eng.drain().then_inc(S["phase"], 1)
            eng.wait_ge(S["phase"], 4 * n)

        FINAL = 4 * (2 + 2 * stages.count('f') + stages.count('r'))
        QB, KB, AVB, SB = bank[6], bank[7], bank[4:6], bank[0:4]
        BLK = [0, 512, 1024, 896]
        CHUNKS = [((0, 0),), ((1, 0), (3, 384)), ((2, 0),)]
        WIDTH = [512, 512, 256]

        ve = nc.vector

        def rsqrt(v, y, t):
            ve.tensor_scalar(y.bitcast(I32), v.bitcast(I32), 1, None, ALU.logical_shift_right)
            ve.drain()
            ve.tensor_scalar(y.bitcast(I32), y.bitcast(I32), -1.0, float(0x5f3759df), ALU.mult, ALU.add)
            ve.drain()
            for _ in range(3):
                ve.tensor_tensor(t, y, y, ALU.mult)
                ve.drain()
                ve.scalar_tensor_tensor(t, t, -0.5, v, ALU.mult, ALU.mult)
                ve.drain()
                ve.scalar_tensor_tensor(y, t, 1.5, y, ALU.add, ALU.mult)
                ve.drain()

        def layernorm(b, outs):
            for t in range(TT):
                ve.bn_stats(st6[:, t, :], x[:, b * TT + t, :])
            ve.drain()
            for t in range(TT):
                ve.bn_aggr(mv[:, t, :], st6[:, t, :])
            ve.drain()
            ve.tensor_scalar(nv[:, 0:TT], mv[:, :, 1], EPS, None, ALU.add)
            ve.drain()
            rsqrt(nv[:, 0:TT], ny[:, 0:TT], nt[:, 0:TT])
            for t in range(TT):
                last = ve.tensor_scalar(outs(t), x[:, b * TT + t, :], mv[:, t, 0:1], ny[:, t:t + 1],
                                        ALU.subtract, ALU.mult)
            return last

        def proj_pe(pe):
            te = nc.tensor
            pe.wait_ge(S["loads"], 7 * 16)
            pe.wait_ge(S["consts_ready"], 1)
            te.matmul(bank[0][:, 0:64], wrows[:, 0:D], wfold[:, 0:64], start=True, stop=True)
            te.matmul(bank[0][:, 64:128], wrows[:, D:2 * D], wfold[:, 64:128], start=True, stop=True)\
                .then_inc(S["fold_ready"], 1)
            pe.wait_ge(S["proj_ready"], 1)
            pe.sem_inc(S["xn_turned"], 1)
            with pe.Fori(0, B) as b:
                pe.wait_ge(S["xn_ready"], b + 1)
                for t in range(TT):
                    last = te.transpose(bank[0][:, t * P:(t + 1) * P], xn[:, t, :], ident)
                last.then_inc(S["xn_turned"], 1)
                pe.wait_ge(S["xnT_ready"], b + 1)
                pe.wait_ge(S["qk_out"], b + 1)
                for t in range(TT):
                    last = te.matmul(bank[1 + t // 2][:, (t % 2) * 256:(t % 2) * 256 + 256],
                                     xnT[:, t * P:(t + 1) * P], wproj[:, :], start=True, stop=True)
                last.then_inc(S["qk_done"], 1)
                for n in range(2 * TT):
                    pe.wait_ge(S["v_out"], b * 2 * TT + n + 1)
                    te.matmul(bank[3 + n % 2][:, :], xnT[:, (n // 2) * P:(n // 2 + 1) * P],
                              wv[:, (n % 2) * 512:(n % 2 + 1) * 512], start=True, stop=True)\
                        .then_inc(S["v_done"], 1)
                pe.wait_ge(S["bonus_ready"], b + 1)
                for t in range(TT):
                    last = te.transpose(bank[5][0:H, t * P:(t + 1) * P],
                                        bont[:, t * H:(t + 1) * H], ident)
                last.then_inc(S["bonus_turned"], 1)
                pe.wait_ge(S["max_ready"], b + 1)
                pe.sem_inc(S["seen"], 1)
                for t in range(TT):
                    last = te.transpose(bank[6][:, t * H:(t + 1) * H], mT[0:H, t * P:(t + 1) * P],
                                        ident[0:H, 0:H])
                last.then_inc(S["max_turned"], 1)

        def proj_act(act):
            se = nc.scalar
            act.wait_ge(S["fold_ready"], 1)
            se.activation(wproj[:, 128:256], bank[0][:, 0:128], ACT.Copy).then_inc(S["proj_ready"], 1)
            act.sem_inc(S["qk_out"], 1)
            act.sem_inc(S["v_out"], 2)
            with act.Fori(0, B) as b:
                act.wait_ge(S["xn_turned"], b + 2)
                se.activation(xnT[:, :], bank[0][:, :], ACT.Copy).then_inc(S["xnT_ready"], 1)
                act.wait_ge(S["qk_done"], b + 1)
                act.wait_ge(S["qk_used"], b + 1)
                for half in range(2):
                    src = bank[1 + half][:, :].rearrange("p (t k g c) -> p t (k g) c", t=2, k=4, g=NG)
                    dst = qk.rearrange("p k (g t r) d -> p t (k g) (r d)", g=NG, t=TT)
                    dsq = sq.rearrange("p (k g t c) -> p t (k g) c", k=3, g=NG, t=TT)
                    for t in range(2):
                        se.activation(dsq[:, 2 * half + t], src[:, t, 0:3 * NG], ACT.Square)
                        last = se.activation(dst[:, 2 * half + t], src[:, t], ACT.Copy)
                last.then_inc(S["qk_out"], 1)
                for n in range(2 * TT):
                    act.wait_ge(S["v_done"], b * 2 * TT + n + 1)
                    for g in range(2):
                        last = se.activation(V[:, b, 2 * (n % 2) + g, n // 2, :, 0:DV],
                                             bank[3 + n % 2][:, g * 256:(g + 1) * 256]
                                             .rearrange("p (r w) -> p r w", r=HG), ACT.Copy)
                    last.then_inc(S["v_out"], 1)
                act.wait_ge(S["dots_ready"], b + 1)
                se.activation(sig.rearrange("p j d -> p (j d)"), dots, ACT.Tanh, scale=1.5)\
                    .then_inc(S["tanh_ready"], 1)

        def proj_pool(pool):
            ge = nc.gpsimd
            with pool.Fori(0, B) as b:
                pool.wait_ge(S["sig_ready"], b + 1)
                ge.tensor_tensor(lvl[:, :, :], bdf[:, :, :], sig[:, :, 3:4].to_broadcast([P, J, 8]), ALU.mult)
                pool.drain()
                ge.tensor_tensor(lvl[:, :, :], lvl[:, :, :], blo[:, :, :], ALU.add)
                for r, n in ((2, 4), (1, 2), (0, 1)):
                    pool.drain()
                    ge.tensor_tensor(dif[:, :, 0:n], lvl[:, :, n:2 * n], lvl[:, :, 0:n], ALU.subtract)
                    pool.drain()
                    ge.tensor_tensor(dif[:, :, 0:n], dif[:, :, 0:n], sig[:, :, r:r + 1].to_broadcast([P, J, n]),
                                     ALU.mult)
                    pool.drain()
                    dst = lvl[:, :, 0:n] if n > 1 else bon.rearrange("p (j c) -> p j c", c=1)
                    ge.tensor_tensor(dst, lvl[:, :, 0:n], dif[:, :, 0:n], ALU.add)
                pool.drain()
                ge.tensor_copy(bont[:, :].rearrange("p (t g r) -> p t g r", g=NG, t=TT),
                               bon.rearrange("p (g t r) -> p t g r", g=NG, t=TT)).then_inc(S["bonus_ready"], 1)
                pool.drain()

        def split(v, parts):
            n = v.shape[1]
            ve.tensor_copy(parts[:, 0, :], v)
            ve.drain()
            ve.tensor_tensor(res[:, 0:n], v, parts[:, 0, :], ALU.subtract)
            ve.drain()
            ve.tensor_copy(parts[:, 1, :], res[:, 0:n])
            ve.drain()
            ve.tensor_tensor(res[:, 0:n], res[:, 0:n], parts[:, 1, :], ALU.subtract)
            ve.drain()
            ve.tensor_copy(parts[:, 2, :], res[:, 0:n])
            ve.drain()

        def place(dst, b, slots, src, width):
            d = dst[:, bass.ds(b * NG, NG), :].rearrange("p g (q s) -> p (g q) s", s=SLOT)
            for s in slots:
                ve.tensor_copy(d[:, :, s:s + width], src.rearrange("p (j w) -> p j w", w=width))

        def proj_dve(dve):
            dve.wait_ge(S["loads"], 7 * 16)
            ve.memset(ones[:, :], 1.0)
            ve.memset(zrow[:, :], 0.0).then_inc(S["zero_set"], 1)
            ve.tensor_copy(identb[:, :], ident).then_inc(S["consts_ready"], 1)
            for s in (qs, ks):
                ve.memset(s[:, :, :].rearrange("p s n -> p (s n)"), 0.0)
            ve.memset(Vs[:, :, :, :, DV:VW].rearrange("p s t r w -> p (s t r) w"), 1.0)
            for t in range(TT):
                hi = btab[:, :, 8:16].rearrange("p (g r) c -> p g r c", g=NG)
                lo = btab[:, :, 0:8].rearrange("p (g r) c -> p g r c", g=NG)
                ve.tensor_tensor(bdf[:, :, :].rearrange("p (g t r) c -> p t g r c", g=NG, t=TT)[:, t], hi, lo,
                                 ALU.subtract)
                ve.tensor_copy(blo[:, :, :].rearrange("p (g t r) c -> p t g r c", g=NG, t=TT)[:, t], lo)
            ve.drain()
            ve.memset(qs[:, :, :].rearrange("p s (q n) -> p (s q) n", n=SLOT)[:, :, 24:27], 1.0)
            ve.memset(ks[:, :, :].rearrange("p s (q n) -> p (s q) n", n=SLOT)[:, :, 27:30], 1.0)
            dve.sem_inc(S["qk_used"], 1)
            with dve.Fori(0, B) as b:
                dve.wait_ge(S["xn_turned"], b + 1)
                layernorm(b, lambda t: xn[:, t, :]).then_inc(S["xn_ready"], 1)
                dve.wait_ge(S["qk_out"], b + 2)
                ve.tensor_reduce(n2, sq.rearrange("p (j d) -> p j d", d=DK), AX.X, ALU.add)
                ve.drain()
                ve.tensor_scalar(nv[:, :], n2[:, 0:2 * J], NORM2, None, ALU.max)
                ve.drain()
                rsqrt(nv[:, :], rqk, nt[:, :])
                rq, rk = rqk[:, 0:J], rqk[:, J:2 * J]

                def wide(v):
                    return v.rearrange("p (j d) -> p j d", d=1).to_broadcast([P, J, DK])

                def by4(v):
                    return v.rearrange("p (j d) -> p j d", d=DK)

                ve.tensor_tensor(by4(dots), qk[:, 3], wide(rk), ALU.mult).then_inc(S["dots_ready"], 1)
                ve.tensor_tensor(by4(kv), qk[:, 1], wide(rk), ALU.mult)
                ve.tensor_tensor(nv[:, 0:J], n2[:, 2 * J:3 * J], rq, ALU.mult)
                ve.drain()
                ve.tensor_tensor(nv[:, 0:J], nv[:, 0:J], rq, ALU.mult)
                ve.drain()
                ve.tensor_scalar(nv[:, 0:J], nv[:, 0:J], NORM2, None, ALU.max)
                ve.drain()
                rsqrt(nv[:, 0:J], ru, nt[:, 0:J])
                ve.scalar_tensor_tensor(fu, ru, 1.0 / np.sqrt(DK), rq, ALU.mult, ALU.mult)
                ve.drain()
                ve.tensor_tensor(by4(qv), qk[:, 2], wide(fu), ALU.mult).then_inc(S["qk_used"], 1)
                dve.wait_ge(S["tanh_ready"], b + 1)
                ve.tensor_scalar(sig, sig, 0.5, 0.5, ALU.mult, ALU.add).then_inc(S["sig_ready"], 1)
                ve.drain()
                split(qv, part)
                place(qs, b, (0, 4, 8), part[:, 0, :], DK)
                place(qs, b, (12, 16), part[:, 1, :], DK)
                place(qs, b, (20,), part[:, 2, :], DK)
                ve.drain()
                split(kv, part)
                place(ks, b, (0, 12, 20), part[:, 0, :], DK)
                place(ks, b, (4, 16), part[:, 1, :], DK)
                place(ks, b, (8,), part[:, 2, :], DK)
                ve.drain()
                dve.wait_ge(S["bonus_turned"], b + 1)
                split(bon, mpart)
                for i in range(3):
                    place(ks, b, (24 + i,), mpart[:, i, :], 1)
                ve.tensor_copy(bT[0:H, :], bank[5][0:H, :])
                ve.drain()
                ve.tensor_tensor_scan(mT[0:H, :], bT[0:H, :], bT[0:H, :], LOW, ALU.max, ALU.max)\
                    .then_inc(S["max_ready"], 1)
                dve.wait_ge(S["max_turned"], b + 1)
                ve.tensor_scalar(mneg.rearrange("p (g t r) -> p t g r", g=NG, t=TT),
                                 bank[6][:, 0:J].rearrange("p (t g r) -> p t g r", t=TT, g=NG),
                                 -1.0, None, ALU.mult)
                ve.drain()
                split(mneg, mpart)
                for i in range(3):
                    place(qs, b, (27 + i,), mpart[:, i, :], 1)
                ve.drain()

        def turn(te, s, to, src):
            for t in range(TT):
                last = te.matmul(to[:, t * P:(t + 1) * P], src[:, s, t * P:(t + 1) * P], identb[:, :],
                                 start=True, stop=True)
            last.then_inc(S["turned"], 1)

        def scores(pe, te, s, g):
            row = slice(SLOT * g, SLOT * (g + 1))
            for c in range(3):
                pe.wait_ge(S["expd"], 12 * s + 3 * g + c + 1)
                for k, off in CHUNKS[c]:
                    last = te.matmul(SB[(3 * g + c) % 4][:, off:off + T - k * P], kt[row, k * P:(k + 1) * P],
                                     qt[row, k * P:T], start=True, stop=True)
                last.then_inc(S["scored"], 1)

        def average(pe, te, s, g, tiles=range(TT)):
            if 0 in tiles:
                pe.wait_ge(S["masked"], HG * s + g + 1)
                pe.wait_ge(S["normed"], HG * s + g + 1)
            for q in tiles:
                for k in range(q + 1):
                    at = BLK[k] + (q - k) * P
                    last = te.matmul(AVB[g % 2][:, q * VW:(q + 1) * VW], probs[:, g, at:at + P],
                                     Vs[:, s, k, g, :], start=(k == 0), stop=(k == q))
            if TT - 1 in tiles:
                last.then_inc(S["averaged"], 1)

        def turn_out(pe, te, s):
            pe.wait_ge(S["normed"], HG * s + HG + 2)
            for c in range(2):
                for t in range(TT):
                    last = te.transpose((QB, KB)[c][:, t * P:(t + 1) * P], o[:, t, c * P:(c + 1) * P], ident)
                last.then_inc(S["o_turned"], 1)

        def project(pe, te, s):
            pe.wait_ge(S["o_copied"], 2 * s + 2)
            for t in range(TT):
                for c in range(2):
                    last = te.matmul(KB[:, t * P:(t + 1) * P], ot[:, c, t * P:(t + 1) * P],
                                     wo[:, (s % NG) * 2 + c, :], start=(c == 0), stop=(c == 1))
            last.then_inc(S["outed"], 1)

        def attn_pe(pe):
            te = nc.tensor
            pe.wait_ge(S["loads_late"], 7 * 16)

            def step(s, first=False, final=False):
                scores(pe, te, s, 1)
                average(pe, te, s, 0)
                if not first:
                    turn_out(pe, te, s - 1)
                scores(pe, te, s, 2)
                average(pe, te, s, 1)
                if not first:
                    project(pe, te, s - 1)
                scores(pe, te, s, 3)
                if not final:
                    turn(te, s + 1, QB, qs)
                    average(pe, te, s, 2, (0, 1))
                    pe.wait_ge(S["added"], s + 1)
                    turn(te, s + 1, KB, ks)
                    average(pe, te, s, 2, (2, 3))
                    pe.wait_ge(S["operands"], 2 * s + 4)
                    scores(pe, te, s + 1, 0)
                else:
                    average(pe, te, s, 2)
                average(pe, te, s, 3)

            turn(te, 0, QB, qs)
            turn(te, 0, KB, ks)
            pe.wait_ge(S["operands"], 2)
            scores(pe, te, 0, 0)
            step(0, first=True)
            with pe.Fori(1, STEPS - 1) as s:
                step(s)
            step(STEPS - 1, final=True)
            turn_out(pe, te, STEPS - 1)
            project(pe, te, STEPS - 1)

        def attn_act(act):
            se = nc.scalar
            act.sem_inc(S["expd"], 4)

            def exps(s, g, reuse=True):
                if reuse:
                    act.wait_ge(S["averaged"], HG * s + g - PB + 1)
                for c in range(3):
                    act.wait_ge(S["scored"], 12 * s + 3 * g + c + 1)
                    se.activation(probs[:, g, 512 * c:512 * c + WIDTH[c]], SB[(3 * g + c) % 4][:, 0:WIDTH[c]],
                                  ACT.Exp).then_inc(S["expd"], 1)

            def step(s, first=False, final=False):
                exps(s, 1, not first)
                exps(s, 2, not first)
                exps(s, 3, not first)
                if not final:
                    exps(s + 1, 0)

            exps(0, 0, False)
            step(0, first=True)
            with act.Fori(1, STEPS - 1) as s:
                step(s)
            step(STEPS - 1, final=True)

        def attn_pool(pool):
            ge = nc.gpsimd

            def mask(s, g):
                for c, at, n in ((0, BLK[0], 1), (1, BLK[1], 2), (2, BLK[2], 1)):
                    pool.wait_ge(S["expd"], 12 * s + 3 * g + c + 5)
                    pool.sem_inc(S["seen"], 1)
                    blk = probs[:, g, at:at + P] if n == 1 else \
                        bass.AP(probs[:, g, at:at + P].tensor, probs[:, g, at:at + P].offset,
                                [probs[:, g, at:at + P].ap[0], [BLK[3] - BLK[1], 2], [1, P]])
                    last = ge.affine_select(out=blk, in_=blk, compare_op=ALU.is_ge, fill=0.0, base=0,
                                            pattern=[[0, n], [1, P]] if n > 1 else [[1, P]],
                                            channel_multiplier=-1)
                last.then_inc(S["masked"], 1)

            with pool.Fori(0, STEPS) as s:
                for g in range(HG):
                    mask(s, g)

        def attn_dve(dve):
            dve.sem_inc(S["normed"], 2)
            dve.sem_inc(S["added"], 1)

            def norm(s, g, first=False):
                dve.wait_ge(S["averaged"], HG * s + g + 1)
                sums = AVB[g % 2][:, 0:TT * VW].rearrange("p (t w) -> p t w", w=VW)
                ve.reciprocal(rec[:, :], sums[:, :, DV])
                ve.drain()
                if g == 0 and not first:
                    dve.wait_ge(S["o_turned"], 2 * s)
                ve.tensor_tensor(o[:, :, g * DV:(g + 1) * DV], sums[:, :, 0:DV],
                                 rec[:, :].rearrange("p (t w) -> p t w", w=1).to_broadcast([P, TT, DV]),
                                 ALU.mult).then_inc(S["normed"], 1)
                ve.drain()

            def add(s):
                dve.wait_ge(S["outed"], s + 1)
                xs_ = x[:, bass.ds((s // NG) * TT, TT), :]
                ve.tensor_tensor(xs_, xs_, KB[:, :].rearrange("p (t d) -> p t d", t=TT), ALU.add)\
                    .then_inc(S["added"], 1)
                ve.drain()

            def operands(s, c):
                dve.wait_ge(S["turned"], 2 * s + c + 1)
                ve.tensor_copy((qt, kt)[c][:, :], (QB, KB)[c][:, :]).then_inc(S["operands"], 1)

            def outputs(s):
                for c in range(2):
                    dve.wait_ge(S["o_turned"], 2 * s + c + 1)
                    ve.tensor_copy(ot[:, c, :], (QB, KB)[c][:, :]).then_inc(S["o_copied"], 1)

            def step(s, first=False, final=False):
                norm(s, 0, first)
                if not first:
                    outputs(s - 1)
                norm(s, 1)
                if not first:
                    add(s - 1)
                if not final:
                    operands(s + 1, 0)
                    operands(s + 1, 1)
                norm(s, 2)
                norm(s, 3)

            operands(0, 0)
            operands(0, 1)
            step(0, first=True)
            with dve.Fori(1, STEPS - 1) as s:
                step(s)
            step(STEPS - 1, final=True)
            outputs(STEPS - 1)
            add(STEPS - 1)

        RW = D + 2
        NB = 4
        NS = -(-((2 * NT * P + E * (P - 1)) // P) // NB) * NB
        late = [0]

        def room2(n):
            late[0] += n
            assert late[0] <= STEPS * TT * HG * VW
            return big[:, late[0] - n:late[0]]

        back = room2(NT * 2 * D).rearrange("p (t k d) -> p t k d", t=NT, k=2)
        shared_room = late[0]
        rows = room2(2 * NT * RW).rearrange("p (k t w) -> p k t w", k=2, t=NT)
        sc = room2(NT * E).rearrange("p (t e) -> p t e", t=NT)
        pair1 = room2(NT * E * E).rearrange("p (t e j) -> p t e j", t=NT, e=E)
        pair2 = room2(NT * E * E).rearrange("p (t e j) -> p t e j", t=NT, e=E)
        rank = room2(NT * E).rearrange("p (t e) -> p t e", t=NT)
        pick = [room2(NT * E).rearrange("p (t e) -> p t e", t=NT) for _ in range(3)]
        tmpe = room2(NT * E).rearrange("p (t e) -> p t e", t=NT)
        tots = room2(NT * E)
        cums = room2(NT * E)
        prev = room2(E)
        ntile = room2(E)
        tend = room2(E)
        tbase = room2(E)
        top = room2(2 * NT).rearrange("p (k t) -> p k t", k=2)
        gts = room2(2 * NT).rearrange("p (k t) -> p k t", k=2)
        slotf = room2(2 * NT)
        exf = room2(NS)
        tileno = cst[:, 837:837 + NS]
        assert late[0] - shared_room <= 9000
        late[0] = shared_room + 2 * NT * RW
        xs = room2(NB * RW).rearrange("p (n w) -> p n w", n=NB)
        xT = room2(NB * P).rearrange("p (n c) -> p n c", n=NB)
        tan = room2(NB * FF).rearrange("p (n c) -> p n c", n=NB)
        hid = room2(NB * FF).rearrange("p (n c) -> p n c", n=NB)
        hT = room2(NB * FF).rearrange("p (n c) -> p n c", n=NB)
        ys = room2(NB * D).rearrange("p (n c) -> p n c", n=NB)
        MID, XTB, HTB, OUTB = bank[0:4], (bank[4], bank[7]), bank[5], bank[6]

        def route_dve(dve, f):
            with dve.Fori(0, B) as b:
                dve.wait_ge(S["x_kept"], f * B + b + 1)
                layernorm(b, lambda t: xn[:, t, :]).then_inc(S["x_static"], 1)
                ve.drain()
            dve.wait_ge(S["f_scored"], (f + 1) * B)
            ve.tensor_copy(sc[:, :, :], bank[2][:, 0:NT * E].rearrange("p (t e) -> p t e", t=NT))
            ve.drain()
            for t in range(NT):
                mine = sc[:, t, :].rearrange("p (e j) -> p e j", j=1).to_broadcast([P, E, E])
                theirs = sc[:, t:t + 1, :].to_broadcast([P, E, E])
                ve.tensor_tensor(pair1[:, t], theirs, mine, ALU.is_gt)
                ve.tensor_tensor(pair2[:, t], theirs, mine, ALU.is_ge)
            ve.drain()
            beforeb = before.rearrange("p (t c) -> p t c", t=1).to_broadcast([P, NT, E * E])
            flat1 = pair1[:, :, :, :].rearrange("p t e j -> p t (e j)")
            flat2 = pair2[:, :, :, :].rearrange("p t e j -> p t (e j)")
            ve.tensor_tensor(flat2, flat2, beforeb, ALU.mult)
            ve.drain()
            ve.tensor_tensor(flat1, flat1, flat2, ALU.max)
            ve.drain()
            ve.tensor_reduce(rank[:, :, :], pair1[:, :, :, :], AX.X, ALU.add)
            ve.drain()
            ve.tensor_scalar(pick[2][:, :, :], rank[:, :, :], 2.0, None, ALU.is_lt).then_inc(S["picked"], 1)
            ve.tensor_scalar(pick[0][:, :, :], rank[:, :, :], 1.0, None, ALU.is_lt)
            ve.tensor_scalar(pick[1][:, :, :], rank[:, :, :], 1.0, None, ALU.is_equal)
            ve.drain()
            for k in range(2):
                ve.tensor_tensor(tmpe[:, :, :], pick[k][:, :, :], sc[:, :, :], ALU.mult)
                ve.drain()
                last = ve.tensor_reduce(top[:, k, :], tmpe[:, :, :], AX.X, ALU.add)
                ve.drain()
            last.then_inc(S["topped"], 1)
            dve.wait_ge(S["counted"], f + 1)
            ve.tensor_copy(tots.rearrange("p (e t) -> p e t", e=E),
                           bank[3][:, 0:NT * E].rearrange("p (t e) -> p e t", t=NT))
            ve.drain()
            ve.tensor_tensor_scan(cums, tots, tots, 0.0, ALU.add, ALU.bypass)
            ve.drain()
            ends = cums.rearrange("p (e t) -> p e t", e=E)[:, :, NT - 1]
            ve.memset(prev[:, 0:1], 0.0)
            ve.tensor_copy(prev[:, 1:E], ends[:, 0:E - 1])
            ve.drain()
            ve.tensor_tensor(cums, cums, tots, ALU.subtract)
            ve.drain()
            totl = tots.rearrange("p (e t) -> p e t", e=E)[:, :, NT - 1]
            ve.tensor_tensor(ntile, ends, totl, ALU.add)
            ve.drain()
            ve.tensor_tensor(ntile, ntile, prev, ALU.subtract)
            ve.drain()
            ve.tensor_scalar(ints[:, 0:E], ntile, float(P - 1), None, ALU.add)
            ve.drain()
            ve.tensor_scalar(ints[:, 0:E], ints[:, 0:E], 7, None, ALU.arith_shift_right)
            ve.drain()
            ve.tensor_copy(ntile, ints[:, 0:E])
            ve.drain()
            ve.tensor_tensor_scan(tend, ntile, ntile, 0.0, ALU.add, ALU.bypass)
            ve.drain()
            ve.tensor_tensor(tbase, tend, ntile, ALU.subtract)
            ve.drain()
            ve.scalar_tensor_tensor(tbase, tbase, float(P), prev, ALU.mult, ALU.subtract)
            ve.drain()
            ve.tensor_scalar(tbase, tbase, -1.0, None, ALU.add)
            ve.drain()
            cumv = cums.rearrange("p (e t) -> p e t", e=E)
            ve.tensor_tensor(cumv, cumv, tbase.rearrange("p (e t) -> p e t", t=1).to_broadcast([P, E, NT]), ALU.add)
            ve.drain()
            ve.tensor_tensor(tmpe[:, :, :], bank[4][:, 0:NT * E].rearrange("p (t e) -> p t e", t=NT),
                             cums.rearrange("p (e t) -> p t e", e=E), ALU.add)
            ve.drain()
            for k in range(2):
                ve.tensor_tensor(pick[k][:, :, :], pick[k][:, :, :], tmpe[:, :, :], ALU.mult)
            ve.drain()
            for k in range(2):
                ve.tensor_reduce(slotf[:, k * NT:(k + 1) * NT], pick[k][:, :, :], AX.X, ALU.add)
            ve.drain()
            ve.tensor_copy(slots[:, :], slotf)
            dve.wait_ge(S["gated"], f + 1)
            ve.tensor_scalar(gts[:, :, :], gts[:, :, :], 0.25, 0.25, ALU.mult, ALU.add)
            ve.drain()
            dve.wait_ge(S["x_kept"], (f + 1) * B + 1)
            ve.tensor_copy(rows[:, :, :, D], gts[:, :, :])
            ve.scalar_tensor_tensor(rows[:, :, :, D + 1], gts[:, :, :], 2.0, gts[:, :, :], ALU.mult, ALU.mult)\
                .then_inc(S["routed"], 1)
            for e in range(E):
                ve.drain()
                if e == 0:
                    ve.tensor_scalar(exf, tileno, tend[:, 0:1], None, ALU.is_ge)
                elif e < E - 1:
                    ve.scalar_tensor_tensor(exf, tileno, tend[:, e:e + 1], exf, ALU.is_ge, ALU.add)
            ve.drain()
            ve.tensor_copy(expert[:, :], exf).then_inc(S["mapped"], 1)
            ve.drain()

        def route_pe(pe, f):
            te = nc.tensor
            with pe.Fori(0, B) as b:
                pe.wait_ge(S["x_static"], f * B + b + 1)
                for t in range(TT):
                    last = te.transpose(bank[0][:, t * P:(t + 1) * P], xn[:, t, :], ident)
                last.then_inc(S["x_turned"], 1)
                pe.wait_ge(S["x_copied"], f * B + b + 1)
                for t in range(TT):
                    last = te.matmul(bank[2][:, bass.ds((b * TT + t) * E, E)], xnT[:, t * P:(t + 1) * P], wr[:, :],
                                     start=True, stop=True)
                last.then_inc(S["f_scored"], 1)
            pe.wait_ge(S["picked"], f + 1)
            either = pick[2][:, :, :].rearrange("p t e -> p (t e)")
            te.matmul(bank[3][:, 0:NT * E], ones[:, :], either, start=True, stop=True)
            te.matmul(bank[4][:, 0:NT * E], causal, either, start=True, stop=True).then_inc(S["counted"], 1)

        def route_act(act, f):
            se = nc.scalar
            if f == 0:
                act.sem_inc(S["x_kept"], 1)
            with act.Fori(0, B) as b:
                act.wait_ge(S["x_turned"], f * B + b + 1)
                se.activation(xnT[:, :], bank[0][:, :], ACT.Copy).then_inc(S["x_copied"], 1)
                for k in range(2):
                    last = se.activation(rows[:, k, bass.ds(b * TT, TT), 0:D], xn[:, :, :], ACT.Copy)
                last.then_inc(S["x_kept"], 1)
            act.wait_ge(S["topped"], f + 1)
            se.activation(gts[:, :, :], top[:, :, :], ACT.Tanh, scale=0.5).then_inc(S["gated"], 1)

        def scatter_pool(pool, f):
            pool.wait_ge(S["routed"], f + 1)
            pool.wait_ge(S["zeroed"], 16)
            for t in range(NT):
                for k in range(2):
                    c = k * NT + t
                    nc.gpsimd.indirect_dma_start(xg[:, :], bass.IndirectOffsetOnAxis(slots[:, c:c + 1], 0),
                                                 rows[:, k, t, :], None).then_inc(S["scattered"], 16)

        def fetch_pool(pool, f):
            for k in range(NB):
                pool.wait_ge(stored_y[k], 16 * ((f + 1) * NS // NB + 1))
            for t in range(NT):
                for k in range(2):
                    c = k * NT + t
                    nc.gpsimd.indirect_dma_start(back[:, t, k, :], None, yg[:, :],
                                                 bass.IndirectOffsetOnAxis(slots[:, c:c + 1], 0))\
                        .then_inc(fetched[t // TT], 16)

        def fetch_dve(dve, f):
            for b in range(B):
                dve.wait_ge(fetched[b], 16 * 2 * TT * (f + 1))
                for k in range(2):
                    ve.tensor_tensor(x[:, b * TT:(b + 1) * TT, :], x[:, b * TT:(b + 1) * TT, :],
                                     back[:, b * TT:(b + 1) * TT, k, :], ALU.add)
                    ve.drain()

        def units_of(f):
            at = f * (NT + NS)
            return ((at, NT // NB, True), (at + NT, NS // NB, False))

        def unit_loop(eng, turns, slot):
            for k in range(NB):
                slot(0, k, True, False)
            with eng.Fori(1, turns - 1) as i:
                for k in range(NB):
                    slot(i, k, False, False)
            for k in range(NB):
                slot(turns - 1, k, False, True)

        def ago(i, k, d):
            return (i, k - d) if k >= d else (i - 1, k - d + NB)

        def units_sp(sp, f):
            for base, turns, shared in units_of(f):
                if shared:
                    sp.wait_ge(S["routed"], f + 1)
                else:
                    sp.wait_ge(S["scattered"], 16 * 2 * NT * (f + 1))
                with sp.Fori(0, turns) as i:
                    for k in range(NB):
                        j = i * NB + k
                        sp.wait_ge(S["hidden"], base + j + 1)
                        src = rows[:, 0, j, :] if shared else xg[bass.ds(j * P, P), :]
                        sp.dma_start(xs[:, k, :], src).then_inc(loaded[k], 16)

        def units_pe(pe, f):
            te = nc.tensor
            for base, turns, shared in units_of(f):
                if not shared:
                    pe.wait_ge(S["mapped"], f + 1)

                def which(i, k):
                    if shared:
                        return U - 1
                    return pe.value_load(expert[0:1, bass.ds(i * NB + k, 1)], min_val=0, max_val=E - 1)

                def turn_x(i, k):
                    pe.wait_ge(loaded[k], 16 * (base // NB + i + 1))
                    pe.wait_ge(S["u_copied"], base + i * NB + k + 1)
                    te.transpose(XTB[k % 2][:, 0:P], xs[:, k, 0:D], ident).then_inc(S["u_turned"], 1)

                def mid(i, k, w):
                    pe.wait_ge(S["u_copied"], base + i * NB + k + 3)
                    pe.wait_ge(S["hidden"], base + i * NB + k + 1)
                    te.matmul(MID[k][:, :], xT[:, k, :], wff[:, w, :], start=True, stop=True)\
                        .then_inc(S["mids"], 1)

                def turn_h(i, k):
                    pe.wait_ge(S["hidden"], base + i * NB + k + 1 + NB)
                    pe.wait_ge(S["h_copied"], base + i * NB + k + 1)
                    for c in range(2):
                        last = te.transpose(HTB[:, c * P:(c + 1) * P], hid[:, k, c * P:(c + 1) * P], ident)
                    last.then_inc(S["h_turned"], 1)

                def down(i, k, w):
                    pe.wait_ge(S["h_copied"], base + i * NB + k + 2)
                    pe.wait_ge(S["y_copied"], base + i * NB + k + 1)
                    for c in range(2):
                        last = te.matmul(OUTB[:, 0:D], hT[:, k, c * P:(c + 1) * P], wfo[:, w, c, :],
                                         start=(c == 0), stop=(c == 1))
                    last.then_inc(S["downs"], 1)

                def slot(i, k, first, final):
                    if k < NB - 1:
                        turn_x(i, k + 1)
                    elif not final:
                        turn_x(i + 1, 0)
                    mid(i, k, which(i, k))
                    if not first or k >= 2:
                        turn_h(*ago(i, k, 2))
                    if not first or k >= 3:
                        down(*ago(i, k, 3), which(*ago(i, k, 3)))

                turn_x(0, 0)
                unit_loop(pe, turns, slot)
                turn_h(turns - 1, NB - 2)
                down(turns - 1, NB - 3, which(turns - 1, NB - 3))
                turn_h(turns - 1, NB - 1)
                down(turns - 1, NB - 2, which(turns - 1, NB - 2))
                down(turns - 1, NB - 1, which(turns - 1, NB - 1))

        def units_act(act, f):
            se = nc.scalar
            if f == 0:
                act.sem_inc(S["h_copied"], 1)
                for k in range(NB):
                    act.sem_inc(stored_y[k], 16)
            for base, turns, shared in units_of(f):
                def copy_h(i, k):
                    act.wait_ge(S["h_turned"], base + i * NB + k + 1)
                    se.activation(hT[:, k, :], HTB[:, 0:FF], ACT.Copy).then_inc(S["h_copied"], 1)

                def store(i, k):
                    act.wait_ge(S["y_copied"], base + i * NB + k + 2)
                    act.dma_start(yg[bass.ds((i * NB + k) * P, P), :], ys[:, k, :]).then_inc(stored_y[k], 16)

                def slot(i, k, first, final):
                    act.wait_ge(S["mids"], base + i * NB + k + 1)
                    se.activation(tan[:, k, :], MID[k][:, 0:FF], ACT.Tanh, scale=0.5 if shared else xs[:, k, D:D + 1])\
                        .then_inc(S["tanhs"], 1)
                    if not first or k >= 2:
                        copy_h(*ago(i, k, 2))
                    if not first and not shared:
                        store(i - 1, k)

                unit_loop(act, turns, slot)
                copy_h(turns - 1, NB - 2)
                copy_h(turns - 1, NB - 1)
                if not shared:
                    for k in range(NB):
                        store(turns - 1, k)

        def units_dve(dve, f):
            if f == 0:
                dve.sem_inc(S["hidden"], NB)
                dve.sem_inc(S["y_copied"], 1)
                dve.sem_inc(S["u_copied"], 2)
            for base, turns, shared in units_of(f):
                def copy_x(i, k):
                    dve.wait_ge(S["u_turned"], base + i * NB + k + 1)
                    ve.tensor_copy(xT[:, k, :], XTB[k % 2][:, 0:P]).then_inc(S["u_copied"], 1)

                def hide(i, k):
                    dve.wait_ge(S["tanhs"], base + i * NB + k + 1)
                    ve.scalar_tensor_tensor(tan[:, k, :], tan[:, k, :], 1.0, MID[k][:, 0:FF], ALU.add, ALU.mult)
                    ve.drain()
                    ve.scalar_tensor_tensor(hid[:, k, :], tan[:, k, :], 0.5 if shared else xs[:, k, D + 1:D + 2],
                                            MID[k][:, FF:2 * FF], ALU.mult, ALU.mult).then_inc(S["hidden"], 1)

                def result(i, k):
                    dve.wait_ge(S["downs"], base + i * NB + k + 1)
                    if shared:
                        xj = x[:, i * NB + k, :]
                        ve.tensor_tensor(xj, xj, OUTB[:, 0:D], ALU.add).then_inc(S["y_copied"], 1)
                    else:
                        dve.wait_ge(stored_y[k], 16 * (f * NS // NB + i + 1))
                        ve.tensor_copy(ys[:, k, :], OUTB[:, 0:D]).then_inc(S["y_copied"], 1)

                def slot(i, k, first, final):
                    if k < NB - 1:
                        copy_x(i, k + 1)
                    elif not final:
                        copy_x(i + 1, 0)
                    if not first or k >= 1:
                        hide(*ago(i, k, 1))
                    if not first or k >= 3:
                        result(*ago(i, k, 3))

                copy_x(0, 0)
                unit_loop(dve, turns, slot)
                hide(turns - 1, NB - 1)
                for k in range(NB - 3, NB):
                    result(turns - 1, k)

        late[0] = 0
        RS = 2
        qk_d = room2(RS * TT * 2 * D).rearrange("p (n t c) -> p n t c", n=RS, t=TT)
        qT = room2(RS * T).rearrange("p (n c) -> p n c", n=RS)
        qR = room2(RS * 4 * T).rearrange("p (n t r c) -> p n t r c", n=RS, t=TT, r=4)
        kT = room2(RS * 4 * T).rearrange("p (n m c) -> p n m c", n=RS, m=4)
        sT = room2(2 * H * P).rearrange("p (n m r q) -> p n m r q", n=2, m=4, r=4)
        state = room2(D)
        stmp = room2(D)
        vm = room[:, 0:RS * TT * 4 * D].rearrange("p (n t m c) -> p n t m c", n=RS, t=TT, m=4)
        y = room[:, RS * TT * 4 * D:RS * TT * 4 * D + T]
        zT = room[:, RS * TT * 4 * D + T:RS * TT * 4 * D + 2 * T]
        st = sb("st", [P, 16])
        SCB, YB, STB, QKB, VB = (bank[1], bank[2]), (bank[0], bank[7]), bank[5], (bank[4], bank[6]), bank[3]

        def newton(e, v, y_, t):
            e.tensor_scalar(y_.bitcast(I32), y_.bitcast(I32), -1.0, float(0x5f3759df), ALU.mult, ALU.add)
            e.drain()
            for _ in range(3):
                e.tensor_tensor(t, y_, y_, ALU.mult)
                e.drain()
                e.tensor_tensor(t, t, v, ALU.mult)
                e.drain()
                e.tensor_scalar(t, t, -0.5, 1.5, ALU.mult, ALU.add)
                e.drain()
                e.tensor_tensor(y_, t, y_, ALU.mult)
                e.drain()

        mean, mu, avar, dev, msq, aa, bb = (st[:, i:i + 1] for i in (0, 2, 3, 4, 5, 6, 7))

        def r_stats_dve(dve, b):
            for t in range(TT):
                ve.bn_stats(st6[:, t, :], x[:, bass.ds(b * TT + t, 1), :].rearrange("p a d -> p (a d)"))
            ve.drain()
            for t in range(TT):
                ve.bn_aggr(mv[:, t, :], st6[:, t, :])
            ve.drain()
            ve.tensor_scalar(nv[:, 0:TT], mv[:, :, 1], EPS, None, ALU.add)
            ve.drain()
            ve.tensor_scalar(ny[:, 0:TT].bitcast(I32), nv[:, 0:TT].bitcast(I32), 1, None, ALU.logical_shift_right)\
                .then_inc(S["r_ln"], 1)
            ve.drain()

        def r_scale_dve(dve, b):
            dve.wait_ge(S["r_inv"], b + 1)
            for t in range(TT):
                last = ve.tensor_scalar(xn[:, t, :], x[:, bass.ds(b * TT + t, 1), :].rearrange("p a d -> p (a d)"),
                                        mv[:, t, 0:1], ny[:, t:t + 1], ALU.subtract, ALU.mult)
            last.then_inc(S["r_xn"], 1)

        def r_decay_dve(dve, b, n, c):
                dve.wait_ge(S["r_qk"], 2 * b + c + 1)
                ve.tensor_tensor(qk_d[:, n, 2 * c:2 * c + 2, :],
                                 QKB[c][:, :].rearrange("p (t c) -> p t c", t=2),
                                 cst[:, 512:768].rearrange("p (t c) -> p t c", t=1).to_broadcast([P, 2, 2 * D]),
                                 ALU.mult).then_inc(S["r_decayed"], 1)

        def r_mask_dve(dve, b, t, m):
            dve.wait_ge(S["r_scored"], (b * TT + t) * 4 + m + 1)
            ve.tensor_tensor(sT[:, t % 2, m, :, :],
                             SCB[m % 2][:, :].rearrange("p (h q) -> p h q", h=4),
                             causal.rearrange("p (h q) -> p h q", h=1).to_broadcast([P, 4, P]),
                             ALU.mult).then_inc(S["r_masked"], 1)

        def r_state_dve(dve, b, t):
            dve.wait_ge(S["r_kv"], b * (TT - 1) + t + 1)
            if t == 0:
                ve.tensor_tensor(state, STB[:, 0:D], statemask, ALU.mult).then_inc(S["r_state"], 1)
            else:
                ve.tensor_tensor(stmp, STB[:, 0:D], statemask, ALU.mult)
                ve.drain()
                ve.scalar_tensor_tensor(state, state, decay128, stmp, ALU.mult, ALU.add)\
                    .then_inc(S["r_state"], 1)
            ve.drain()

        def r_norm_dve(dve, b, part):
            if part == 0:
                dve.wait_ge(S["r_ycopied"], b + 1)
                ve.bn_stats(st6[:, 0, :], y)
                ve.drain()
                ve.bn_aggr(st[:, 8:10], st6[:, 0, :]).then_inc(S["r_stats"], 1)
                ve.drain()
            elif part == 1:
                dve.wait_ge(S["r_avg"], 2 * b + 1)
                ve.tensor_copy(st[:, 2:4], YBn(b)[:, 0:2])
                ve.drain()
                ve.tensor_tensor(dev, st[:, 8:9], mu, ALU.subtract)
                ve.drain()
                ve.tensor_tensor(dev, dev, dev, ALU.mult).then_inc(S["r_stats"], 1)
                ve.drain()
            elif part == 2:
                dve.wait_ge(S["r_avg"], 2 * b + 2)
                ve.tensor_copy(msq, YBn(b)[:, 2:3])
                ve.drain()
                ve.scalar_tensor_tensor(nv[:, TT:TT + 1], msq, EPS, avar, ALU.add, ALU.add)
                ve.drain()
                ve.tensor_scalar(ny[:, TT:TT + 1].bitcast(I32), nv[:, TT:TT + 1].bitcast(I32), 1, None,
                                 ALU.logical_shift_right).then_inc(S["r_var"], 1)
                ve.drain()
            else:
                dve.wait_ge(S["r_affine"], b + 1)
                ve.tensor_scalar(zT, y, aa, bb, ALU.mult, ALU.add).then_inc(S["r_z"], 1)

        def r_add_dve(dve, b, n):
            dve.wait_ge(S["r_out"], b + 1)
            xb = x[:, bass.ds(b * TT, TT), :]
            ve.tensor_tensor(xb, xb, YB[n][:, :].rearrange("p (t d) -> p t d", t=TT), ALU.add)\
                .then_inc(S["r_added"], 1)

        def YBn(b):
            return YB[parity[0]]

        parity = [0]

        def retain_loop(eng, batch):
            batch(0, 0, True, False)
            with eng.Fori(0, (B - 2) // RS) as i:
                for n in (1, 0):
                    batch(i * RS + 2 - n, n, False, False)
            batch(B - 1, 1, False, True)

        def retain_dve(dve):
            dve.sem_inc(S["r_masked"], 2)

            def batch(b, n, first, final):
                o_ = 1 - n
                for t in range(TT):
                    for r in range(4):
                        if t < TT - 1:
                            r_mask_dve(dve, b, t + 1, r)
                        elif not final:
                            r_mask_dve(dve, b + 1, 0, r)
                        if r == 0 and t > 0:
                            r_state_dve(dve, b, t - 1)
                        if not final:
                            if (t, r) == (0, 0):
                                r_scale_dve(dve, b + 1)
                            if (t, r) in ((1, 1), (1, 3)):
                                r_decay_dve(dve, b + 1, o_, r // 2)
                            if (t, r) == (2, 2) and not (isinstance(b, int) and b == B - 2):
                                r_stats_dve(dve, b + 2)
                        if not first:
                            parity[0] = o_
                            if (t, r) in ((0, 1), (1, 0), (2, 0), (3, 0)):
                                r_norm_dve(dve, b - 1, t)
                            if (t, r) == (3, 2):
                                r_add_dve(dve, b - 1, o_)
                ve.drain()

            r_stats_dve(dve, 0)
            r_scale_dve(dve, 0)
            r_stats_dve(dve, 1)
            for c in range(2):
                r_decay_dve(dve, 0, 0, c)
            for r in range(4):
                r_mask_dve(dve, 0, 0, r)
            retain_loop(dve, batch)
            parity[0] = (B - 1) % RS
            for part_ in range(4):
                r_norm_dve(dve, B - 1, part_)
            r_add_dve(dve, B - 1, (B - 1) % RS)
            ve.drain()

        def retain_pool(pool):
            ge = nc.gpsimd

            def ln(b):
                pool.wait_ge(S["r_ln"], b + 1)
                pool.sem_inc(S["seen"], 1)
                newton(ge, nv[:, 0:TT], ny[:, 0:TT], nt[:, 0:TT])
                pool.sem_inc(S["r_inv"], 1)

            def affine(b):
                pool.wait_ge(S["r_var"], b + 1)
                pool.sem_inc(S["seen"], 1)
                newton(ge, nv[:, TT:TT + 1], ny[:, TT:TT + 1], nt[:, TT:TT + 1])
                ge.tensor_tensor(aa, ny[:, TT:TT + 1], gnw[:, 0:1], ALU.mult)
                pool.drain()
                ge.tensor_tensor(bb, mu, aa, ALU.mult)
                pool.drain()
                ge.tensor_tensor(bb, gnw[:, 1:2], bb, ALU.subtract).then_inc(S["r_affine"], 1)
                pool.drain()

            ge.memset(room[:, 0:RS * TT * 4 * D], 0.0).then_inc(S["r_zeroed"], 1)
            ln(0)
            ln(1)
            with pool.Fori(0, B - 2) as b:
                ln(b + 2)
                affine(b)
            affine(B - 2)
            affine(B - 1)

        def r_turn_pe(pe, te, b):
            pe.wait_ge(S["r_xn"], b + 1)
            for t in range(TT):
                last = te.transpose(VB[:, t * P:(t + 1) * P], xn[:, t, :], ident)
            last.then_inc(S["r_turned"], 1)

        def r_project_pe(pe, te, b, c):
            if c == 0:
                pe.wait_ge(S["r_xT"], b + 1)
                pe.wait_ge(S["r_opq"], b + 1)
            for t in (2 * c, 2 * c + 1):
                last = te.matmul(QKB[c][:, (t % 2) * 2 * D:(t % 2 + 1) * 2 * D], xnT[:, t * P:(t + 1) * P],
                                 rqkv[:, 0:2 * D], start=True, stop=True)
            last.then_inc(S["r_qk"], 1)
            if c == 1:
                for t in range(TT):
                    last = te.matmul(VB[:, t * P:(t + 1) * P], xnT[:, t * P:(t + 1) * P], rqkv[:, 2 * D:3 * D],
                                     start=True, stop=True)
                last.then_inc(S["r_v"], 1)

        def r_operands_pe(pe, te, b, n):
            pe.wait_ge(S["r_decayed"], 2 * b + 2)
            for c in range(2):
                for t in range(TT):
                    last = te.transpose(QKB[c][:, t * P:(t + 1) * P], qk_d[:, n, t, c * D:(c + 1) * D], ident)
                last.then_inc(S["r_opT"], 1)

        def r_score_pe(pe, te, b, n, t, m):
            pe.wait_ge(S["r_masked"], (b * TT + t) * 4 + m + 1)
            te.matmul(SCB[m % 2][:, :], kT[:, n, m, t * P:(t + 1) * P],
                      qR[:, n, t, :, :].rearrange("p r c -> p (r c)"), start=True, stop=True)\
                .then_inc(S["r_scored"], 1)

        def r_average_pe(pe, te, b, n, t, r):
            tok = slice(t * P, (t + 1) * P)
            if r == 0:
                pe.wait_ge(S["r_masked"], (b * TT + t) * 4 + 4 + 2)
                pe.sem_inc(S["seen"], 1)
            for m in range(4):
                last = te.matmul(YB[n][32 * r:32 * r + 32, tok], vm[:, n, t, m, 32 * r:32 * r + 32],
                                 sT[:, t % 2, m, r, :], start=(m == 0), stop=(m == 3 and t == 0))
            if t > 0 and r == 3:
                pe.wait_ge(S["r_state"], b * (TT - 1) + t)
                last = te.matmul(YB[n][:, tok], state, qT[:, n, tok], start=False, stop=True)
            if t == TT - 1 and r == 3:
                last.then_inc(S["r_summed"], 1)

        def r_state_pe(pe, te, b, n, t):
            for m in range(4):
                last = te.matmul(STB[:, 0:D], qk_d[:, n, t, D:2 * D], vm[:, n, t, m, :],
                                 start=(m == 0), stop=(m == 3))
            last.then_inc(S["r_kv"], 1)

        def r_stat_pe(pe, te, b, n, part_):
            pe.wait_ge(S["r_stats"], 2 * b + part_ + 1)
            src, at = ((st[:, 8:10], slice(0, 2)), (st[:, 4:5], slice(2, 3)))[part_]
            te.matmul(YB[n][:, at], groupavg, src, start=True, stop=True).then_inc(S["r_avg"], 1)

        def r_out_pe(pe, te, b, n):
            pe.wait_ge(S["r_z"], b + 1)
            for t in range(TT):
                last = te.matmul(YB[n][:, t * P:(t + 1) * P], zT[:, t * P:(t + 1) * P], rwo[:, :],
                                 start=True, stop=True)
            last.then_inc(S["r_out"], 1)

        def retain_pe(pe):
            te = nc.tensor

            def batch(b, n, first, final):
                o_ = 1 - n
                if not first:
                    pe.wait_ge(S["r_added"], b)
                for t in range(TT):
                    for r in range(4):
                        if t < TT - 1:
                            r_score_pe(pe, te, b, n, t + 1, r)
                        elif not final:
                            if r == 0:
                                pe.wait_ge(S["r_op"], b + 2)
                            r_score_pe(pe, te, b + 1, o_, 0, r)
                        if (t, r) == (0, 0):
                            pe.wait_ge(S["r_vspread"], b + 1)
                        r_average_pe(pe, te, b, n, t, r)
                        if r == 3 and t < TT - 1:
                            r_state_pe(pe, te, b, n, t)
                        if not final:
                            if (t, r) == (0, 2):
                                r_turn_pe(pe, te, b + 1)
                            if (t, r) in ((1, 0), (1, 2)):
                                r_project_pe(pe, te, b + 1, r // 2)
                            if (t, r) == (2, 0):
                                r_operands_pe(pe, te, b + 1, o_)
                        if not first:
                            if (t, r) in ((0, 3), (1, 3)):
                                r_stat_pe(pe, te, b - 1, o_, t)
                            if (t, r) == (3, 1):
                                r_out_pe(pe, te, b - 1, o_)

            r_turn_pe(pe, te, 0)
            for c in range(2):
                r_project_pe(pe, te, 0, c)
            r_operands_pe(pe, te, 0, 0)
            pe.wait_ge(S["r_op"], 1)
            for r in range(4):
                r_score_pe(pe, te, 0, 0, 0, r)
            retain_loop(pe, batch)
            for part_ in range(2):
                r_stat_pe(pe, te, B - 1, (B - 1) % RS, part_)
            r_out_pe(pe, te, B - 1, (B - 1) % RS)

        def retain_act(act):
            se = nc.scalar
            act.sem_inc(S["r_opq"], 1)
            act.sem_inc(S["r_added"], 1)
            act.wait_ge(S["r_zeroed"], 1)

            def prepare(b, n):
                act.wait_ge(S["r_turned"], b + 1)
                se.activation(xnT[:, :], VB[:, :], ACT.Copy).then_inc(S["r_xT"], 1)
                act.wait_ge(S["r_v"], b + 1)
                vs = VB[:, :].rearrange("p (t r m c) -> p t m r c", t=TT, r=4, m=4)
                for m in range(4):
                    last = se.activation(vm[:, n, :, m, :].rearrange("p t (r m c) -> p t m r c", r=4, m=4)[:, :, m],
                                         vs[:, :, m], ACT.Copy)
                last.then_inc(S["r_vspread"], 1)
                act.wait_ge(S["r_opT"], 2 * b + 1)
                se.activation(qT[:, n, :], QKB[0][:, :], ACT.Copy)
                for r in range(4):
                    se.activation(qR[:, n, :, r, :], QKB[0][:, :].rearrange("p (t c) -> p t c", t=TT), ACT.Copy,
                                  scale=cst[:, 877 + r:878 + r])
                act.wait_ge(S["r_opT"], 2 * b + 2)
                for m in range(4):
                    last = se.activation(kT[:, n, m, :], QKB[1][:, :], ACT.Copy, scale=cst[:, 833 + m:834 + m])
                last.then_inc(S["r_op"], 1)
                act.sem_inc(S["r_opq"], 1)

            def batch(b, n, first, final):
                if not final:
                    prepare(b + 1, 1 - n)
                act.wait_ge(S["r_summed"], b + 1)
                if not first:
                    act.wait_ge(S["r_z"], b)
                se.activation(y, YB[n][:, :], ACT.Copy).then_inc(S["r_ycopied"], 1)

            prepare(0, 0)
            retain_loop(act, batch)

        @block.sync
        def _(sp):
            early = ((x[:], x_in.rearrange("b (t p) d -> p (b t) d", p=P)), (cst[:], consts),
                     (wproj[:, 0:2 * H * DK], w_qk), (wrows[:], w_qk_rows), (wfold[:], fold),
                     (btab[:], bonus.partition_broadcast(P)), (wv[:], w_v))
            for dst, src in early:
                sp.dma_start(dst, src).then_inc(S["loads"], 16)
            sp.wait_ge(S["zero_set"], 1)
            sp.dma_start(xg.rearrange("(j p) w -> p j w", p=P),
                         bass.AP(zrow[:, :].tensor, zrow[:, :].offset, [zrow[:, :].ap[0], [0, NS], [1, D + 2]])).then_inc(S["zeroed"], 16)
            late = ((wo[:], w_out), (wr[:], router), (wff[:], ffn_in), (wfo[:], ffn_out),
                    (rqkv[:], ret_qkv), (rwo[:], ret_o), (gnw[:], gn))
            for dst, src in late:
                sp.dma_start(dst, src).then_inc(S["loads_late"], 16)
            for f in range(stages.count("f")):
                units_sp(sp, f)
            sp.wait_ge(S["phase"], FINAL)
            sp.dma_start(out.rearrange("b (t p) d -> p (b t) d", p=P), x[:]).then_inc(S["stored"], 16)
            sp.wait_ge(S["stored"], 16)

        @block.tensor
        def _(pe):
            proj_pe(pe)
            barrier(pe, 1)
            attn_pe(pe)
            barrier(pe, 2)
            n, f = 2, 0
            for st in stages:
                if st == "f":
                    route_pe(pe, f)
                    barrier(pe, n + 1)
                    units_pe(pe, f)
                    n, f = n + 2, f + 1
                else:
                    retain_pe(pe)
                    n += 1
                barrier(pe, n)

        @block.scalar
        def _(act):
            proj_act(act)
            barrier(act, 1)
            attn_act(act)
            barrier(act, 2)
            n, f = 2, 0
            for st in stages:
                if st == "f":
                    route_act(act, f)
                    barrier(act, n + 1)
                    units_act(act, f)
                    n, f = n + 2, f + 1
                else:
                    retain_act(act)
                    n += 1
                barrier(act, n)

        @block.gpsimd
        def _(pool):
            proj_pool(pool)
            barrier(pool, 1)
            attn_pool(pool)
            barrier(pool, 2)
            n, f = 2, 0
            for st in stages:
                if st == "f":
                    barrier(pool, n + 1)
                    scatter_pool(pool, f)
                    fetch_pool(pool, f)
                    n, f = n + 2, f + 1
                else:
                    retain_pool(pool)
                    n += 1
                barrier(pool, n)

        @block.vector
        def _(dve):
            proj_dve(dve)
            barrier(dve, 1)
            attn_dve(dve)
            barrier(dve, 2)
            n, f = 2, 0
            for st in stages:
                if st == "f":
                    route_dve(dve, f)
                    barrier(dve, n + 1)
                    units_dve(dve, f)
                    fetch_dve(dve, f)
                    n, f = n + 2, f + 1
                else:
                    retain_dve(dve)
                    n += 1
                barrier(dve, n)


def host_layout(i):
    H, DK, D, P, E = 16, 4, 128, 128, 8
    f = lambda n: np.asarray(i[n])
    a = {}
    a["x_in"] = f("L0_attn_a_x")
    wq, wk = f("L0_attn_a_W_q"), f("L0_attn_a_W_k")
    a["w_qk"] = np.concatenate([wq.T, wk.T], 1)
    a["w_qk_rows"] = np.concatenate([wq, wk], 1)
    fold = np.zeros((H * DK, 2 * H * DK), np.float32)
    for h in range(H):
        s = slice(h * DK, (h + 1) * DK)
        fold[s, s] = f("L0_attn_a_W_nudge")[h]
        fold[s, slice(H * DK + h * DK, H * DK + (h + 1) * DK)] = f("L0_attn_a_simple_roots").T
    a["fold"] = fold
    a["w_v"] = f("L0_attn_a_W_v").T
    a["bonus"] = f("L0_attn_a_chamber_bonus")
    a["w_out"] = f("L0_attn_a_W_out").T.reshape(8, P, D).transpose(1, 0, 2)
    a["ret_qkv"] = np.concatenate([f(f"L0_attn_b_W{n}").T for n in "qkv"], 1)
    a["ret_o"] = f("L0_attn_b_Wo").T
    a["gn"] = np.stack([f("L0_attn_b_gn_w"), f("L0_attn_b_gn_b")], 1)
    a["router"] = f("L0_ffn_router_DE")
    pairs = [np.concatenate([f("L0_ffn_w_in_eDF")[e], f("L0_ffn_w_swiglu_eDF")[e]], 1) for e in range(E)]
    pairs.append(np.concatenate([f("L0_ffn_w_in_shared_FD").T, f("L0_ffn_w_swiglu_FD").T], 1))
    a["ffn_in"] = np.concatenate(pairs, 1)
    outs = [f("L0_ffn_w_out_eFD")[e] for e in range(E)] + [f("L0_ffn_w_out_shared_DF").T]
    a["ffn_out"] = np.concatenate([w.reshape(2, P, D).transpose(1, 0, 2).reshape(P, 2 * D) for w in outs], 1)
    gam = 1.0 - 2.0 ** (-5.0 - np.arange(H) * (8.0 / H))
    ch = np.repeat(gam, D // H)
    tok = np.arange(P)[:, None]
    same = (np.arange(D)[:, None] // 8 == np.arange(D)[None, :] // 8)
    c = [np.eye(P), np.arange(P)[:, None] <= np.arange(P)[None, :], same / 8.0, same * (ch[:, None] ** P),
         ch[None, :] ** tok / np.sqrt(8.0), ch[None, :] ** -tok,
         np.broadcast_to((np.arange(E)[None, :] < np.arange(E)[:, None]).reshape(1, -1), (P, E * E)),
         ch[:, None] ** P,
         (np.arange(D)[:, None] // 8 % 4 == np.arange(4)[None, :]),
         np.broadcast_to(np.arange(40)[None, :], (P, 40)),
         (np.arange(D)[:, None] // 32 == np.arange(4)[None, :])]
    a["consts"] = np.concatenate([np.asarray(m, np.float32) for m in c], 1)
    return {n: np.ascontiguousarray(v) for n, v in a.items()}


def kernel(**inputs):
    import concourse.bacc as _bacc
    from concourse.bass_utils import run_bass_kernel_spmd as _run

    arrays = host_layout(inputs)
    nc = _bacc.Bacc("TRN2", target_bir_lowering=False, num_devices=1)
    args = [nc.dram_tensor(f"in_{n}", v.shape, mybir.dt.from_np(v.dtype), kind="ExternalInput").ap()
            for n, v in arrays.items()]
    res = nc.dram_tensor("out_0", arrays["x_in"].shape, mybir.dt.float32, kind="ExternalOutput").ap()
    hybrid_block_kernel(nc, *args, res)
    r = _run(nc, [{f"in_{n}": v for n, v in arrays.items()}], core_ids=[0])
    return r.results[0]["out_0"]
```

```python
import numpy as np
import concourse.bass as bass
from concourse import mybir
from contextlib import ExitStack


def hybrid_block_kernel(nc: bass.Bass, x_in: bass.AP, w_qk: bass.AP, w_qk_rows: bass.AP, fold: bass.AP,
                        w_v: bass.AP, bonus: bass.AP, w_out: bass.AP, ret_qkv: bass.AP, ret_o: bass.AP,
                        gn: bass.AP, router: bass.AP, ffn_in: bass.AP, ffn_out: bass.AP,
                        consts: bass.AP, out: bass.AP):
    F32 = mybir.dt.float32
    BF16 = mybir.dt.bfloat16
    I32 = mybir.dt.int32
    ALU = mybir.AluOpType
    ACT = mybir.ActivationFunctionType
    AX = mybir.AxisListType

    P = 128
    B, T, D = x_in.shape
    TT = T // P
    NT = B * TT
    H = 16
    HG = 4
    NG = H // HG
    assert NG >= 3
    STEPS = B * NG
    J = TT * H
    DK = 4
    DV = w_v.shape[1] // H
    VW = DV + 1
    SLOT = 32
    E = router.shape[1]
    U = E + 1
    FF = ffn_in.shape[1] // (2 * U)
    EPS = 1e-5
    NORM2 = 1e-24
    LOW = -3.0e38
    PB = 4
    SPAN = 10 * P

    RW = D + 3
    NB = 4
    NS = -(-((2 * NT * P + E * (P - 1)) // P) // NB) * NB
    xg = [nc.dram_tensor(f"slot_rows{f}", (NS * P, RW), F32, kind="Internal").ap() for f in range(2)]
    yg = [nc.dram_tensor(f"results{f}", ((2 * NT + NS) * P, D), F32, kind="Internal").ap() for f in range(2)]

    ctx = ExitStack()
    with ctx:
        def sb(name, shape, dt=F32):
            return ctx.enter_context(nc.sbuf_tensor(name, shape, dt))

        def sem(name):
            return ctx.enter_context(nc.semaphore(name))

        x = sb("x", [P, NT, D])
        cst = sb("cst", [P, consts.shape[1]])
        ident = cst[:, 0:128]
        causal = cst[:, 128:256]
        groupavg = cst[:, 256:384]
        statemask = cst[:, 384:512]
        qkdecay = cst[:, 512:768]
        order = cst[:, 768:776]
        decay128 = cst[:, 832:833]
        keyheads = cst[:, 833:837]
        tileno = cst[:, 837:837 + NS]
        queryheads = cst[:, 837 + NS:841 + NS]
        rowno = cst[:, 841 + NS:841 + 2 * NT + 2 * NS]
        identb = sb("identb", [P, P], BF16)
        wff = sb("wff", [P, U, 2 * FF])
        wfo = sb("wfo", [P, U, 2, D])
        wr = sb("wr", [P, E])
        rqkv = sb("rqkv", [P, 3 * D])
        rwo = sb("rwo", [P, D])
        gnw = sb("gnw", [P, 2])
        wproj = sb("wproj", [P, 4 * H * DK])
        wrows = sb("wrows", [H * DK, 2 * D])
        wfold = sb("wfold", [H * DK, 2 * H * DK])
        wv = sb("wv", [P, H * DV])
        wo = sb("wo", [P, 2 * NG, D])
        slots = sb("slots", [P, 2 * NT], I32)
        expert = sb("expert", [P, NS], I32)
        ints = sb("ints", [P, E], I32)
        ones = sb("ones", [P, P])
        zrow = sb("zrow", [P, D + 2])
        homes = sb("homes", [P, 2 * NT + NS], I32)
        home = sb("home", [P, NB], I32)
        st6 = sb("st6", [P, NT + 1, 6])
        mv = sb("mv", [P, NT, 2])
        lninv = sb("lninv", [P, NT])
        nv = sb("nv", [P, 3 * J])
        ny = sb("ny", [P, 3 * J])
        nt = sb("nt", [P, 3 * J])
        xn = sb("xn", [P, TT, D])
        xnT = sb("xnT", [P, T])
        big = sb("big", [P, STEPS * TT * HG * VW])
        V = big[:, :].rearrange("p (b g t r w) -> p b g t r w", b=B, g=NG, t=TT, r=HG)
        Vs = big[:, :].rearrange("p (s t r w) -> p s t r w", s=STEPS, t=TT, r=HG)
        qks = sb("qks", [P, 2 * STEPS, TT * P], BF16)
        qs, ks = qks[:, 0:STEPS, :], qks[:, STEPS:2 * STEPS, :]
        probs = sb("probs", [P, PB, SPAN])
        qt = sb("qt", [P, T], BF16)
        kt = sb("kt", [P, T], BF16)
        o = sb("o", [P, TT, HG * DV])
        ot = sb("ot", [P, 2, T])
        rec = sb("rec", [P, TT])

        room = probs[:, :, :].rearrange("p a n -> p (a n)")
        taken = [0]

        def take(n):
            taken[0] += n
            assert taken[0] <= PB * SPAN
            return room[:, taken[0] - n:taken[0]]

        qk = take(4 * J * DK).rearrange("p (k j d) -> p k j d", k=4, d=DK)
        sq = take(3 * J * DK)
        n2 = take(3 * J)
        rqk = take(3 * J)
        fu = take(J)
        dots = take(J * DK)
        sig = take(J * DK).rearrange("p (j d) -> p j d", d=DK)
        bon = take(J)
        bont = take(J)
        mneg = take(J)
        bT = take(T)
        mT = take(T)
        res = take(J * DK)
        bonres = take(J)
        oflat = o[:, :, :].rearrange("p a n -> p (a n)")
        otflat = ot[:, :, :].rearrange("p a n -> p (a n)")
        qv, kv = oflat[:, 0:J * DK], oflat[:, J * DK:2 * J * DK]
        lvl = otflat[:, 0:J * 8].rearrange("p (j c) -> p j c", c=8)
        dif = otflat[:, J * 8:J * 12].rearrange("p (j c) -> p j c", c=4)
        btab = sb("btab", [P, H, 16])
        blo = sb("blo", [P, J, 8])
        bdf = sb("bdf", [P, J, 8])
        qpart = sb("qpart", [P, 3, J * DK], BF16)
        kpart = sb("kpart", [P, 3, J * DK], BF16)
        mpart = sb("mpart", [P, 3, J], BF16)
        bpart = sb("bpart", [P, 3, J], BF16)

        bank = [ctx.enter_context(nc.psum_tensor(f"bank{i}", [P, 512], F32)) for i in range(8)]

        names = """
            x_loaded x_rest loads loads_v loads_late consts_ready zero_set zeroed finished stored phase seen
            fold_ready proj_ready xn_ready xn_turned xnT_ready qk_done qk_out qk_used v_done v_out
            dots_ready tanh_ready sig_used bonus_ready bonus_turned max_ready max_turned max_used
            k_cleared k_parts k_placed
            turned operands scored expd masked averaged normed o_turned o_copied outed added
            x_static x_turned x_copied x_kept f_scored picked counted gated mapped routed scattered
            u_turned u_copied mids tanhs hidden h_turned h_copied downs y_copied homed
            r_zeroed r_xn r_turned r_xT r_qk r_v r_vspread r_decayed r_opT r_op r_opq r_scored r_masked
            r_kv r_state r_summed r_ycopied r_stats r_avg r_var r_affine r_z r_out r_added"""
        S = {n: sem(n) for n in names.split()}
        loaded = [sem(f"loaded{k}") for k in range(4)]
        stored_y = [sem(f"stored_y{k}") for k in range(4)]
        fetched = [sem(f"fetched{b}") for b in range(B)]
        block = ctx.enter_context(nc.Block())

        def projected(eng):
            eng.drain().then_inc(S["phase"], 1)
            eng.wait_ge(S["phase"], 4)

        QB, KB, AVB, SB = bank[6], bank[7], bank[4:6], bank[0:4]
        BLK = [0, 512, 1024, 896]
        CHUNKS = [((0, 0),), ((1, 0), (3, 384)), ((2, 0),)]
        WIDTH = [512, 512, 256]

        TINY = 1e-38

        ve = nc.vector

        def rsqrt(v, y, t):
            ve.tensor_scalar(y.bitcast(I32), v.bitcast(I32), 1, None, ALU.logical_shift_right)
            ve.drain()
            ve.tensor_scalar(y.bitcast(I32), y.bitcast(I32), -1.0, float(0x5f3759df), ALU.mult, ALU.add)
            ve.drain()
            for _ in range(3):
                ve.tensor_tensor(t, y, y, ALU.mult)
                ve.drain()
                ve.scalar_tensor_tensor(t, t, -0.5, v, ALU.mult, ALU.mult)
                ve.drain()
                ve.scalar_tensor_tensor(y, t, 1.5, y, ALU.add, ALU.mult)
                ve.drain()

        def layernorm_stats(tiles):
            tiles = list(tiles)
            for t in tiles:
                ve.bn_stats(st6[:, t, :], x[:, t, :])
            ve.drain()
            for t in tiles:
                ve.bn_aggr(mv[:, t, :], st6[:, t, :])
            ve.drain()
            inverse_deviations(slice(tiles[0], tiles[-1] + 1))

        def inverse_deviations(own):
            ve.tensor_scalar(nv[:, own], mv[:, own, 1], EPS, None, ALU.add)
            ve.drain()
            rsqrt(nv[:, own], lninv[:, own], nt[:, own])

        def normalise(b, outs, at=None):
            for t in range(TT):
                j = bass.ds(b * TT + t, 1)
                k = j if at is None else bass.ds(at + t, 1)
                last = ve.tensor_scalar(outs(t), x[:, j, :].rearrange("p a d -> p (a d)"),
                                        mv[:, k, 0:1].rearrange("p a d -> p (a d)"), lninv[:, k],
                                        ALU.subtract, ALU.mult)
            return last

        def normalise_early(b, part, rows):
            if part == 0:
                for t in range(TT):
                    ve.bn_stats(st6[:, t, :], x[:, bass.ds(b * TT + t, 1), :].rearrange("p a d -> p (a d)"))
                ve.drain()
                for t in range(TT):
                    ve.bn_aggr(mv[:, t, :], st6[:, t, :])
                ve.drain()
            elif part == 1:
                inverse_deviations(slice(0, TT))
                ve.drain()
            elif part == 2:
                normalise(b, lambda t: rows[:, 0, bass.ds(b * TT + t, 1), 0:D].rearrange("p a d -> p (a d)"),
                          at=0).then_inc(S["x_static"], 1)

        late_room = qks[:, :, :].rearrange("p s n -> p (s n)").bitcast(F32)
        rows_of = [v.rearrange("p (k t w) -> p k t w", k=2, t=NT)
                   for v in (big[:, 0:2 * NT * RW], late_room[:, STEPS * TT * P - 2 * NT * RW:STEPS * TT * P])]
        assert NT * RW <= NG * TT * HG * VW

        def proj_pe(pe):
            te = nc.tensor

            def project(b):
                pe.wait_ge(S["xn_ready"], b + 1)
                pe.sem_inc(S["seen"], 1)
                for t in range(TT):
                    last = te.transpose(bank[0][:, t * P:(t + 1) * P], xn[:, t, :], ident)
                last.then_inc(S["xn_turned"], 1)
                pe.wait_ge(S["xnT_ready"], b + 1)
                pe.wait_ge(S["qk_out"], b + 1)
                for t in range(TT):
                    last = te.matmul(bank[1 + t // 2][:, (t % 2) * 256:(t % 2) * 256 + 256],
                                     xnT[:, t * P:(t + 1) * P], wproj[:, :], start=True, stop=True)
                last.then_inc(S["qk_done"], 1)
                if isinstance(b, int) and b == 0:
                    pe.wait_ge(S["loads_v"], 2 * 16)
                for n in range(2 * TT):
                    pe.wait_ge(S["v_out"], b * 2 * TT + n + 1)
                    te.matmul(bank[3 + n % 2][:, :], xnT[:, (n // 2) * P:(n // 2 + 1) * P],
                              wv[:, (n % 2) * 512:(n % 2 + 1) * 512], start=True, stop=True)\
                        .then_inc(S["v_done"], 1)

            def turn_max(b):
                pe.wait_ge(S["max_ready"], b + 1)
                pe.wait_ge(S["max_used"], b + 1)
                pe.sem_inc(S["seen"], 1)
                for t in range(TT):
                    last = te.transpose(bank[6][:, t * H:(t + 1) * H], mT[0:H, t * P:(t + 1) * P],
                                        ident[0:H, 0:H])
                last.then_inc(S["max_turned"], 1)

            def turn_bonus(b):
                pe.wait_ge(S["bonus_ready"], b + 1)
                pe.sem_inc(S["seen"], 1)
                for t in range(TT):
                    last = te.transpose(bank[5][0:H, t * P:(t + 1) * P],
                                        bont[:, t * H:(t + 1) * H], ident)
                last.then_inc(S["bonus_turned"], 1)

            pe.wait_ge(S["loads"], 3 * 16)
            pe.wait_ge(S["consts_ready"], 1)
            te.matmul(bank[0][:, 0:64], wrows[:, 0:D], wfold[:, 0:64], start=True, stop=True)
            te.matmul(bank[0][:, 64:128], wrows[:, D:2 * D], wfold[:, 64:128], start=True, stop=True)\
                .then_inc(S["fold_ready"], 1)
            pe.wait_ge(S["proj_ready"], 1)
            pe.sem_inc(S["xn_turned"], 1)
            project(0)
            project(1)
            turn_bonus(0)
            with pe.Fori(1, B - 1) as b:
                project(b + 1)
                turn_max(b - 1)
                turn_bonus(b)
            turn_max(B - 2)
            turn_bonus(B - 1)
            turn_max(B - 1)

        def proj_act(act):
            se = nc.scalar
            act.wait_ge(S["fold_ready"], 1)
            se.activation(wproj[:, 128:256], bank[0][:, 0:128], ACT.Copy).then_inc(S["proj_ready"], 1)
            act.sem_inc(S["qk_out"], 1)
            act.sem_inc(S["v_out"], 2)

            def tanh(b):
                act.wait_ge(S["dots_ready"], b + 1)
                act.wait_ge(S["sig_used"], b + 1)
                se.activation(sig.rearrange("p j d -> p (j d)"), dots, ACT.Tanh, scale=1.5)\
                    .then_inc(S["tanh_ready"], 1)

            def copy_x(b):
                act.wait_ge(S["xn_turned"], b + 2)
                se.activation(xnT[:, :], bank[0][:, :], ACT.Copy).then_inc(S["xnT_ready"], 1)

            def copies(b):
                act.wait_ge(S["qk_done"], b + 1)
                act.wait_ge(S["qk_used"], b + 1)
                for half in range(2):
                    src = bank[1 + half][:, :].rearrange("p (t k g c) -> p t (k g) c", t=2, k=4, g=NG)
                    dst = qk.rearrange("p k (g t r) d -> p t (k g) (r d)", g=NG, t=TT)
                    dsq = sq.rearrange("p (k g t c) -> p t (k g) c", k=3, g=NG, t=TT)
                    for t in range(2):
                        se.activation(dsq[:, 2 * half + t], src[:, t, 0:3 * NG], ACT.Square)
                        last = se.activation(dst[:, 2 * half + t], src[:, t], ACT.Copy)
                last.then_inc(S["qk_out"], 1)

            def values(b, half):
                for n in range(half * TT, (half + 1) * TT):
                    act.wait_ge(S["v_done"], b * 2 * TT + n + 1)
                    for g in range(2):
                        last = se.activation(V[:, b, 2 * (n % 2) + g, n // 2, :, 0:DV],
                                             bank[3 + n % 2][:, g * 256:(g + 1) * 256]
                                             .rearrange("p (r w) -> p r w", r=HG), ACT.Copy)
                    last.then_inc(S["v_out"], 1)

            act.sem_inc(S["sig_used"], 1)
            act.wait_ge(S["k_cleared"], 1)
            def batch(b, final=False):
                copies(b)
                values(b, 0)
                values(b, 1)
                if not final:
                    copy_x(b + 1)
                tanh(b)
                act.wait_ge(S["k_parts"], b + 1)
                for slots_, i in (((0, 12, 20), 0), ((4, 16), 1), ((8,), 2)):
                    d = ks[:, bass.ds(b * NG, NG), :].rearrange("p g (q s) -> p (g q) s", s=SLOT)
                    for c in slots_:
                        last = se.activation(d[:, :, c:c + DK],
                                             kpart[:, i, :].rearrange("p (j w) -> p j w", w=DK), ACT.Copy)
                last.then_inc(S["k_placed"], 1)

            copy_x(0)
            with act.Fori(0, B - 1) as b:
                batch(b)
            batch(B - 1, True)

        def split(e, v, parts, left):
            n = v.shape[1]
            e.tensor_copy(parts[:, 0, :], v)
            e.drain()
            e.tensor_tensor(left[:, 0:n], v, parts[:, 0, :], ALU.subtract)
            e.drain()
            e.tensor_copy(parts[:, 1, :], left[:, 0:n])
            e.drain()
            e.tensor_tensor(left[:, 0:n], left[:, 0:n], parts[:, 1, :], ALU.subtract)
            e.drain()
            e.tensor_copy(parts[:, 2, :], left[:, 0:n])
            e.drain()

        def place(e, dst, b, slots_, src, width):
            d = dst[:, bass.ds(b * NG, NG), :].rearrange("p g (q s) -> p (g q) s", s=SLOT)
            for s in slots_:
                last = e.tensor_copy(d[:, :, s:s + width], src.rearrange("p (j w) -> p j w", w=width))
            return last

        def proj_pool(pool):
            ge = nc.gpsimd
            ge.memset(ks.rearrange("p s n -> p (s n)"), 0.0)
            ge.memset(Vs[:, :, :, :, DV:VW].rearrange("p s t r w -> p (s t r) w"), 1.0)
            pool.drain()
            ge.memset(ks.rearrange("p s (q n) -> p (s q) n", n=SLOT)[:, :, 27:30], 1.0)
            pool.drain().then_inc(S["k_cleared"], 1)
            ge.memset(ones[:, :], 1.0)
            ge.memset(zrow[:, :], 0.0)
            pool.wait_ge(S["x_loaded"], 2 * 16)
            ge.tensor_copy(homes[:, :], rowno).then_inc(S["zero_set"], 1)
            pool.wait_ge(S["loads_v"], 2 * 16)
            for t in range(TT):
                hi = btab[:, :, 8:16].rearrange("p (g r) c -> p g r c", g=NG)
                lo = btab[:, :, 0:8].rearrange("p (g r) c -> p g r c", g=NG)
                ge.tensor_tensor(bdf[:, :, :].rearrange("p (g t r) c -> p t g r c", g=NG, t=TT)[:, t], hi, lo,
                                 ALU.subtract)
                ge.tensor_copy(blo[:, :, :].rearrange("p (g t r) c -> p t g r c", g=NG, t=TT)[:, t], lo)
            pool.drain()
            with pool.Fori(0, B) as b:
                pool.wait_ge(S["tanh_ready"], b + 1)
                pool.sem_inc(S["seen"], 1)
                ge.tensor_scalar(sig, sig, 0.5, 0.5, ALU.mult, ALU.add)
                pool.drain()
                ge.tensor_tensor(lvl[:, :, :], bdf[:, :, :], sig[:, :, 3:4].to_broadcast([P, J, 8]), ALU.mult)
                pool.drain()
                ge.tensor_tensor(lvl[:, :, :], lvl[:, :, :], blo[:, :, :], ALU.add)
                for r, n in ((2, 4), (1, 2), (0, 1)):
                    pool.drain()
                    ge.tensor_tensor(dif[:, :, 0:n], lvl[:, :, n:2 * n], lvl[:, :, 0:n], ALU.subtract)
                    pool.drain()
                    ge.tensor_tensor(dif[:, :, 0:n], dif[:, :, 0:n], sig[:, :, r:r + 1].to_broadcast([P, J, n]),
                                     ALU.mult)
                    pool.drain()
                    dst = lvl[:, :, 0:n] if n > 1 else bon.rearrange("p (j c) -> p j c", c=1)
                    ge.tensor_tensor(dst, lvl[:, :, 0:n], dif[:, :, 0:n], ALU.add)
                pool.drain()
                pool.sem_inc(S["sig_used"], 1)
                pool.wait_ge(S["bonus_turned"], b + 1)
                pool.sem_inc(S["seen"], 1)
                ge.tensor_copy(bont[:, :].rearrange("p (t g r) -> p t g r", g=NG, t=TT),
                               bon.rearrange("p (g t r) -> p t g r", g=NG, t=TT)).then_inc(S["bonus_ready"], 1)
                split(ge, bon, bpart, bonres)
                for i in range(3):
                    place(ge, ks, b, (24 + i,), bpart[:, i, :], 1)
                pool.drain()

        def proj_dve(dve):
            ve.memset(qs.rearrange("p s n -> p (s n)"), 0.0)
            dve.wait_ge(S["x_loaded"], 2 * 16)
            ve.tensor_copy(identb[:, :], ident).then_inc(S["consts_ready"], 1)
            layernorm_stats(range(TT))
            dve.sem_inc(S["qk_used"], 1)
            dve.sem_inc(S["k_placed"], 1)
            dve.sem_inc(S["max_used"], 1)
            dve.sem_inc(S["bonus_turned"], 1)

            def scale(b):
                dve.wait_ge(S["xn_turned"], b + 1)
                dve.sem_inc(S["seen"], 1)
                normalise(b, lambda t: xn[:, t, :]).then_inc(S["xn_ready"], 1)

            def wide(v):
                return v.rearrange("p (j d) -> p j d", d=1).to_broadcast([P, J, DK])

            def by4(v):
                return v.rearrange("p (j d) -> p j d", d=DK)

            def main(b, first=False):
                dve.wait_ge(S["qk_out"], b + 2)
                ve.tensor_reduce(n2, sq.rearrange("p (j d) -> p j d", d=DK), AX.X, ALU.add)
                ve.drain()
                ve.tensor_scalar(nv[:, 0:2 * J], n2[:, 0:2 * J], NORM2, None, ALU.max)
                ve.tensor_scalar(nv[:, 2 * J:3 * J], n2[:, 2 * J:3 * J], TINY, None, ALU.max)
                ve.drain()
                rsqrt(nv[:, :], rqk, nt[:, :])
                rq, rk, ru = (rqk[:, i * J:(i + 1) * J] for i in range(3))
                if not first:
                    dve.wait_ge(S["tanh_ready"], b)
                ve.tensor_tensor(by4(dots), qk[:, 3], wide(rk), ALU.mult).then_inc(S["dots_ready"], 1)
                ve.tensor_tensor(by4(kv), qk[:, 1], wide(rk), ALU.mult)
                ve.scalar_tensor_tensor(fu, rq, 1e12, ru, ALU.mult, ALU.min)
                ve.drain()
                ve.scalar_tensor_tensor(by4(qv), qk[:, 2], 1.0 / np.sqrt(DK), wide(fu), ALU.mult, ALU.mult)\
                    .then_inc(S["qk_used"], 1)
                ve.drain()
                dve.wait_ge(S["k_placed"], b + 1)
                dve.sem_inc(S["seen"], 1)
                split(ve, kv, kpart, res)
                dve.sem_inc(S["k_parts"], 1)
                split(ve, qv, qpart, res)
                place(ve, qs, b, (0, 4, 8), qpart[:, 0, :], DK)
                place(ve, qs, b, (12, 16), qpart[:, 1, :], DK)
                place(ve, qs, b, (20,), qpart[:, 2, :], DK)
                ve.drain()

            def scan(b):
                dve.wait_ge(S["bonus_turned"], b + 2)
                dve.sem_inc(S["seen"], 1)
                ve.tensor_copy(bT[0:H, :], bank[5][0:H, :])
                ve.drain()
                ve.tensor_tensor_scan(mT[0:H, :], bT[0:H, :], bT[0:H, :], LOW, ALU.max, ALU.max)\
                    .then_inc(S["max_ready"], 1)
                ve.drain()

            def place_max(b):
                dve.wait_ge(S["max_turned"], b + 1)
                ve.tensor_scalar(mneg.rearrange("p (g t r) -> p t g r", g=NG, t=TT),
                                 bank[6][:, 0:J].rearrange("p (t g r) -> p t g r", t=TT, g=NG),
                                 -1.0, None, ALU.mult).then_inc(S["max_used"], 1)
                ve.drain()
                split(ve, mneg, mpart, res)
                for i in range(3):
                    place(ve, qs, b, (27 + i,), mpart[:, i, :], 1)
                ve.drain()

            scale(0)
            dve.wait_ge(S["x_rest"], (B - 1) * 16)
            ve.drain()
            layernorm_stats(range(TT, NT))
            scale(1)
            ve.memset(qs.rearrange("p s (q n) -> p (s q) n", n=SLOT)[:, :, 24:27], 1.0)
            ve.drain()
            main(0, first=True)
            scale(2)
            main(1)
            scan(0)
            with dve.Fori(2, B - 1) as b:
                scale(b + 1)
                main(b)
                place_max(b - 2)
                scan(b - 1)
            main(B - 1)
            place_max(B - 3)
            scan(B - 2)
            place_max(B - 2)
            scan(B - 1)
            place_max(B - 1)

        def turn(te, s, to, src):
            for t in range(TT):
                last = te.matmul(to[:, t * P:(t + 1) * P], src[:, s, t * P:(t + 1) * P], identb[:, :],
                                 start=True, stop=True)
            last.then_inc(S["turned"], 1)

        def scores(pe, te, s, g):
            row = slice(SLOT * g, SLOT * (g + 1))
            for c in range(3):
                pe.wait_ge(S["expd"], 12 * s + 3 * g + c + 1)
                for k, off in CHUNKS[c]:
                    last = te.matmul(SB[(3 * g + c) % 4][:, off:off + T - k * P], kt[row, k * P:(k + 1) * P],
                                     qt[row, k * P:T], start=True, stop=True)
                last.then_inc(S["scored"], 1)

        def average(pe, te, s, g, tiles=range(TT)):
            if 0 in tiles:
                pe.wait_ge(S["masked"], HG * s + g + 1)
                pe.wait_ge(S["normed"], HG * s + g + 1)
            for q in tiles:
                for k in range(q + 1):
                    at = BLK[k] + (q - k) * P
                    last = te.matmul(AVB[g % 2][:, q * VW:(q + 1) * VW], probs[:, g, at:at + P],
                                     Vs[:, s, k, g, :], start=(k == 0), stop=(k == q))
            if TT - 1 in tiles:
                last.then_inc(S["averaged"], 1)

        def turn_out(pe, te, s):
            pe.wait_ge(S["normed"], HG * s + HG + 2)
            for c in range(2):
                for t in range(TT):
                    last = te.transpose((QB, KB)[c][:, t * P:(t + 1) * P], o[:, t, c * P:(c + 1) * P], ident)
                last.then_inc(S["o_turned"], 1)

        def project(pe, te, s):
            pe.wait_ge(S["o_copied"], 2 * s + 2)
            for t in range(TT):
                for c in range(2):
                    last = te.matmul(KB[:, t * P:(t + 1) * P], ot[:, c, t * P:(t + 1) * P],
                                     wo[:, (s % NG) * 2 + c, :], start=(c == 0), stop=(c == 1))
            last.then_inc(S["outed"], 1)

        def attn_pe(pe):
            te = nc.tensor
            pe.wait_ge(S["loads_late"], 7 * 16)

            def step(s, first=False, final=False):
                scores(pe, te, s, 1)
                average(pe, te, s, 0)
                if not first:
                    turn_out(pe, te, s - 1)
                scores(pe, te, s, 2)
                average(pe, te, s, 1)
                if not first:
                    project(pe, te, s - 1)
                scores(pe, te, s, 3)
                if not final:
                    turn(te, s + 1, QB, qs)
                    average(pe, te, s, 2, (0, 1))
                    pe.wait_ge(S["added"], s + 1)
                    turn(te, s + 1, KB, ks)
                    average(pe, te, s, 2, (2, 3))
                    pe.wait_ge(S["operands"], 2 * s + 4)
                    scores(pe, te, s + 1, 0)
                else:
                    average(pe, te, s, 2)
                average(pe, te, s, 3)

            turn(te, 0, QB, qs)
            turn(te, 0, KB, ks)
            pe.wait_ge(S["operands"], 2)
            scores(pe, te, 0, 0)
            step(0, first=True)
            with pe.Fori(1, STEPS - 1) as s:
                step(s)
            step(STEPS - 1, final=True)
            turn_out(pe, te, STEPS - 1)
            project(pe, te, STEPS - 1)

        def attn_act(act):
            se = nc.scalar
            act.sem_inc(S["expd"], 4)

            def exps(s, g, reuse=True):
                if reuse:
                    act.wait_ge(S["averaged"], HG * s + g - PB + 1)
                for c in range(3):
                    act.wait_ge(S["scored"], 12 * s + 3 * g + c + 1)
                    se.activation(probs[:, g, 512 * c:512 * c + WIDTH[c]], SB[(3 * g + c) % 4][:, 0:WIDTH[c]],
                                  ACT.Exp).then_inc(S["expd"], 1)

            def step(s, first=False, final=False):
                exps(s, 1, not first)
                exps(s, 2, not first)
                exps(s, 3, not first)
                if not final:
                    exps(s + 1, 0)

            exps(0, 0, False)
            step(0, first=True)
            with act.Fori(1, STEPS - 1) as s:
                step(s)
            step(STEPS - 1, final=True)

        def attn_pool(pool):
            ge = nc.gpsimd

            def mask(s, g):
                for c, at, n in ((0, BLK[0], 1), (1, BLK[1], 2), (2, BLK[2], 1)):
                    pool.wait_ge(S["expd"], 12 * s + 3 * g + c + 5)
                    pool.sem_inc(S["seen"], 1)
                    blk = probs[:, g, at:at + P] if n == 1 else \
                        bass.AP(probs[:, g, at:at + P].tensor, probs[:, g, at:at + P].offset,
                                [probs[:, g, at:at + P].ap[0], [BLK[3] - BLK[1], 2], [1, P]])
                    last = ge.affine_select(out=blk, in_=blk, compare_op=ALU.is_ge, fill=0.0, base=0,
                                            pattern=[[0, n], [1, P]] if n > 1 else [[1, P]],
                                            channel_multiplier=-1)
                last.then_inc(S["masked"], 1)

            with pool.Fori(0, STEPS) as s:
                for g in range(HG):
                    mask(s, g)

        def attn_dve(dve):
            dve.sem_inc(S["normed"], 2)
            dve.sem_inc(S["added"], 1)

            def norm(s, g, first=False):
                dve.wait_ge(S["averaged"], HG * s + g + 1)
                sums = AVB[g % 2][:, 0:TT * VW].rearrange("p (t w) -> p t w", w=VW)
                ve.reciprocal(rec[:, :], sums[:, :, DV])
                ve.drain()
                if g == 0 and not first:
                    dve.wait_ge(S["o_turned"], 2 * s)
                ve.tensor_tensor(o[:, :, g * DV:(g + 1) * DV], sums[:, :, 0:DV],
                                 rec[:, :].rearrange("p (t w) -> p t w", w=1).to_broadcast([P, TT, DV]),
                                 ALU.mult).then_inc(S["normed"], 1)
                ve.drain()

            def add(s):
                dve.wait_ge(S["outed"], s + 1)
                xs_ = x[:, bass.ds((s // NG) * TT, TT), :]
                ve.tensor_tensor(xs_, xs_, KB[:, :].rearrange("p (t d) -> p t d", t=TT), ALU.add)\
                    .then_inc(S["added"], 1)
                ve.drain()

            def operands(s, c):
                dve.wait_ge(S["turned"], 2 * s + c + 1)
                ve.tensor_copy((qt, kt)[c][:, :], (QB, KB)[c][:, :]).then_inc(S["operands"], 1)

            def outputs(s):
                for c in range(2):
                    dve.wait_ge(S["o_turned"], 2 * s + c + 1)
                    ve.tensor_copy(ot[:, c, :], (QB, KB)[c][:, :]).then_inc(S["o_copied"], 1)

            def step(s, first=False, final=False, before=None, part=None):
                norm(s, 0, first)
                if not first:
                    outputs(s - 1)
                norm(s, 1)
                if not first:
                    add(s - 1)
                if not final:
                    operands(s + 1, 0)
                    operands(s + 1, 1)
                norm(s, 2)
                if before is not None:
                    normalise_early(before, part, rows_of[0])
                norm(s, 3)

            operands(0, 0)
            operands(0, 1)
            step(0, first=True)
            with dve.Fori(1, NG) as s:
                step(s)
            with dve.Fori(1, B - 1) as b:
                for g in range(NG):
                    step(b * NG + g, before=b - 1, part=g)
            for g in range(NG):
                step((B - 1) * NG + g, final=(g == NG - 1), before=B - 2, part=g)
            outputs(STEPS - 1)
            add(STEPS - 1)

        late = [0]

        def room2(n):
            late[0] += n
            assert late[0] <= STEPS * TT * HG * VW
            return big[:, late[0] - n:late[0]]

        back = late_room[:, 0:NT * 2 * D].rearrange("p (t k d) -> p t k d", t=NT, k=2)
        room2(2 * NT * RW)
        sc = room2(NT * E).rearrange("p (t e) -> p t e", t=NT)
        past = room2(NS * (E - 1)).rearrange("p (s e) -> p s e", s=NS)
        best = room2(NT)
        pick = [room2(NT * E).rearrange("p (t e) -> p t e", t=NT) for _ in range(3)]
        tmpe = room2(NT * E).rearrange("p (t e) -> p t e", t=NT)
        tots = room2(NT * E)
        cums = room2(NT * E)
        prev = room2(E)
        ntile = room2(E)
        tend = room2(E)
        tbase = room2(E)
        top = room2(2 * NT).rearrange("p (k t) -> p k t", k=2)
        gts = room2(2 * NT).rearrange("p (k t) -> p k t", k=2)
        slotf = room2(2 * NT)
        exf = room2(NS)
        xs = room2(NB * RW).rearrange("p (n w) -> p n w", n=NB)
        gate = room2(NB * 3).rearrange("p (n w) -> p n w", n=NB)
        xT = room2(NB * P).rearrange("p (n c) -> p n c", n=NB)
        tan = room2(NB * FF).rearrange("p (n c) -> p n c", n=NB)
        hid = room2(NB * FF).rearrange("p (n c) -> p n c", n=NB)
        hT = room2(NB * FF).rearrange("p (n c) -> p n c", n=NB)
        ys = room2(NB * D).rearrange("p (n c) -> p n c", n=NB)
        xT2 = (xnT[:, :], xn[:, :, :].rearrange("p t d -> p (t d)"))
        MID, XTB, HTB, OUTB = bank[0:4], (bank[4], bank[7]), bank[5], bank[6]

        def route_dve(dve, f):
            rows = rows_of[f]
            layernorm_stats(range(NT - TT, NT))
            ve.drain()
            normalise(B - 1, lambda t: rows[:, 0, NT - TT + t, 0:D]).then_inc(S["x_static"], 1)
            dve.wait_ge(S["f_scored"], (f + 1) * B)
            ve.tensor_copy(sc[:, :, :], bank[2][:, 0:NT * E].rearrange("p (t e) -> p t e", t=NT))
            ve.drain()

            def each(v):
                return v.rearrange("p (t e) -> p t e", e=1).to_broadcast([P, NT, E])

            for k in range(2):
                ve.tensor_reduce(top[:, k, :], sc[:, :, :], AX.X, ALU.max)
                ve.drain()
                ve.tensor_tensor(tmpe[:, :, :], sc[:, :, :], each(top[:, k, :]), ALU.is_equal)
                ve.drain()
                ve.tensor_tensor(tmpe[:, :, :], tmpe[:, :, :],
                                 order.rearrange("p (t e) -> p t e", t=1).to_broadcast([P, NT, E]), ALU.mult)
                ve.drain()
                ve.tensor_reduce(best, tmpe[:, :, :], AX.X, ALU.max)
                ve.drain()
                ve.tensor_tensor(pick[k][:, :, :], tmpe[:, :, :], each(best), ALU.is_equal)
                ve.drain()
                if k == 0:
                    ve.scalar_tensor_tensor(sc[:, :, :], pick[0][:, :, :], LOW, sc[:, :, :], ALU.mult, ALU.add)
                    ve.drain()
            ve.tensor_tensor(pick[2][:, :, :], pick[0][:, :, :], pick[1][:, :, :], ALU.add).then_inc(S["picked"], 1)
            ve.tensor_copy(rows[:, :, :, D + 2].bitcast(I32),
                           homes[:, 0:2 * NT].rearrange("p (k t) -> p k t", k=2))
            dve.wait_ge(S["gated"], f + 1)
            ve.tensor_scalar(gts[:, :, :], gts[:, :, :], 0.25, 0.25, ALU.mult, ALU.add)
            ve.drain()
            dve.wait_ge(S["x_kept"], (f + 1) * B)
            ve.tensor_copy(rows[:, :, :, D], gts[:, :, :])
            ve.scalar_tensor_tensor(rows[:, :, :, D + 1], gts[:, :, :], 2.0, gts[:, :, :], ALU.mult, ALU.mult)
            ve.drain()
            dve.wait_ge(S["counted"], f + 1)
            ve.tensor_copy(tots.rearrange("p (e t) -> p e t", e=E),
                           bank[3][:, 0:NT * E].rearrange("p (t e) -> p e t", t=NT))
            ve.drain()
            ve.tensor_tensor_scan(cums, tots, tots, 0.0, ALU.add, ALU.bypass)
            ve.drain()
            ends = cums.rearrange("p (e t) -> p e t", e=E)[:, :, NT - 1]
            ve.memset(prev[:, 0:1], 0.0)
            ve.tensor_copy(prev[:, 1:E], ends[:, 0:E - 1])
            ve.drain()
            ve.tensor_tensor(ntile, ends, prev, ALU.subtract)
            ve.drain()
            ve.tensor_tensor(cums, cums, tots, ALU.subtract)
            ve.tensor_scalar(ints[:, 0:E], ntile, float(P - 1), None, ALU.add)
            ve.drain()
            ve.tensor_scalar(ints[:, 0:E], ints[:, 0:E], 7, None, ALU.arith_shift_right)
            ve.drain()
            ve.tensor_copy(ntile, ints[:, 0:E])
            ve.drain()
            ve.tensor_tensor_scan(tend, ntile, ntile, 0.0, ALU.add, ALU.bypass)
            ve.drain()
            ve.tensor_tensor(tbase, tend, ntile, ALU.subtract)
            ve.drain()
            ve.scalar_tensor_tensor(tbase, tbase, float(P), prev, ALU.mult, ALU.subtract)
            ve.drain()
            cumv = cums.rearrange("p (e t) -> p e t", e=E)
            ve.tensor_tensor(cumv, cumv, tbase.rearrange("p (e t) -> p e t", t=1).to_broadcast([P, E, NT]), ALU.add)
            ve.drain()
            ve.scalar_tensor_tensor(tmpe[:, :, :], bank[4][:, 0:NT * E].rearrange("p (t e) -> p t e", t=NT), -1.0,
                                    cums.rearrange("p (e t) -> p t e", e=E), ALU.add, ALU.add)
            ve.drain()
            for k in range(2):
                ve.tensor_tensor(pick[k][:, :, :], pick[k][:, :, :], tmpe[:, :, :], ALU.mult)
            ve.drain()
            for k in range(2):
                ve.tensor_reduce(slotf[:, k * NT:(k + 1) * NT], pick[k][:, :, :], AX.X, ALU.add)
            ve.drain()
            ve.tensor_copy(slots[:, :], slotf).then_inc(S["routed"], 1)
            ve.tensor_tensor(past[:, :, :], tileno.rearrange("p (s e) -> p s e", e=1).to_broadcast([P, NS, E - 1]),
                             tend[:, 0:E - 1].rearrange("p (s e) -> p s e", s=1).to_broadcast([P, NS, E - 1]),
                             ALU.is_ge)
            ve.drain()
            ve.tensor_reduce(exf, past[:, :, :], AX.X, ALU.add)
            ve.drain()
            ve.tensor_copy(expert[:, :], exf).then_inc(S["mapped"], 1)

        def route_pe(pe, f):
            te = nc.tensor
            rows = rows_of[f]

            def score(b):
                pe.wait_ge(S["x_copied"], f * B + b + 1)
                for t in range(TT):
                    last = te.matmul(bank[2][:, (b * TT + t) * E:(b * TT + t + 1) * E],
                                     xT2[b % 2][:, t * P:(t + 1) * P], wr[:, :], start=True, stop=True)
                last.then_inc(S["f_scored"], 1)

            for b in range(B):
                pe.wait_ge(S["x_static"], f * B + b + 1)
                for t in range(TT):
                    last = te.transpose(bank[b % 2][:, t * P:(t + 1) * P], rows[:, 0, b * TT + t, 0:D], ident)
                last.then_inc(S["x_turned"], 1)
                if b > 0:
                    score(b - 1)
            score(B - 1)
            pe.wait_ge(S["picked"], f + 1)
            either = pick[2][:, :, :].rearrange("p t e -> p (t e)")
            te.matmul(bank[3][:, 0:NT * E], ones[:, :], either, start=True, stop=True)
            te.matmul(bank[4][:, 0:NT * E], causal, either, start=True, stop=True).then_inc(S["counted"], 1)

        def route_act(act, f):
            se = nc.scalar
            rows = rows_of[f]
            for b in range(B):
                act.wait_ge(S["x_turned"], f * B + b + 1)
                if b >= 2:
                    act.wait_ge(S["f_scored"], f * B + b - 1)
                se.activation(xT2[b % 2], bank[b % 2][:, :], ACT.Copy).then_inc(S["x_copied"], 1)
                se.activation(rows[:, 1, b * TT:(b + 1) * TT, 0:D], rows[:, 0, b * TT:(b + 1) * TT, 0:D], ACT.Copy)\
                    .then_inc(S["x_kept"], 1)
            act.wait_ge(S["picked"], f + 1)
            se.activation(gts[:, :, :], top[:, :, :], ACT.Tanh, scale=0.5).then_inc(S["gated"], 1)

        def scatter_pool(pool, f):
            pool.wait_ge(S["routed"], f + 1)
            pool.wait_ge(S["zeroed"], 4 * 16)
            for t in range(NT):
                for k in range(2):
                    c = k * NT + t
                    nc.gpsimd.indirect_dma_start(xg[f][:, :], bass.IndirectOffsetOnAxis(slots[:, c:c + 1], 0),
                                                 rows_of[f][:, k, t, :], None).then_inc(S["scattered"], 16)

        def results_pool(pool, f):
            base = f * (NT + NS) + NT
            with pool.Fori(0, NS // NB) as i:
                for k in range(NB):
                    pool.wait_ge(S["y_copied"], base + i * NB + k + 2)
                    pool.wait_ge(S["homed"], f * NS + i * NB + k + 1)
                    pool.sem_inc(S["seen"], 1)
                    nc.gpsimd.indirect_dma_start(yg[f][:, :], bass.IndirectOffsetOnAxis(home[:, k:k + 1], 0),
                                                 ys[:, k, :], None).then_inc(stored_y[k], 16)

        def fetch_dve(dve, f, b):
            dve.wait_ge(fetched[b], 16 * 2 * (f + 1))
            for k in range(2):
                last = ve.tensor_tensor(x[:, b * TT:(b + 1) * TT, :], x[:, b * TT:(b + 1) * TT, :],
                                        back[:, b * TT:(b + 1) * TT, k, :], ALU.add)
                if k == 0:
                    ve.drain()
            return last

        def units_of(f):
            at = f * (NT + NS)
            return ((at, NT // NB, True), (at + NT, NS // NB, False))

        def unit_loop(eng, turns, slot):
            for k in range(NB):
                slot(0, k, True, False)
            with eng.Fori(1, turns - 1) as i:
                for k in range(NB):
                    slot(i, k, False, False)
            for k in range(NB):
                slot(turns - 1, k, False, True)

        def ago(i, k, d):
            return (i, k - d) if k >= d else (i - 1, k - d + NB)

        def units_sp(sp, f):
            for base, turns, shared in units_of(f):
                if shared:
                    sp.wait_ge(S["routed"], f + 1)
                else:
                    sp.wait_ge(S["scattered"], 16 * 2 * NT * (f + 1))
                with sp.Fori(0, turns) as i:
                    for k in range(NB):
                        j = i * NB + k
                        sp.wait_ge(S["u_copied"], base + j + 1)
                        src = rows_of[f][:, 0, j, :] if shared else xg[f][bass.ds(j * P, P), :]
                        sp.dma_start(xs[:, k, :], src).then_inc(loaded[k], 16)
            for k in range(NB):
                sp.wait_ge(stored_y[k], 16 * ((f + 1) * NS // NB))
            for b in range(B):
                for k in range(2):
                    at = (k * NT + b * TT) * P
                    sp.dma_start(back[:, b * TT:(b + 1) * TT, k, :],
                                 yg[f][at:at + TT * P, :].rearrange("(t p) d -> p t d", p=P))\
                        .then_inc(fetched[b], 16)

        def units_pe(pe, f):
            te = nc.tensor
            held = [pe.alloc_register(f"expert{f}{k}") for k in range(NB)]
            nc.disable_value_cache = True
            for base, turns, shared in units_of(f):
                if not shared:
                    pe.wait_ge(S["mapped"], f + 1)

                whose = [U - 1] * NB if shared else \
                    [bass.RuntimeValue.of_register_unchecked(h, min_val=0, max_val=E - 1) for h in held]

                def load_expert(i, k):
                    if not shared:
                        pe.load(held[k], expert[0:1, bass.ds(i * NB + k, 1)])

                def turn_x(i, k):
                    pe.wait_ge(loaded[k], 16 * (base // NB + i + 1))
                    pe.wait_ge(S["u_copied"], base + i * NB + k + NB - 1)
                    te.transpose(XTB[k % 2][:, 0:P], xs[:, k, 0:D], ident).then_inc(S["u_turned"], 1)

                def mid(i, k, w):
                    pe.wait_ge(S["u_copied"], base + i * NB + k + 1 + NB)
                    pe.wait_ge(S["hidden"], base + i * NB + k + 1)
                    te.matmul(MID[k][:, :], xT[:, k, :], wff[:, w, :], start=True, stop=True)\
                        .then_inc(S["mids"], 1)

                def turn_h(i, k):
                    pe.wait_ge(S["hidden"], base + i * NB + k + 1 + NB)
                    pe.wait_ge(S["h_copied"], base + i * NB + k + 1)
                    for c in range(2):
                        last = te.transpose(HTB[:, c * P:(c + 1) * P], hid[:, k, c * P:(c + 1) * P], ident)
                    last.then_inc(S["h_turned"], 1)

                def down(i, k, w):
                    pe.wait_ge(S["h_copied"], base + i * NB + k + 2)
                    pe.wait_ge(S["y_copied"], base + i * NB + k + 1)
                    for c in range(2):
                        last = te.matmul(OUTB[:, 0:D], hT[:, k, c * P:(c + 1) * P], wfo[:, w, c, :],
                                         start=(c == 0), stop=(c == 1))
                    last.then_inc(S["downs"], 1)

                def slot(i, k, first, final):
                    if k < NB - 1:
                        turn_x(i, k + 1)
                    elif not final:
                        turn_x(i + 1, 0)
                    mid(i, k, whose[k])
                    if not first or k >= 2:
                        turn_h(*ago(i, k, 2))
                    if not first or k >= 3:
                        down(*ago(i, k, 3), whose[(k + 1) % NB])
                    if k < NB - 1:
                        load_expert(i, k + 1)
                    elif not final:
                        load_expert(i + 1, 0)

                load_expert(0, 0)
                turn_x(0, 0)
                unit_loop(pe, turns, slot)
                turn_h(turns - 1, NB - 2)
                down(turns - 1, NB - 3, whose[NB - 3])
                turn_h(turns - 1, NB - 1)
                down(turns - 1, NB - 2, whose[NB - 2])
                down(turns - 1, NB - 1, whose[NB - 1])
            nc.disable_value_cache = False

        def units_act(act, f):
            se = nc.scalar
            if f == 0:
                act.sem_inc(S["h_copied"], 1)
            for base, turns, shared in units_of(f):
                def copy_h(i, k):
                    act.wait_ge(S["h_turned"], base + i * NB + k + 1)
                    se.activation(hT[:, k, :], HTB[:, 0:FF], ACT.Copy).then_inc(S["h_copied"], 1)

                def slot(i, k, first, final):
                    act.wait_ge(S["mids"], base + i * NB + k + 1)
                    se.activation(tan[:, k, :], MID[k][:, 0:FF], ACT.Tanh, scale=0.5 if shared else gate[:, k, 0:1])\
                        .then_inc(S["tanhs"], 1)
                    if not first or k >= 2:
                        copy_h(*ago(i, k, 2))
                    if not shared and (not first or k >= 3):
                        result(*ago(i, k, 3))

                def result(i, k):
                    if not (f == 0 and isinstance(i, int) and i == 0):
                        act.wait_ge(stored_y[k], 16 * (f * NS // NB + i))
                    act.wait_ge(S["downs"], base + i * NB + k + 1)
                    se.activation(ys[:, k, :], OUTB[:, 0:D], ACT.Copy).then_inc(S["y_copied"], 1)

                unit_loop(act, turns, slot)
                copy_h(turns - 1, NB - 2)
                if not shared:
                    result(turns - 1, NB - 3)
                copy_h(turns - 1, NB - 1)
                if not shared:
                    result(turns - 1, NB - 2)
                    result(turns - 1, NB - 1)

        def units_dve(dve, f):
            if f == 0:
                dve.sem_inc(S["hidden"], NB)
                dve.sem_inc(S["y_copied"], 1)
                dve.sem_inc(S["u_copied"], NB)
            for base, turns, shared in units_of(f):
                def copy_x(i, k):
                    dve.wait_ge(S["u_turned"], base + i * NB + k + 1)
                    ve.tensor_copy(gate[:, k, 0:2], xs[:, k, D:D + 2])
                    if not shared:
                        ve.tensor_copy(gate[:, k, 2:3].bitcast(I32), xs[:, k, D + 2:RW].bitcast(I32))
                    ve.tensor_copy(xT[:, k, :], XTB[k % 2][:, 0:P]).then_inc(S["u_copied"], 1)

                def hide(i, k):
                    dve.wait_ge(S["tanhs"], base + i * NB + k + 1)
                    ve.scalar_tensor_tensor(tan[:, k, :], tan[:, k, :], 1.0, MID[k][:, 0:FF], ALU.add, ALU.mult)
                    ve.drain()
                    ve.scalar_tensor_tensor(hid[:, k, :], tan[:, k, :], 0.5 if shared else gate[:, k, 1:2],
                                            MID[k][:, FF:2 * FF], ALU.mult, ALU.mult).then_inc(S["hidden"], 1)

                def result(i, k):
                    dve.wait_ge(S["downs"], base + i * NB + k + 1)
                    xj = x[:, i * NB + k, :]
                    ve.tensor_tensor(xj, xj, OUTB[:, 0:D], ALU.add).then_inc(S["y_copied"], 1)

                def keep_home(i, k):
                    if not (f == 0 and isinstance(i, int) and i == 0):
                        dve.wait_ge(stored_y[k], 16 * (f * NS // NB + i))
                    ve.tensor_copy(home[:, k:k + 1], gate[:, k, 2:3].bitcast(I32)).then_inc(S["homed"], 1)

                def slot(i, k, first, final):
                    if k < NB - 1:
                        copy_x(i, k + 1)
                    elif not final:
                        copy_x(i + 1, 0)
                    if not shared and (not first or k >= 2):
                        keep_home(*ago(i, k, 2))
                    if not first or k >= 1:
                        hide(*ago(i, k, 1))
                    if shared and (not first or k >= 3):
                        result(*ago(i, k, 3))

                copy_x(0, 0)
                unit_loop(dve, turns, slot)
                hide(turns - 1, NB - 1)
                if not shared:
                    keep_home(turns - 1, NB - 2)
                    keep_home(turns - 1, NB - 1)
                for k in range(NB - 3, NB):
                    if shared:
                        result(turns - 1, k)

        late[0] = 0
        RS = 2
        qk_d = room2(RS * TT * 2 * D).rearrange("p (n t c) -> p n t c", n=RS, t=TT)
        qT = room2(RS * T).rearrange("p (n c) -> p n c", n=RS)
        qR = room2(RS * 4 * T).rearrange("p (n t r c) -> p n t r c", n=RS, t=TT, r=4)
        kT = room2(RS * 4 * T).rearrange("p (n m c) -> p n m c", n=RS, m=4)
        sT = room2(2 * H * P).rearrange("p (n m r q) -> p n m r q", n=2, m=4, r=4)
        state = room2(D)
        stmp = room2(D)
        vm = room[:, 0:RS * TT * 4 * D].rearrange("p (n t m c) -> p n t m c", n=RS, t=TT, m=4)
        y = room[:, RS * TT * 4 * D:RS * TT * 4 * D + T]
        zT = room[:, RS * TT * 4 * D + T:RS * TT * 4 * D + 2 * T]
        st = sb("st", [P, 16])
        SCB, YB, STB, QKB, VB = (bank[1], bank[2]), (bank[0], bank[7]), bank[5], (bank[4], bank[6]), bank[3]

        def newton(e, v, y_, t):
            e.tensor_scalar(y_.bitcast(I32), y_.bitcast(I32), -1.0, float(0x5f3759df), ALU.mult, ALU.add)
            e.drain()
            for _ in range(3):
                e.tensor_tensor(t, y_, y_, ALU.mult)
                e.drain()
                e.tensor_tensor(t, t, v, ALU.mult)
                e.drain()
                e.tensor_scalar(t, t, -0.5, 1.5, ALU.mult, ALU.add)
                e.drain()
                e.tensor_tensor(y_, t, y_, ALU.mult)
                e.drain()

        mu, avar, dev, msq, aa, bb = (st[:, i:i + 1] for i in range(2, 8))

        def r_scale_dve(dve, b):
            normalise(b, lambda t: xn[:, t, :]).then_inc(S["r_xn"], 1)

        def r_decay_dve(dve, b, n, c):
            dve.wait_ge(S["r_qk"], 2 * b + c + 1)
            ve.tensor_tensor(qk_d[:, n, 2 * c:2 * c + 2, :],
                             QKB[c][:, :].rearrange("p (t c) -> p t c", t=2),
                             qkdecay.rearrange("p (t c) -> p t c", t=1).to_broadcast([P, 2, 2 * D]),
                             ALU.mult).then_inc(S["r_decayed"], 1)

        def r_mask_dve(dve, b, t, m):
            dve.wait_ge(S["r_scored"], (b * TT + t) * 4 + m + 1)
            ve.tensor_tensor(sT[:, t % 2, m, :, :],
                             SCB[m % 2][:, :].rearrange("p (h q) -> p h q", h=4),
                             causal.rearrange("p (h q) -> p h q", h=1).to_broadcast([P, 4, P]),
                             ALU.mult).then_inc(S["r_masked"], 1)

        def r_state_dve(dve, b, t):
            dve.wait_ge(S["r_kv"], b * (TT - 1) + t + 1)
            if t == 0:
                ve.tensor_tensor(state, STB[:, 0:D], statemask, ALU.mult).then_inc(S["r_state"], 1)
            else:
                ve.tensor_tensor(stmp, STB[:, 0:D], statemask, ALU.mult)
                ve.drain()
                ve.scalar_tensor_tensor(state, state, decay128, stmp, ALU.mult, ALU.add)\
                    .then_inc(S["r_state"], 1)
            ve.drain()

        def r_norm_dve(dve, b, n, part):
            if part == 0:
                dve.wait_ge(S["r_ycopied"], b + 1)
                ve.bn_stats(st6[:, NT, :], y)
                ve.drain()
                ve.bn_aggr(st[:, 8:10], st6[:, NT, :]).then_inc(S["r_stats"], 1)
                ve.drain()
            elif part == 1:
                dve.wait_ge(S["r_avg"], 2 * b + 1)
                ve.tensor_copy(st[:, 2:4], YB[n][:, 0:2])
                ve.drain()
                ve.tensor_tensor(dev, st[:, 8:9], mu, ALU.subtract)
                ve.drain()
                ve.tensor_tensor(dev, dev, dev, ALU.mult).then_inc(S["r_stats"], 1)
                ve.drain()
            elif part == 2:
                dve.wait_ge(S["r_avg"], 2 * b + 2)
                ve.tensor_copy(msq, YB[n][:, 2:3])
                ve.drain()
                ve.scalar_tensor_tensor(nv[:, TT:TT + 1], msq, EPS, avar, ALU.add, ALU.add)
                ve.drain()
                ve.tensor_scalar(ny[:, TT:TT + 1].bitcast(I32), nv[:, TT:TT + 1].bitcast(I32), 1, None,
                                 ALU.logical_shift_right).then_inc(S["r_var"], 1)
                ve.drain()
            else:
                dve.wait_ge(S["r_affine"], b + 1)
                ve.tensor_scalar(zT, y, aa, bb, ALU.mult, ALU.add).then_inc(S["r_z"], 1)

        def r_add_dve(dve, b, n):
            dve.wait_ge(S["r_out"], b + 1)
            xb = x[:, bass.ds(b * TT, TT), :]
            ve.tensor_tensor(xb, xb, YB[n][:, :].rearrange("p (t d) -> p t d", t=TT), ALU.add)\
                .then_inc(S["r_added"], 1)

        assert B == 4

        def retain_loop(eng, batch):
            batch(0, 0, True, False)
            with eng.Fori(0, (B - 2) // RS) as i:
                for n in (1, 0):
                    batch(i * RS + 2 - n, n, False, False)
            batch(B - 1, 1, False, True)

        def retain_dve(dve):
            dve.sem_inc(S["r_masked"], 2)

            def batch(b, n, first, final):
                o_ = 1 - n
                for t in range(TT):
                    for r in range(4):
                        if t < TT - 1:
                            r_mask_dve(dve, b, t + 1, r)
                        elif not final:
                            r_mask_dve(dve, b + 1, 0, r)
                        if r == 0 and t > 0:
                            r_state_dve(dve, b, t - 1)
                        if not final:
                            if (t, r) == (0, 0):
                                r_scale_dve(dve, b + 1)
                            if (t, r) in ((1, 1), (1, 3)):
                                r_decay_dve(dve, b + 1, o_, r // 2)
                        if not first:
                            if (t, r) in ((0, 1), (1, 0), (2, 0), (3, 0)):
                                r_norm_dve(dve, b - 1, o_, t)
                            if (t, r) == (3, 2):
                                r_add_dve(dve, b - 1, o_)
                        if n == 0 and not first or final:
                            if (t, r) in ((0, 3), (1, 2), (2, 2)):
                                normalise_early(b - 2, t, rows_of[1])
                ve.drain()

            fetch_dve(dve, 0, 0)
            ve.drain()
            layernorm_stats(range(TT))
            ve.drain()
            r_scale_dve(dve, 0)
            for b in range(1, B):
                fetch_dve(dve, 0, b)
            for c in range(2):
                r_decay_dve(dve, 0, 0, c)
            ve.drain()
            layernorm_stats(range(TT, NT))
            ve.drain()
            for r in range(4):
                r_mask_dve(dve, 0, 0, r)
            retain_loop(dve, batch)
            for part_ in range(4):
                r_norm_dve(dve, B - 1, (B - 1) % RS, part_)
                if part_ != 1:
                    normalise_early(B - 2, (0, None, 1, 2)[part_], rows_of[1])
            r_add_dve(dve, B - 1, (B - 1) % RS)
            ve.drain()

        def retain_pool(pool):
            ge = nc.gpsimd

            def affine(b):
                pool.wait_ge(S["r_var"], b + 1)
                pool.sem_inc(S["seen"], 1)
                newton(ge, nv[:, TT:TT + 1], ny[:, TT:TT + 1], nt[:, TT:TT + 1])
                ge.tensor_tensor(aa, ny[:, TT:TT + 1], gnw[:, 0:1], ALU.mult)
                pool.drain()
                ge.tensor_tensor(bb, mu, aa, ALU.mult)
                pool.drain()
                ge.tensor_tensor(bb, gnw[:, 1:2], bb, ALU.subtract).then_inc(S["r_affine"], 1)
                pool.drain()

            ge.memset(room[:, 0:RS * TT * 4 * D], 0.0).then_inc(S["r_zeroed"], 1)
            with pool.Fori(0, B) as b:
                affine(b)

        def r_turn_pe(pe, te, b):
            pe.wait_ge(S["r_xn"], b + 1)
            for t in range(TT):
                last = te.transpose(VB[:, t * P:(t + 1) * P], xn[:, t, :], ident)
            last.then_inc(S["r_turned"], 1)

        def r_project_pe(pe, te, b, c):
            if c == 0:
                pe.wait_ge(S["r_xT"], b + 1)
                pe.wait_ge(S["r_opq"], b + 1)
            for t in (2 * c, 2 * c + 1):
                last = te.matmul(QKB[c][:, (t % 2) * 2 * D:(t % 2 + 1) * 2 * D], xnT[:, t * P:(t + 1) * P],
                                 rqkv[:, 0:2 * D], start=True, stop=True)
            last.then_inc(S["r_qk"], 1)
            if c == 1:
                for t in range(TT):
                    last = te.matmul(VB[:, t * P:(t + 1) * P], xnT[:, t * P:(t + 1) * P], rqkv[:, 2 * D:3 * D],
                                     start=True, stop=True)
                last.then_inc(S["r_v"], 1)

        def r_operands_pe(pe, te, b, n):
            pe.wait_ge(S["r_decayed"], 2 * b + 2)
            for c in range(2):
                for t in range(TT):
                    last = te.transpose(QKB[c][:, t * P:(t + 1) * P], qk_d[:, n, t, c * D:(c + 1) * D], ident)
                last.then_inc(S["r_opT"], 1)

        def r_score_pe(pe, te, b, n, t, m):
            pe.wait_ge(S["r_masked"], (b * TT + t) * 4 + m + 1)
            te.matmul(SCB[m % 2][:, :], kT[:, n, m, t * P:(t + 1) * P],
                      qR[:, n, t, :, :].rearrange("p r c -> p (r c)"), start=True, stop=True)\
                .then_inc(S["r_scored"], 1)

        def r_average_pe(pe, te, b, n, t, r):
            tok = slice(t * P, (t + 1) * P)
            if r == 0:
                pe.wait_ge(S["r_masked"], (b * TT + t) * 4 + 4 + 2)
                pe.sem_inc(S["seen"], 1)
            for m in range(4):
                last = te.matmul(YB[n][32 * r:32 * r + 32, tok], vm[:, n, t, m, 32 * r:32 * r + 32],
                                 sT[:, t % 2, m, r, :], start=(m == 0), stop=(m == 3 and t == 0))
            if t > 0 and r == 3:
                pe.wait_ge(S["r_state"], b * (TT - 1) + t)
                last = te.matmul(YB[n][:, tok], state, qT[:, n, tok], start=False, stop=True)
            if t == TT - 1 and r == 3:
                last.then_inc(S["r_summed"], 1)

        def r_state_pe(pe, te, b, n, t):
            for m in range(4):
                last = te.matmul(STB[:, 0:D], qk_d[:, n, t, D:2 * D], vm[:, n, t, m, :],
                                 start=(m == 0), stop=(m == 3))
            last.then_inc(S["r_kv"], 1)

        def r_stat_pe(pe, te, b, n, part_):
            pe.wait_ge(S["r_stats"], 2 * b + part_ + 1)
            src, at = ((st[:, 8:10], slice(0, 2)), (st[:, 4:5], slice(2, 3)))[part_]
            te.matmul(YB[n][:, at], groupavg, src, start=True, stop=True).then_inc(S["r_avg"], 1)

        def r_out_pe(pe, te, b, n):
            pe.wait_ge(S["r_z"], b + 1)
            for t in range(TT):
                last = te.matmul(YB[n][:, t * P:(t + 1) * P], zT[:, t * P:(t + 1) * P], rwo[:, :],
                                 start=True, stop=True)
            last.then_inc(S["r_out"], 1)

        def retain_pe(pe):
            te = nc.tensor

            def batch(b, n, first, final):
                o_ = 1 - n
                if not first:
                    pe.wait_ge(S["r_added"], b)
                for t in range(TT):
                    for r in range(4):
                        if t < TT - 1:
                            r_score_pe(pe, te, b, n, t + 1, r)
                        elif not final:
                            pe.wait_ge(S["r_op"], 4 * (b + 1) + r + 1)
                            r_score_pe(pe, te, b + 1, o_, 0, r)
                        if (t, r) == (0, 0):
                            pe.wait_ge(S["r_vspread"], b + 1)
                        r_average_pe(pe, te, b, n, t, r)
                        if r == 3 and t < TT - 1:
                            r_state_pe(pe, te, b, n, t)
                        if not final:
                            if (t, r) == (0, 2):
                                r_turn_pe(pe, te, b + 1)
                            if (t, r) in ((1, 0), (1, 2)):
                                r_project_pe(pe, te, b + 1, r // 2)
                            if (t, r) == (2, 0):
                                r_operands_pe(pe, te, b + 1, o_)
                        if not first:
                            if (t, r) in ((0, 3), (1, 3)):
                                r_stat_pe(pe, te, b - 1, o_, t)
                            if (t, r) == (3, 1):
                                r_out_pe(pe, te, b - 1, o_)

            r_turn_pe(pe, te, 0)
            for c in range(2):
                r_project_pe(pe, te, 0, c)
            r_operands_pe(pe, te, 0, 0)
            for r in range(4):
                pe.wait_ge(S["r_op"], r + 1)
                r_score_pe(pe, te, 0, 0, 0, r)
            retain_loop(pe, batch)
            for part_ in range(2):
                r_stat_pe(pe, te, B - 1, (B - 1) % RS, part_)
            r_out_pe(pe, te, B - 1, (B - 1) % RS)

        def retain_act(act):
            se = nc.scalar
            act.sem_inc(S["r_opq"], 1)
            act.sem_inc(S["r_added"], 1)
            act.wait_ge(S["r_zeroed"], 1)

            def prepare(b, n):
                act.wait_ge(S["r_turned"], b + 1)
                se.activation(xnT[:, :], VB[:, :], ACT.Copy).then_inc(S["r_xT"], 1)
                act.wait_ge(S["r_v"], b + 1)
                vs = VB[:, :].rearrange("p (t r m c) -> p t m r c", t=TT, r=4, m=4)
                for m in range(4):
                    last = se.activation(vm[:, n, :, m, :].rearrange("p t (r m c) -> p t m r c", r=4, m=4)[:, :, m],
                                         vs[:, :, m], ACT.Copy)
                last.then_inc(S["r_vspread"], 1)
                act.wait_ge(S["r_opT"], 2 * b + 1)
                for r in range(4):
                    se.activation(qR[:, n, :, r, :], QKB[0][:, :].rearrange("p (t c) -> p t c", t=TT), ACT.Copy,
                                  scale=queryheads[:, r:r + 1])
                act.wait_ge(S["r_opT"], 2 * b + 2)
                for m in range(4):
                    if m == 3:
                        se.activation(qT[:, n, :], QKB[0][:, :], ACT.Copy)
                    se.activation(kT[:, n, m, :], QKB[1][:, :], ACT.Copy, scale=keyheads[:, m:m + 1])\
                        .then_inc(S["r_op"], 1)
                act.sem_inc(S["r_opq"], 1)

            def batch(b, n, first, final):
                if not final:
                    prepare(b + 1, 1 - n)
                act.wait_ge(S["r_summed"], b + 1)
                if not first:
                    act.wait_ge(S["r_z"], b)
                se.activation(y, YB[n][:, :], ACT.Copy).then_inc(S["r_ycopied"], 1)

            prepare(0, 0)
            retain_loop(act, batch)

        @block.sync
        def _(sp):
            x_src = x_in.rearrange("b (t p) d -> p b t d", p=P)
            for dst, src in ((x[:, 0:TT, :], x_src[:, 0]), (cst[:], consts)):
                sp.dma_start(dst, src).then_inc(S["x_loaded"], 16)
            early = ((wproj[:, 0:2 * H * DK], w_qk), (wrows[:], w_qk_rows), (wfold[:], fold),
                     (btab[:], bonus.partition_broadcast(P)), (wv[:], w_v))
            for dst, src in early[0:3]:
                sp.dma_start(dst, src).then_inc(S["loads"], 16)
            for b in range(1, B):
                sp.dma_start(x[:, b * TT:(b + 1) * TT, :], x_src[:, b]).then_inc(S["x_rest"], 16)
            for dst, src in early[3:]:
                sp.dma_start(dst, src).then_inc(S["loads_v"], 16)
            late = ((wo[:], w_out), (wr[:], router), (wff[:], ffn_in), (wfo[:], ffn_out),
                    (rqkv[:], ret_qkv), (rwo[:], ret_o), (gnw[:], gn))
            for dst, src in late:
                sp.dma_start(dst, src).then_inc(S["loads_late"], 16)
            sp.wait_ge(S["zero_set"], 1)
            for f in range(2):
                slot_rows = xg[f].rearrange("(j p) w -> p j w", p=P)
                sp.dma_start(slot_rows[:, :, 0:D + 2],
                             bass.AP(zrow[:, :].tensor, zrow[:, :].offset, [zrow[:, :].ap[0], [0, NS], [1, D + 2]]))\
                    .then_inc(S["zeroed"], 16)
                with nc.allow_non_contiguous_dma(reason="a word of each slot's row"):
                    sp.dma_start(slot_rows[:, :, D + 2:RW].bitcast(I32),
                                 homes[:, 2 * NT:2 * NT + NS].rearrange("p (j w) -> p j w", w=1))\
                        .then_inc(S["zeroed"], 16)
            for f in range(2):
                units_sp(sp, f)
            for b in range(B):
                sp.wait_ge(S["finished"], b + 1)
                sp.dma_start(out[b].rearrange("(t p) d -> p t d", p=P), x[:, b * TT:(b + 1) * TT, :])\
                    .then_inc(S["stored"], 16)
            sp.wait_ge(S["stored"], B * 16)

        @block.tensor
        def _(pe):
            proj_pe(pe)
            projected(pe)
            attn_pe(pe)
            route_pe(pe, 0)
            units_pe(pe, 0)
            retain_pe(pe)
            route_pe(pe, 1)
            units_pe(pe, 1)

        @block.scalar
        def _(act):
            proj_act(act)
            projected(act)
            attn_act(act)
            route_act(act, 0)
            units_act(act, 0)
            retain_act(act)
            route_act(act, 1)
            units_act(act, 1)

        @block.gpsimd
        def _(pool):
            proj_pool(pool)
            projected(pool)
            attn_pool(pool)
            scatter_pool(pool, 0)
            results_pool(pool, 0)
            retain_pool(pool)
            scatter_pool(pool, 1)
            results_pool(pool, 1)

        @block.vector
        def _(dve):
            proj_dve(dve)
            projected(dve)
            attn_dve(dve)
            route_dve(dve, 0)
            units_dve(dve, 0)
            retain_dve(dve)
            route_dve(dve, 1)
            units_dve(dve, 1)
            for b in range(B):
                fetch_dve(dve, 1, b).then_inc(S["finished"], 1)


def host_layout(i):
    H, DK, D, P, E = 16, 4, 128, 128, 8
    NT = i["L0_attn_a_x"].size // D // P
    NS = -(-((2 * NT * P + E * (P - 1)) // P) // 4) * 4
    f = lambda n: np.asarray(i[n])
    a = {}
    a["x_in"] = f("L0_attn_a_x")
    wq, wk = f("L0_attn_a_W_q"), f("L0_attn_a_W_k")
    a["w_qk"] = np.concatenate([wq.T, wk.T], 1)
    a["w_qk_rows"] = np.concatenate([wq, wk], 1)
    fold = np.zeros((H * DK, 2 * H * DK), np.float32)
    for h in range(H):
        s = slice(h * DK, (h + 1) * DK)
        fold[s, s] = f("L0_attn_a_W_nudge")[h]
        fold[s, slice(H * DK + h * DK, H * DK + (h + 1) * DK)] = f("L0_attn_a_simple_roots").T
    a["fold"] = fold
    a["w_v"] = f("L0_attn_a_W_v").T
    a["bonus"] = f("L0_attn_a_chamber_bonus")
    a["w_out"] = f("L0_attn_a_W_out").T.reshape(8, P, D).transpose(1, 0, 2)
    a["ret_qkv"] = np.concatenate([f(f"L0_attn_b_W{n}").T for n in "qkv"], 1)
    a["ret_o"] = f("L0_attn_b_Wo").T
    a["gn"] = np.stack([f("L0_attn_b_gn_w"), f("L0_attn_b_gn_b")], 1)
    a["router"] = f("L0_ffn_router_DE")
    pairs = [np.concatenate([f("L0_ffn_w_in_eDF")[e], f("L0_ffn_w_swiglu_eDF")[e]], 1) for e in range(E)]
    pairs.append(np.concatenate([f("L0_ffn_w_in_shared_FD").T, f("L0_ffn_w_swiglu_FD").T], 1))
    a["ffn_in"] = np.concatenate(pairs, 1)
    outs = [f("L0_ffn_w_out_eFD")[e] for e in range(E)] + [f("L0_ffn_w_out_shared_DF").T]
    a["ffn_out"] = np.concatenate([w.reshape(2, P, D).transpose(1, 0, 2).reshape(P, 2 * D) for w in outs], 1)
    gam = 1.0 - 2.0 ** (-5.0 - np.arange(H) * (8.0 / H))
    ch = np.repeat(gam, D // H)
    tok = np.arange(P)[:, None]
    same = (np.arange(D)[:, None] // 8 == np.arange(D)[None, :] // 8)
    c = [np.eye(P), np.arange(P)[:, None] <= np.arange(P)[None, :], same / 8.0, same * (ch[:, None] ** P),
         ch[None, :] ** tok / np.sqrt(8.0), ch[None, :] ** -tok,
         np.broadcast_to(np.arange(8 * E, 0, -1)[None, :] - 7 * E, (P, 8 * E)),
         ch[:, None] ** P,
         (np.arange(D)[:, None] // 8 % 4 == np.arange(4)[None, :]),
         np.broadcast_to(np.arange(NS)[None, :], (P, NS)),
         (np.arange(D)[:, None] // 32 == np.arange(4)[None, :]),
         np.arange(2 * NT + NS)[None, :] * P + tok]
    a["consts"] = np.concatenate([np.asarray(m, np.float32) for m in c], 1)
    return {n: np.ascontiguousarray(v) for n, v in a.items()}


def kernel(**inputs):
    import concourse.bacc as _bacc
    from concourse.bass_utils import run_bass_kernel_spmd as _run

    arrays = host_layout(inputs)
    nc = _bacc.Bacc("TRN2", target_bir_lowering=False, num_devices=1)
    args = [nc.dram_tensor(f"in_{n}", v.shape, mybir.dt.from_np(v.dtype), kind="ExternalInput").ap()
            for n, v in arrays.items()]
    res = nc.dram_tensor("out_0", arrays["x_in"].shape, mybir.dt.float32, kind="ExternalOutput").ap()
    hybrid_block_kernel(nc, *args, res)
    r = _run(nc, [{f"in_{n}": v for n, v in arrays.items()}], core_ids=[0])
    return r.results[0]["out_0"]
```
